# Optimizing a Trainium2 kernel written in Bass

```python
import numpy as np
import jax
import jax.numpy as jnp

def _softmax(x, axis=-1):
    return jax.nn.softmax(x, axis=axis)

def _gelu(x):
    return jax.nn.gelu(x, approximate=True)

def _silu(x):
    return jax.nn.silu(x)

def _sigmoid(x):
    return jax.nn.sigmoid(x)

def _layernorm(x, axis=-1, eps=1e-05):
    m = jnp.mean(x, axis=axis, keepdims=True)
    v = jnp.var(x, axis=axis, keepdims=True)
    return (x - m) / jnp.sqrt(v + eps)

def _scatter_add(tgt, idx, src, axis=0):
    return tgt.at[idx].add(src)

def _segment_sum(src, seg, n):
    return jax.ops.segment_sum(src, seg, n)
kernel_name = 'mk_early_fusion_d2_tok_img768_r4_9e3809'

def setup_inputs(seed: int=0):
    np.random.seed(seed)
    _w = jnp.asarray

    def _rec_inputs():
        import jax
        import jax.numpy as jnp
        _rk = jax.random.key(seed)
        x = -0.000596345 + 1.00056 * jax.random.normal(jax.random.fold_in(_rk, 1), (8, 3, 64, 64), jnp.float32)
        txt = -0.000190561 + 0.886117 * jax.random.normal(jax.random.fold_in(_rk, 2), (8, 128, 192), jnp.float32)
        return (x, txt)
    x, txt = _rec_inputs()

    def _L0_tok_setup():
        import jax, jax.numpy as jnp
        import numpy as np
        B = 16
        IMG = 64
        CH = 3
        EMBED = 64
        GP = 16
        PRE = [1, 2, 4]
        N_LEVELS = 3
        FUSED = EMBED * N_LEVELS

        def hilbert_flat_indices(n):
            t = np.arange(n * n, dtype=np.int64)
            x = np.zeros(n * n, dtype=np.int64)
            y = np.zeros(n * n, dtype=np.int64)
            s = 1
            while s < n:
                rx = 1 & t // 2
                ry = 1 & (t ^ rx)
                swap = ry == 0
                flip = swap & (rx == 1)
                x = np.where(flip, s - 1 - x, x)
                y = np.where(flip, s - 1 - y, y)
                x2 = np.where(swap, y, x)
                y2 = np.where(swap, x, y)
                x, y = (x2, y2)
                x = x + s * rx
                y = y + s * ry
                t = t // 4
                s *= 2
            return y * n + x

        def _level(x, idx, W, b, p, gp):
            Bsz, C, H, _ = x.shape
            h = H // p
            t = x.reshape(Bsz, C, h, p, h, p).transpose(0, 2, 4, 3, 5, 1).reshape(Bsz, h * h, p * p * C)
            t = t[:, idx]
            t = t.reshape(Bsz, h * h // gp, gp * p * p * C)
            return t @ W.T + b

        def _interp_linear(x, n_out):
            L = x.shape[1]
            pos = (jnp.arange(n_out, dtype=jnp.float32) + 0.5) * (L / n_out) - 0.5
            pos = jnp.clip(pos, 0.0, L - 1)
            i0 = jnp.floor(pos).astype(jnp.int32)
            i1 = jnp.minimum(i0 + 1, L - 1)
            w = (pos - i0).astype(x.dtype)
            return x[:, i0] * (1.0 - w)[None, :, None] + x[:, i1] * w[None, :, None]
        key = jax.random.key(seed)
        ks = jax.random.split(key, 9)
        inp = {'x': jax.random.normal(ks[0], (B, CH, IMG, IMG), jnp.float32)}
        for i, p in enumerate(PRE):
            din = CH * p * p * GP
            inp[f'W{i}'] = jax.random.normal(ks[1 + 2 * i], (EMBED, din), jnp.float32) * din ** (-0.5)
            inp[f'b{i}'] = jax.random.normal(ks[2 + 2 * i], (EMBED,), jnp.float32) * 0.02
        inp['Wf'] = jax.random.normal(ks[7], (FUSED, FUSED), jnp.float32) * FUSED ** (-0.5)
        inp['bf'] = jax.random.normal(ks[8], (FUSED,), jnp.float32) * 0.02
        for i, p in enumerate(PRE):
            inp[f'idx{i}'] = jnp.asarray(hilbert_flat_indices(IMG // p), jnp.int32)
        return inp
    _L0_tok_all = _L0_tok_setup()
    _L0_tok_in = {k: v for k, v in _L0_tok_all.items() if k in ('W0', 'b0', 'W1', 'b1', 'W2', 'b2', 'Wf', 'bf', 'idx0', 'idx1', 'idx2')}
    del _L0_tok_all

    def _L0_attn_setup():
        import jax, jax.numpy as jnp
        import numpy as np
        NUM_HEADS = 8
        key = jax.random.key(seed)
        k1, k2, k3, k4 = jax.random.split(key, 4)
        B, N, C = (2, 1024, 192)
        x = jax.random.normal(k1, (B, N, C), dtype=jnp.float32)
        w_qkv = jax.random.normal(k2, (C, 3 * C), dtype=jnp.float32) * C ** (-0.5)
        w_proj = jax.random.normal(k3, (C, C), dtype=jnp.float32) * C ** (-0.5)
        b_proj = jax.random.normal(k4, (C,), dtype=jnp.float32) * 0.02
        return {'x': x, 'w_qkv': w_qkv, 'w_proj': w_proj, 'b_proj': b_proj}
    _L0_attn_all = _L0_attn_setup()
    _L0_attn_in = {k: v for k, v in _L0_attn_all.items() if k in ('w_qkv', 'w_proj', 'b_proj')}
    del _L0_attn_all

    def _L0_ffn_setup():
        import jax, jax.numpy as jnp
        import numpy as np
        N_EMBD = 192
        N_EXPERTS = 8
        TOP_K = 2
        D_FF = 4 * N_EMBD
        key = jax.random.key(seed)
        ks = jax.random.split(key, 7)
        B, T, C, E, H = (4, 512, N_EMBD, N_EXPERTS, D_FF)
        s_gate = 1.0 / np.sqrt(C)
        s1 = 1.0 / np.sqrt(C)
        s2 = 1.0 / np.sqrt(H)
        return {'x': jax.random.normal(ks[0], (B, T, C), dtype=jnp.float32), 'gate_w': jax.random.uniform(ks[1], (C, E), jnp.float32, -s_gate, s_gate), 'gate_b': jax.random.uniform(ks[2], (E,), jnp.float32, -s_gate, s_gate), 'w1': jax.random.uniform(ks[3], (E, C, H), jnp.float32, -s1, s1), 'b1': jax.random.uniform(ks[4], (E, H), jnp.float32, -s1, s1), 'w2': jax.random.uniform(ks[5], (E, H, C), jnp.float32, -s2, s2), 'b2': jax.random.uniform(ks[6], (E, C), jnp.float32, -s2, s2)}
    _L0_ffn_all = _L0_ffn_setup()
    _L0_ffn_in = {k: v for k, v in _L0_ffn_all.items() if k in ('gate_w', 'gate_b', 'w1', 'b1', 'w2', 'b2')}
    del _L0_ffn_all

    def _L1_attn_setup():
        import jax, jax.numpy as jnp
        import numpy as np
        B, S, D, H, HD = (4, 512, 192, 12, 64)
        P = H * HD
        LR = 0.1

        def _ln(x, g, b, eps=1e-05):
            m = jnp.mean(x, axis=-1, keepdims=True)
            v = jnp.mean((x - m) ** 2, axis=-1, keepdims=True)
            return (x - m) / jnp.sqrt(v + eps) * g + b

        def _modifier(x, w1, b1, w2, b2):
            h = jax.nn.gelu(x @ w1.T + b1, approximate=False)
            return h @ w2.T + b2

        def _reference_tuple_inner(x, ln_in_g, ln_in_b, Wk, Wv, Wq, km_w1, km_b1, km_w2, km_b2, vm_w1, vm_b1, vm_w2, vm_b2, qm_w1, qm_b1, qm_w2, qm_b2, lnk_g, lnk_b, lnv_g, lnv_b, lnq_g, lnq_b, Wo, lr_scale, Wg, bg):
            b, s, d = x.shape
            xn = _ln(x, ln_in_g, ln_in_b)
            k = xn @ Wk.T + 0.1 * _modifier(xn, km_w1, km_b1, km_w2, km_b2)
            v = xn @ Wv.T + 0.1 * _modifier(xn, vm_w1, vm_b1, vm_w2, vm_b2)
            q = xn @ Wq.T + 0.1 * _modifier(xn, qm_w1, qm_b1, qm_w2, qm_b2)
            k = _ln(k.reshape(b, s, H, HD), lnk_g, lnk_b)
            v = _ln(v.reshape(b, s, H, HD), lnv_g, lnv_b)
            q = _ln(q.reshape(b, s, H, HD), lnq_g, lnq_b)
            k_s = jnp.transpose(k, (1, 0, 2, 3))
            v_s = jnp.transpose(v, (1, 0, 2, 3))
            q_s = jnp.transpose(q, (1, 0, 2, 3))
            lr = jax.nn.sigmoid(lr_scale) * LR * 2.0
            M0 = jnp.zeros((b, H, HD, HD), x.dtype)

            def step(M, kvq):
                k_t, v_t, q_t = kvq
                out_t = jnp.einsum('bhdk,bhk->bhd', M, q_t)
                kn = k_t / (jnp.linalg.norm(k_t, axis=-1, keepdims=True) + 1e-06)
                pred = jnp.einsum('bhdk,bhk->bhd', M, kn)
                surprise = pred - v_t
                coef = pred + lr[None, :, None] * surprise
                M_new = M - jnp.einsum('bhd,bhk->bhdk', coef, kn)
                return (M_new, out_t)
            M_final, outs = jax.lax.scan(step, M0, (k_s, v_s, q_s))
            out = jnp.transpose(outs, (1, 0, 2, 3)).reshape(b, s, H * HD)
            out = out @ Wo.T
            gate = jax.nn.sigmoid(x @ Wg.T + bg)
            out = gate * out
            return (out, M_final)
        key = jax.random.key(seed)
        ks = jax.random.split(key, 16)

        def n(k, shape, s=0.02):
            return jax.random.normal(k, shape, jnp.float32) * s
        inp = {}
        inp['x'] = jax.random.normal(ks[0], (B, S, D), jnp.float32)
        inp['ln_in_g'] = jnp.ones((D,), jnp.float32)
        inp['ln_in_b'] = jnp.zeros((D,), jnp.float32)
        inp['Wk'] = n(ks[1], (P, D))
        inp['Wv'] = n(ks[2], (P, D))
        inp['Wq'] = n(ks[3], (P, D))
        inp['km_w1'] = n(ks[4], (D // 4, D), 0.01)
        inp['km_b1'] = jnp.zeros((D // 4,), jnp.float32)
        inp['km_w2'] = n(ks[5], (P, D // 4), 0.01)
        inp['km_b2'] = jnp.zeros((P,), jnp.float32)
        inp['vm_w1'] = n(ks[6], (D // 4, D), 0.01)
        inp['vm_b1'] = jnp.zeros((D // 4,), jnp.float32)
        inp['vm_w2'] = n(ks[7], (P, D // 4), 0.01)
        inp['vm_b2'] = jnp.zeros((P,), jnp.float32)
        inp['qm_w1'] = n(ks[8], (D // 4, D), 0.01)
        inp['qm_b1'] = jnp.zeros((D // 4,), jnp.float32)
        inp['qm_w2'] = n(ks[9], (P, D // 4), 0.01)
        inp['qm_b2'] = jnp.zeros((P,), jnp.float32)
        inp['lnk_g'] = jnp.ones((HD,), jnp.float32)
        inp['lnk_b'] = jnp.zeros((HD,), jnp.float32)
        inp['lnv_g'] = jnp.ones((HD,), jnp.float32)
        inp['lnv_b'] = jnp.zeros((HD,), jnp.float32)
        inp['lnq_g'] = jnp.ones((HD,), jnp.float32)
        inp['lnq_b'] = jnp.zeros((HD,), jnp.float32)
        inp['Wo'] = n(ks[10], (D, P))
        inp['lr_scale'] = jnp.ones((H,), jnp.float32)
        inp['Wg'] = n(ks[11], (D, D))
        inp['bg'] = jnp.zeros((D,), jnp.float32)
        return inp
    _L1_attn_all = _L1_attn_setup()
    _L1_attn_in = {k: v for k, v in _L1_attn_all.items() if k in ('ln_in_g', 'ln_in_b', 'Wk', 'Wv', 'Wq', 'km_w1', 'km_b1', 'km_w2', 'km_b2', 'vm_w1', 'vm_b1', 'vm_w2', 'vm_b2', 'qm_w1', 'qm_b1', 'qm_w2', 'qm_b2', 'lnk_g', 'lnk_b', 'lnv_g', 'lnv_b', 'lnq_g', 'lnq_b', 'Wo', 'lr_scale', 'Wg', 'bg')}
    del _L1_attn_all

    def _L1_ffn_setup():
        import jax, jax.numpy as jnp
        import numpy as np
        S, B, DIM = (256, 4, 192)
        N_EXPERTS = 8
        HID = 512
        key = jax.random.key(seed)
        ks = jax.random.split(key, 6)
        scale = 0.02
        return {'hidden_states': jax.random.normal(ks[0], (S, B, DIM), dtype=jnp.float32), 'router_w': jax.random.normal(ks[1], (DIM, N_EXPERTS), dtype=jnp.float32) * scale, 'router_b': jnp.zeros((N_EXPERTS,), dtype=jnp.float32), 'w1': jax.random.normal(ks[2], (N_EXPERTS, DIM, HID), dtype=jnp.float32) * scale, 'w2': jax.random.normal(ks[3], (N_EXPERTS, DIM, HID), dtype=jnp.float32) * scale, 'w3': jax.random.normal(ks[4], (N_EXPERTS, HID, DIM), dtype=jnp.float32) * scale}
    _L1_ffn_all = _L1_ffn_setup()
    _L1_ffn_in = {k: v for k, v in _L1_ffn_all.items() if k in ('router_w', 'router_b', 'w1', 'w2', 'w3')}
    del _L1_ffn_all
    return {'x': x, 'txt': txt, 'L0_tok_W0': _L0_tok_in['W0'], 'L0_tok_b0': _L0_tok_in['b0'], 'L0_tok_W1': _L0_tok_in['W1'], 'L0_tok_b1': _L0_tok_in['b1'], 'L0_tok_W2': _L0_tok_in['W2'], 'L0_tok_b2': _L0_tok_in['b2'], 'L0_tok_Wf': _L0_tok_in['Wf'], 'L0_tok_bf': _L0_tok_in['bf'], 'L0_tok_idx0': _L0_tok_in['idx0'], 'L0_tok_idx1': _L0_tok_in['idx1'], 'L0_tok_idx2': _L0_tok_in['idx2'], 'L0_attn_w_qkv': _L0_attn_in['w_qkv'], 'L0_attn_w_proj': _L0_attn_in['w_proj'], 'L0_attn_b_proj': _L0_attn_in['b_proj'], 'L0_ffn_gate_w': _L0_ffn_in['gate_w'], 'L0_ffn_gate_b': _L0_ffn_in['gate_b'], 'L0_ffn_w1': _L0_ffn_in['w1'], 'L0_ffn_b1': _L0_ffn_in['b1'], 'L0_ffn_w2': _L0_ffn_in['w2'], 'L0_ffn_b2': _L0_ffn_in['b2'], 'L1_attn_ln_in_g': _L1_attn_in['ln_in_g'], 'L1_attn_ln_in_b': _L1_attn_in['ln_in_b'], 'L1_attn_Wk': _L1_attn_in['Wk'], 'L1_attn_Wv': _L1_attn_in['Wv'], 'L1_attn_Wq': _L1_attn_in['Wq'], 'L1_attn_km_w1': _L1_attn_in['km_w1'], 'L1_attn_km_b1': _L1_attn_in['km_b1'], 'L1_attn_km_w2': _L1_attn_in['km_w2'], 'L1_attn_km_b2': _L1_attn_in['km_b2'], 'L1_attn_vm_w1': _L1_attn_in['vm_w1'], 'L1_attn_vm_b1': _L1_attn_in['vm_b1'], 'L1_attn_vm_w2': _L1_attn_in['vm_w2'], 'L1_attn_vm_b2': _L1_attn_in['vm_b2'], 'L1_attn_qm_w1': _L1_attn_in['qm_w1'], 'L1_attn_qm_b1': _L1_attn_in['qm_b1'], 'L1_attn_qm_w2': _L1_attn_in['qm_w2'], 'L1_attn_qm_b2': _L1_attn_in['qm_b2'], 'L1_attn_lnk_g': _L1_attn_in['lnk_g'], 'L1_attn_lnk_b': _L1_attn_in['lnk_b'], 'L1_attn_lnv_g': _L1_attn_in['lnv_g'], 'L1_attn_lnv_b': _L1_attn_in['lnv_b'], 'L1_attn_lnq_g': _L1_attn_in['lnq_g'], 'L1_attn_lnq_b': _L1_attn_in['lnq_b'], 'L1_attn_Wo': _L1_attn_in['Wo'], 'L1_attn_lr_scale': _L1_attn_in['lr_scale'], 'L1_attn_Wg': _L1_attn_in['Wg'], 'L1_attn_bg': _L1_attn_in['bg'], 'L1_ffn_router_w': _L1_ffn_in['router_w'], 'L1_ffn_router_b': _L1_ffn_in['router_b'], 'L1_ffn_w1': _L1_ffn_in['w1'], 'L1_ffn_w2': _L1_ffn_in['w2'], 'L1_ffn_w3': _L1_ffn_in['w3']}

def reference(x, txt, L0_tok_W0, L0_tok_b0, L0_tok_W1, L0_tok_b1, L0_tok_W2, L0_tok_b2, L0_tok_Wf, L0_tok_bf, L0_tok_idx0, L0_tok_idx1, L0_tok_idx2, L0_attn_w_qkv, L0_attn_w_proj, L0_attn_b_proj, L0_ffn_gate_w, L0_ffn_gate_b, L0_ffn_w1, L0_ffn_b1, L0_ffn_w2, L0_ffn_b2, L1_attn_ln_in_g, L1_attn_ln_in_b, L1_attn_Wk, L1_attn_Wv, L1_attn_Wq, L1_attn_km_w1, L1_attn_km_b1, L1_attn_km_w2, L1_attn_km_b2, L1_attn_vm_w1, L1_attn_vm_b1, L1_attn_vm_w2, L1_attn_vm_b2, L1_attn_qm_w1, L1_attn_qm_b1, L1_attn_qm_w2, L1_attn_qm_b2, L1_attn_lnk_g, L1_attn_lnk_b, L1_attn_lnv_g, L1_attn_lnv_b, L1_attn_lnq_g, L1_attn_lnq_b, L1_attn_Wo, L1_attn_lr_scale, L1_attn_Wg, L1_attn_bg, L1_ffn_router_w, L1_ffn_router_b, L1_ffn_w1, L1_ffn_w2, L1_ffn_w3):
    import jax
    import jax.numpy as jnp

    def _L0_tok_ref(x, W0, b0, W1, b1, W2, b2, Wf, bf, idx0, idx1, idx2):
        import jax, jax.numpy as jnp
        import numpy as np
        B = 16
        IMG = 64
        CH = 3
        EMBED = 64
        GP = 16
        PRE = [1, 2, 4]
        N_LEVELS = 3
        FUSED = EMBED * N_LEVELS

        def hilbert_flat_indices(n):
            t = np.arange(n * n, dtype=np.int64)
            x = np.zeros(n * n, dtype=np.int64)
            y = np.zeros(n * n, dtype=np.int64)
            s = 1
            while s < n:
                rx = 1 & t // 2
                ry = 1 & (t ^ rx)
                swap = ry == 0
                flip = swap & (rx == 1)
                x = np.where(flip, s - 1 - x, x)
                y = np.where(flip, s - 1 - y, y)
                x2 = np.where(swap, y, x)
                y2 = np.where(swap, x, y)
                x, y = (x2, y2)
                x = x + s * rx
                y = y + s * ry
                t = t // 4
                s *= 2
            return y * n + x

        def _level(x, idx, W, b, p, gp):
            Bsz, C, H, _ = x.shape
            h = H // p
            t = x.reshape(Bsz, C, h, p, h, p).transpose(0, 2, 4, 3, 5, 1).reshape(Bsz, h * h, p * p * C)
            t = t[:, idx]
            t = t.reshape(Bsz, h * h // gp, gp * p * p * C)
            return t @ W.T + b

        def _interp_linear(x, n_out):
            L = x.shape[1]
            pos = (jnp.arange(n_out, dtype=jnp.float32) + 0.5) * (L / n_out) - 0.5
            pos = jnp.clip(pos, 0.0, L - 1)
            i0 = jnp.floor(pos).astype(jnp.int32)
            i1 = jnp.minimum(i0 + 1, L - 1)
            w = (pos - i0).astype(x.dtype)
            return x[:, i0] * (1.0 - w)[None, :, None] + x[:, i1] * w[None, :, None]
        Ws = [(idx0, W0, b0, PRE[0]), (idx1, W1, b1, PRE[1]), (idx2, W2, b2, PRE[2])]
        outs = [_level(x, idx, W, b, p, GP) for idx, W, b, p in Ws]
        n_tokens = outs[0].shape[1]
        outs = [outs[0]] + [_interp_linear(o, n_tokens) for o in outs[1:]]
        y = jnp.concatenate(outs, axis=-1)
        return y @ Wf.T + bf

    def _L0_attn_ref(x, w_qkv, w_proj, b_proj):
        import jax, jax.numpy as jnp
        import numpy as np
        NUM_HEADS = 8
        B, N, C = x.shape
        H = NUM_HEADS
        Dh = C // H
        scale = Dh ** (-0.5)
        qkv = (x @ w_qkv).reshape(B, N, 3, H, Dh).transpose(2, 0, 3, 1, 4)
        q, k, v = (qkv[0], qkv[1], qkv[2])
        attn = jnp.einsum('bhqd,bhkd->bhqk', q, k) * scale
        attn = jax.nn.softmax(attn, axis=-1)
        out = jnp.einsum('bhqk,bhkd->bhqd', attn, v)
        out = out.transpose(0, 2, 1, 3).reshape(B, N, C)
        return out @ w_proj + b_proj

    def _L0_ffn_ref(x, gate_w, gate_b, w1, b1, w2, b2):
        import jax, jax.numpy as jnp
        import numpy as np
        N_EMBD = 192
        N_EXPERTS = 8
        TOP_K = 2
        D_FF = 4 * N_EMBD
        B, T, C = x.shape
        x_flat = x.reshape(B * T, C)
        gate_logits = x_flat @ gate_w + gate_b
        gate_probs = jax.nn.softmax(gate_logits, axis=-1)
        topk_probs, topk_idx = jax.lax.top_k(gate_probs, TOP_K)
        topk_probs = topk_probs / jnp.sum(topk_probs, axis=-1, keepdims=True)
        h = jax.nn.gelu(jnp.einsum('nc,ech->neh', x_flat, w1) + b1[None], approximate=False)
        expert_out = jnp.einsum('neh,ehc->nec', h, w2) + b2[None]
        sel = jnp.take_along_axis(expert_out, topk_idx[:, :, None], axis=1)
        combined = jnp.sum(topk_probs[:, :, None] * sel, axis=1)
        return combined.reshape(B, T, C)

    def _L1_attn_ref(x, ln_in_g, ln_in_b, Wk, Wv, Wq, km_w1, km_b1, km_w2, km_b2, vm_w1, vm_b1, vm_w2, vm_b2, qm_w1, qm_b1, qm_w2, qm_b2, lnk_g, lnk_b, lnv_g, lnv_b, lnq_g, lnq_b, Wo, lr_scale, Wg, bg):
        import jax, jax.numpy as jnp
        import numpy as np
        B, S, D, H, HD = (4, 512, 192, 12, 64)
        P = H * HD
        LR = 0.1

        def _ln(x, g, b, eps=1e-05):
            m = jnp.mean(x, axis=-1, keepdims=True)
            v = jnp.mean((x - m) ** 2, axis=-1, keepdims=True)
            return (x - m) / jnp.sqrt(v + eps) * g + b

        def _modifier(x, w1, b1, w2, b2):
            h = jax.nn.gelu(x @ w1.T + b1, approximate=False)
            return h @ w2.T + b2

        def _reference_tuple_inner(x, ln_in_g, ln_in_b, Wk, Wv, Wq, km_w1, km_b1, km_w2, km_b2, vm_w1, vm_b1, vm_w2, vm_b2, qm_w1, qm_b1, qm_w2, qm_b2, lnk_g, lnk_b, lnv_g, lnv_b, lnq_g, lnq_b, Wo, lr_scale, Wg, bg):
            b, s, d = x.shape
            xn = _ln(x, ln_in_g, ln_in_b)
            k = xn @ Wk.T + 0.1 * _modifier(xn, km_w1, km_b1, km_w2, km_b2)
            v = xn @ Wv.T + 0.1 * _modifier(xn, vm_w1, vm_b1, vm_w2, vm_b2)
            q = xn @ Wq.T + 0.1 * _modifier(xn, qm_w1, qm_b1, qm_w2, qm_b2)
            k = _ln(k.reshape(b, s, H, HD), lnk_g, lnk_b)
            v = _ln(v.reshape(b, s, H, HD), lnv_g, lnv_b)
            q = _ln(q.reshape(b, s, H, HD), lnq_g, lnq_b)
            k_s = jnp.transpose(k, (1, 0, 2, 3))
            v_s = jnp.transpose(v, (1, 0, 2, 3))
            q_s = jnp.transpose(q, (1, 0, 2, 3))
            lr = jax.nn.sigmoid(lr_scale) * LR * 2.0
            M0 = jnp.zeros((b, H, HD, HD), x.dtype)

            def step(M, kvq):
                k_t, v_t, q_t = kvq
                out_t = jnp.einsum('bhdk,bhk->bhd', M, q_t)
                kn = k_t / (jnp.linalg.norm(k_t, axis=-1, keepdims=True) + 1e-06)
                pred = jnp.einsum('bhdk,bhk->bhd', M, kn)
                surprise = pred - v_t
                coef = pred + lr[None, :, None] * surprise
                M_new = M - jnp.einsum('bhd,bhk->bhdk', coef, kn)
                return (M_new, out_t)
            M_final, outs = jax.lax.scan(step, M0, (k_s, v_s, q_s))
            out = jnp.transpose(outs, (1, 0, 2, 3)).reshape(b, s, H * HD)
            out = out @ Wo.T
            gate = jax.nn.sigmoid(x @ Wg.T + bg)
            out = gate * out
            return (out, M_final)
        return _reference_tuple_inner(x, ln_in_g, ln_in_b, Wk, Wv, Wq, km_w1, km_b1, km_w2, km_b2, vm_w1, vm_b1, vm_w2, vm_b2, qm_w1, qm_b1, qm_w2, qm_b2, lnk_g, lnk_b, lnv_g, lnv_b, lnq_g, lnq_b, Wo, lr_scale, Wg, bg)[0]

    def _L1_ffn_ref(hidden_states, router_w, router_b, w1, w2, w3):
        import jax, jax.numpy as jnp
        import numpy as np
        S, B, DIM = (256, 4, 192)
        N_EXPERTS = 8
        HID = 512
        s, b, h = hidden_states.shape
        route = jax.nn.softmax(hidden_states @ router_w + router_b, axis=2)
        max_prob = jnp.max(route, axis=2).reshape(-1, 1)
        max_ind = jnp.argmax(route, axis=2).reshape(-1)
        x = hidden_states.reshape(-1, h)
        out = jnp.zeros_like(x)
        for e in range(N_EXPERTS):
            mask = (max_ind == e)[:, None]
            xe = jnp.where(mask, x, 0.0)
            oe = jax.nn.silu(xe @ w1[e]) * (xe @ w2[e]) @ w3[e]
            out = out + jnp.where(mask, oe, 0.0)
        out = out.astype(jnp.bfloat16) * max_prob
        return out.reshape(s, b, h)
    h = _L0_tok_ref(x, L0_tok_W0, L0_tok_b0, L0_tok_W1, L0_tok_b1, L0_tok_W2, L0_tok_b2, L0_tok_Wf, L0_tok_bf, L0_tok_idx0, L0_tok_idx1, L0_tok_idx2)
    h = jnp.concatenate([h, txt], axis=1)
    h = h + _L0_attn_ref(_layernorm(h, axis=-1), L0_attn_w_qkv, L0_attn_w_proj, L0_attn_b_proj)
    h = h + _L0_ffn_ref(_layernorm(h, axis=-1), L0_ffn_gate_w, L0_ffn_gate_b, L0_ffn_w1, L0_ffn_b1, L0_ffn_w2, L0_ffn_b2)
    h = h + _L1_attn_ref(_layernorm(h, axis=-1), L1_attn_ln_in_g, L1_attn_ln_in_b, L1_attn_Wk, L1_attn_Wv, L1_attn_Wq, L1_attn_km_w1, L1_attn_km_b1, L1_attn_km_w2, L1_attn_km_b2, L1_attn_vm_w1, L1_attn_vm_b1, L1_attn_vm_w2, L1_attn_vm_b2, L1_attn_qm_w1, L1_attn_qm_b1, L1_attn_qm_w2, L1_attn_qm_b2, L1_attn_lnk_g, L1_attn_lnk_b, L1_attn_lnv_g, L1_attn_lnv_b, L1_attn_lnq_g, L1_attn_lnq_b, L1_attn_Wo, L1_attn_lr_scale, L1_attn_Wg, L1_attn_bg)
    h = h + _L1_ffn_ref(_layernorm(h, axis=-1), L1_ffn_router_w, L1_ffn_router_b, L1_ffn_w1, L1_ffn_w2, L1_ffn_w3)
    return h

_drawn_inputs = setup_inputs


def setup_inputs(seed=0):
    import zlib

    import numpy as np

    out = dict(_drawn_inputs(seed))
    spreads = {'L1_attn_ln_in_g': (1.0, 0.2),
     'L1_attn_ln_in_b': (0.0, 0.1),
     'L1_attn_km_b1': (0.0, 0.8),
     'L1_attn_km_b2': (0.0, 0.637),
     'L1_attn_vm_b1': (0.0, 0.8),
     'L1_attn_vm_b2': (0.0, 0.8),
     'L1_attn_qm_b1': (0.0, 0.8),
     'L1_attn_qm_b2': (0.0, 0.8),
     'L1_attn_lnk_g': (1.0, 0.2),
     'L1_attn_lnk_b': (0.0, 0.281),
     'L1_attn_lnv_g': (1.0, 0.2),
     'L1_attn_lnv_b': (0.0, 0.376),
     'L1_attn_lnq_g': (1.0, 0.2),
     'L1_attn_lnq_b': (0.0, 0.343),
     'L1_attn_lr_scale': (1.0, 0.6),
     'L1_attn_bg': (0.0, 0.575),
     'L1_ffn_router_b': (0.0, 0.8)}
    factors = {'L0_tok_b1': 3.105,
     'L0_ffn_b1': 4.346,
     'L0_ffn_b2': 3.116,
     'L1_attn_km_w1': 8.0,
     'L1_attn_km_w2': 8.0,
     'L1_attn_vm_w1': 8.0,
     'L1_attn_vm_w2': 8.0,
     'L1_attn_qm_w1': 8.0,
     'L1_attn_qm_w2': 8.0,
     'L1_ffn_router_w': 8.0,
     'L1_ffn_w1': 8.0,
     'L1_ffn_w2': 8.0,
     'L1_ffn_w3': 8.0}
    for name, (base, spread) in spreads.items():
        noise = np.random.default_rng([zlib.crc32(name.encode()), seed]).standard_normal(out[name].shape)
        drawn = base * np.exp(spread * noise) if base else spread * noise
        out[name] = jnp.asarray(drawn.astype(out[name].dtype))
    for name, factor in factors.items():
        out[name] = (out[name] * factor).astype(out[name].dtype)
    return out
```

```python
from contextlib import ExitStack

import numpy as np
import concourse.bass as bass
from concourse import mybir

F32 = mybir.dt.float32
BF16 = mybir.dt.bfloat16
I32 = mybir.dt.int32
ACT = mybir.ActivationFunctionType
ALU = mybir.AluOpType
AX = mybir.AxisListType

P = 128
B = 8
C = 192
KT = 96
NT = 3
G = B * NT
NTOK = NT * P
EPS = 1e-5
E = 8
NH0, DH0 = 8, 24
SCALE = DH0 ** -0.5
F0, F1 = 768, 512
N0 = 56
N1 = 32
H, HD = 12, 64
PW = H * HD
MOD = 48
KB = 64 + MOD + 1
NG = 3
LEVELS = 7


def ds(start, size):
    return bass.ds(start, size)


def after(n):
    return n + 1


class Core:

    def __init__(self, nc, ctx, d):
        self.nc, self.ctx, self.d = nc, ctx, d
        self.fresh, self.used = [], []
        self.h = self.sb("h", [P, G, C])
        self.ident = self.sb("ident", [P, P])
        self.ones = self.sb("ones", [P, P])
        self.stats = self.sb("stats", [P, G, 6])
        self.tmp24 = self.sb("tmp24", [P, 4, G])
        self.mean = self.sb("mean", [P, G])
        self.rstd = self.sb("rstd", [P, G])
        self.vare = self.sb("vare", [P, G])
        self.half2 = self.sb("half2", [P, G])
        self.half = self.sb("half", [P, 2 * G])
        self.wtop = self.sb("wtop", [P, 2, G])
        self.pos = self.sb("pos", [P, 2, G], I32)
        self.eid = self.sb("eid", [1, N0], I32)
        self.xs = nc.dram_tensor("xs", (N0 * P, C), F32, kind="Internal").ap()
        self.ys = nc.dram_tensor("ys", (N0 * P, C), F32, kind="Internal").ap()
        self.ys1 = nc.dram_tensor("ys1", (N1 * P, C), BF16, kind="Internal").ap()
        self.s_consts = self.sem("s_consts")

    def sb(self, name, shape, dt=F32, ctx=None):
        return (ctx or self.ctx).enter_context(self.nc.sbuf_tensor(name, shape, dt))

    def ps(self, name, shape, ctx, dt=F32):
        return ctx.enter_context(self.nc.psum_tensor(name, shape, dt))

    def sem(self, name):
        self.fresh.append(self.plain_sem(name))
        return self.fresh[-1]

    def plain_sem(self, name):
        self.used.append(self.nc.alloc_semaphore(name))
        return self.used[-1]

    def recycle(self):
        self.nc.clear_and_free_semaphores(self.used)
        self.nc.all_engine_barrier()
        self.used = []

    def start_at_one(self, eng):
        for s in self.fresh:
            eng.sem_inc(s, 1)
        self.fresh = []


def linker(eng, sem, base=0):
    n = [0]

    def link(ins):
        n[0] += 1
        ins.then_inc(sem, 1)
        eng.wait_ge(sem, after(base + n[0]))
    return link


def root_step(k, pool, s_var, s_root):
    pool.wait_ge(s_var, after(1))
    k.nc.gpsimd.tensor_tensor(k.rstd[:], k.vare[:], k.half[:, 0:G], ALU.pow).then_inc(s_root, 1)


def finish_stats(k, link):
    v = k.nc.vector
    me, mo = k.stats[:, :, 1], k.stats[:, :, 4]
    ve, vo = k.stats[:, :, 2], k.stats[:, :, 5]
    a, b, c = k.tmp24[:, 0, :], k.tmp24[:, 1, :], k.tmp24[:, 2, :]
    link(v.tensor_tensor(a, me, mo, ALU.add))
    link(v.tensor_scalar(k.mean[:, :], a, 0.5, None, ALU.mult))
    link(v.tensor_tensor(b, me, mo, ALU.subtract))
    link(v.tensor_tensor(a, b, b, ALU.mult))
    link(v.tensor_tensor(c, ve, vo, ALU.add))
    link(v.tensor_scalar(b, c, 1.0 / C, None, ALU.mult))
    link(v.scalar_tensor_tensor(out=c, in0=a, scalar=0.25, in1=b, op0=ALU.mult, op1=ALU.add))
    return v.tensor_scalar(k.vare[:], c, EPS, None, ALU.add)


def stats_of_h(k, dve, s_st, s_link, s_var, s_root):
    with dve.Fori(0, G) as g:
        k.nc.vector.bn_stats(k.stats[:, ds(g, 1), :].rearrange("p a b -> p (a b)"),
                             k.h[:, ds(g, 1), :].rearrange("p a b -> p (a b)")).then_inc(s_st, 1)
    dve.wait_ge(s_st, after(G))
    finish_stats(k, linker(dve, s_link)).then_inc(s_var, 1)
    dve.wait_ge(s_root, after(1))


def tile_of(t, g):
    return t[:, ds(g, 1), :].rearrange("p a b -> p (a b)")


def column_of(t, g):
    return t[:, ds(g, 1)]


def tokenizer(k):
    nc, d = k.nc, k.d
    with ExitStack() as ctx:
        sb = lambda n, s, dt=F32: k.sb(n, s, dt, ctx)
        ix0 = sb("ix0", [P, 2, 16], I32)
        ix1 = sb("ix1", [64, 16], I32)
        ix2 = sb("ix2", [16, 16], I32)
        g0 = sb("g0", [P, 2, 16, 3 * B])
        g1 = sb("g1", [64, 16, 12 * B])
        g2 = sb("g2", [16, 16, 48 * B])
        c0 = sb("c0", [P, 2, 64])
        c1 = sb("c1", [64, 16, 12])
        c2 = sb("c2", [16, 16, 48])
        t0T = sb("t0T", [P, P])
        t1T = sb("t1T", [KT, 2, 64])
        t2T = sb("t2T", [P, 6, 16])
        w0T = sb("w0T", [P, 64])
        w1T = sb("w1T", [KT, 2, 64])
        w2T = sb("w2T", [P, 6, 64])
        wfT = sb("wfT", [64, 3, C])
        lb = sb("lb", [64, 3])
        bf = sb("bf", [P, C])
        up1 = sb("up1", [64, 256])
        up2 = sb("up2", [16, 256])
        o1 = sb("o1", [64, 64])
        o2 = sb("o2", [16, 64])
        yT = sb("yT", [64, 3, 256])
        zero = sb("zero", [P, C])
        pT0 = k.ps("pT0", [P, 512], ctx)
        pT1 = k.ps("pT1", [P, 512], ctx)
        pY = k.ps("pY", [P, 2, 512], ctx)
        pO = k.ps("pO", [P, 512], ctx)
        pU = k.ps("pU", [P, 512], ctx)
        pH = k.ps("pH", [P, 512], ctx)
        s_ix, s_w, s_id, s_c0 = (k.sem("t_" + n) for n in ("ix", "w", "id", "c0"))
        s_g = k.plain_sem("t_g")
        s_cut, s_tr, s_trs, s_lv, s_lvs, s_up, s_y, s_h, s_hs, s_z = (
            k.sem("t_" + n) for n in ("cut", "tr", "trs", "lv", "lvs", "up", "y", "h", "hs", "z"))
        block = ctx.enter_context(nc.Block())

        @block.sync
        def _(sp):
            k.start_at_one(sp)
            sp.dma_start(ix0[:], d["idx0"].rearrange("(t p j) -> p t j", t=2, j=16)).then_inc(s_ix, 16)
            sp.dma_start(ix1[:], d["idx1"].rearrange("(p j) -> p j", j=16)).then_inc(s_ix, 16)
            sp.dma_start(ix2[:], d["idx2"].rearrange("(p j) -> p j", j=16)).then_inc(s_ix, 16)
            for t, name in ((w0T, "w0T"), (w1T, "w1T"), (w2T, "w2T"), (wfT, "wfT"), (lb, "lb"),
                            (up1, "up1"), (up2, "up2")):
                sp.dma_start(t[:], d[name]).then_inc(s_w, 16)
            sp.dma_start(bf[:], d["bf"].broadcast_to([P, C])).then_inc(s_w, 16)
            sp.dma_start(k.h[:, :, :].rearrange("p (b t) c -> p b t c", t=NT)[:, :, 2, :],
                         d["txt"].rearrange("b p c -> p b c")).then_inc(s_w, 16)
            sp.wait_ge(s_z, after(1))
            for n in range(0, N0, 8):
                sp.dma_start(k.xs[n * P:(n + 8) * P, :].rearrange("(n p) c -> p n c", p=P),
                             zero[:, :].rearrange("p (a c) -> p a c", a=1).broadcast_to([P, 8, C])).then_inc(k.s_consts, 16)
            sp.wait_ge(s_w, after(16 * 9))

        @block.gpsimd
        def _(pool):
            nc.gpsimd.memset(k.ident[:], 0.0).then_inc(s_id, 1)
            nc.gpsimd.memset(k.half[:], -0.5)
            nc.gpsimd.memset(k.half2[:], 0.5)
            nc.gpsimd.memset(k.ones[:], 1.0).then_inc(s_id, 1)
            pool.wait_ge(s_id, after(2))
            nc.gpsimd.affine_select(out=k.ident[:], in_=k.ident[:], compare_op=ALU.not_equal, fill=1.0, base=0,
                                    pattern=[[-1, P]], channel_multiplier=1).then_inc(s_id, 1)
            pool.wait_ge(s_ix, after(48))
            for j in range(16):
                for t in range(2):
                    nc.gpsimd.indirect_dma_start(g0[:, t, j, :], None, d["x0r"],
                                                 bass.IndirectOffsetOnAxis(ap=ix0[:, t, j:j + 1], axis=0)).then_inc(s_g, 16)
                nc.gpsimd.indirect_dma_start(g1[:, j, :], None, d["x1r"],
                                             bass.IndirectOffsetOnAxis(ap=ix1[:, j:j + 1], axis=0)).then_inc(s_g, 16)
                nc.gpsimd.indirect_dma_start(g2[:, j, :], None, d["x2r"],
                                             bass.IndirectOffsetOnAxis(ap=ix2[:, j:j + 1], axis=0)).then_inc(s_g, 16)

        @block.vector
        def _(dve):
            nc.vector.memset(zero[:], 0.0).then_inc(s_z, 1)
            nc.vector.memset(c0[:], 0.0).then_inc(s_c0, 1)
            dve.wait_ge(s_c0, after(1))
            dve.wait_ge(s_g, 64 * 16)
            dve.wait_ge(s_w, after(16 * 9))
            with dve.Fori(0, B) as b:
                dve.wait_ge(s_tr, after(b))
                nc.vector.tensor_copy(c0[:, :, 0:48].rearrange("p t (j c) -> p t j c", c=3),
                                      g0[:, :, :, ds(b * 3, 3)])
                nc.vector.tensor_copy(c1[:], g1[:, :, ds(b * 12, 12)])
                nc.vector.tensor_copy(c2[:], g2[:, :, ds(b * 48, 48)]).then_inc(s_cut, 1)
                dve.wait_ge(s_h, after(b + 1))
                for t in range(2):
                    nc.vector.tensor_tensor(tile_of(k.h, b * NT + t), pH[:, t * C:(t + 1) * C], bf[:],
                                            ALU.add).then_inc(s_hs, 1)

        @block.tensor
        def _(pe):
            pe.wait_ge(s_id, after(3))
            pe.wait_ge(s_w, after(16 * 9))
            with pe.Fori(0, B) as b:
                pe.wait_ge(s_cut, after(b + 1))
                pe.wait_ge(s_trs, after(3 * b))
                nc.tensor.transpose(pT0[:, 0:P], c0[:, :, :].rearrange("p t c -> p (t c)"), k.ident[:])
                for i in range(2):
                    nc.tensor.transpose(pT1[0:KT, i * 64:(i + 1) * 64],
                                        c1[:, i * 8:(i + 1) * 8, :].rearrange("p j c -> p (j c)"), k.ident[0:64, 0:64])
                flat2 = c2[:, :, :].rearrange("p j c -> p (j c)")
                for i in range(6):
                    last = nc.tensor.transpose(pT1[:, P + i * 16:P + (i + 1) * 16], flat2[:, i * P:(i + 1) * P],
                                               k.ident[0:16, 0:16])
                last.then_inc(s_tr, 1)
                pe.wait_ge(s_trs, after(3 * b + 3))
                pe.wait_ge(s_y, after(5 * b))
                pe.wait_ge(s_lvs, after(2 * b))
                for i in range(6):
                    nc.tensor.matmul(pO[0:16, 64:128], t2T[:, i, :], w2T[:, i, :], start=i == 0, stop=i == 5)
                for i in range(2):
                    nc.tensor.matmul(pO[0:64, 0:64], t1T[:, i, :], w1T[:, i, :], start=i == 0, stop=i == 1)
                for t in range(2):
                    last = nc.tensor.matmul(pY[0:64, t, 0:P], w0T[64 * t:64 * t + 48, :], t0T[64 * t:64 * t + 48, :],
                                            start=True, stop=True)
                last.then_inc(s_lv, 1)
                pe.wait_ge(s_lvs, after(2 * b + 2))
                nc.tensor.matmul(pU[0:64, 256:512], o2[:], up2[:], start=True, stop=True)
                nc.tensor.matmul(pU[0:64, 0:256], o1[:], up1[:], start=True, stop=True).then_inc(s_up, 1)
                pe.wait_ge(s_y, after(5 * b + 5))
                pe.wait_ge(s_hs, after(2 * b))
                for t in range(2):
                    for i in range(3):
                        last = nc.tensor.matmul(pH[:, t * C:(t + 1) * C], yT[:, i, t * P:(t + 1) * P], wfT[:, i, :],
                                                start=i == 0, stop=i == 2)
                last.then_inc(s_h, 1)

        @block.scalar
        def _(act):
            act.wait_ge(s_w, after(16 * 9))
            with act.Fori(0, B) as b:
                act.wait_ge(s_tr, after(b + 1))
                act.wait_ge(s_lv, after(b))
                nc.scalar.activation(t0T[:], pT0[:, 0:P], ACT.Copy).then_inc(s_trs, 1)
                nc.scalar.activation(t1T[:].rearrange("p i t -> p (i t)"), pT1[0:KT, 0:128], ACT.Copy).then_inc(s_trs, 1)
                nc.scalar.activation(t2T[:].rearrange("p i t -> p (i t)"), pT1[:, 128:224], ACT.Copy).then_inc(s_trs, 1)
                act.wait_ge(s_lv, after(b + 1))
                act.wait_ge(s_up, after(b))
                nc.scalar.activation(o1[:], pO[0:64, 0:64], ACT.Copy).then_inc(s_lvs, 1)
                nc.scalar.activation(o2[:], pO[0:16, 64:128], ACT.Copy).then_inc(s_lvs, 1)
                act.wait_ge(s_h, after(b))
                for t in range(2):
                    nc.scalar.activation(yT[:, 0, t * P:(t + 1) * P], pY[0:64, t, 0:P], ACT.Identity,
                                         bias=lb[:, 0:1]).then_inc(s_y, 1)
                act.wait_ge(s_up, after(b + 1))
                for i in (1, 2):
                    nc.scalar.activation(yT[:, i, :], pU[0:64, (i - 1) * 256:i * 256], ACT.Identity,
                                         bias=lb[:, i:i + 1]).then_inc(s_y, 1)
                act.wait_ge(s_y, after(5 * b + 4))
                act.sem_inc(s_y, 1)


def attention(k):
    nc, d = k.nc, k.d
    with ExitStack() as ctx:
        sb = lambda n, s, dt=F32: k.sb(n, s, dt, ctx)
        wq = sb("wq", [KT, 2, 2, P])
        wk = sb("wk", [KT, 2, 2, P])
        wv = sb("wv", [KT, 2, C])
        wp = sb("wp", [KT, 2, C])
        bp = sb("bp", [1, C])
        krow = sb("krow", [P, 1])
        xn = sb("xn", [P, NT, C])
        xnT = sb("xnT", [KT, 2, NTOK])
        qT = sb("qT", [P, 2, NTOK])
        kT = sb("kT", [P, 2, NTOK])
        qA = sb("qA", [P, 2, NTOK])
        va = sb("va", [P, NT, NH0, DH0 + 1])
        mp = sb("mp", [P, NT, 2, 4, 32])
        pT = sb("pT", [P, NT, 2, 4, NTOK])
        rec = sb("rec", [P, NT, NH0])
        at = sb("at", [P, NT, NH0, DH0])
        aT = sb("aT", [KT, 2, NTOK])
        S = k.ps("aS", [P, 4, 512], ctx)
        Gp = k.ps("aG", [P, 4, 512], ctx)
        names = ("w", "st", "lk", "pre", "xn", "xt", "xts", "q", "k", "v", "qs", "ks", "vs", "s1", "mx", "mt", "qa", "s2",
                 "ex", "pv", "rc", "at", "tt", "tts", "pj", "hs")
        (s_w, s_st, s_lk, s_pre, s_xn, s_xt, s_xts, s_q, s_k, s_v, s_qs, s_ks, s_vs, s_s1, s_mx, s_mt, s_qa, s_s2, s_ex,
         s_pv, s_rc, s_at, s_tt, s_tts, s_pj, s_hs) = (k.sem("a_" + n) for n in names)
        s_var, s_root = k.sem("a_var"), k.sem("a_root")
        block = ctx.enter_context(nc.Block())

        @block.sync
        def _(sp):
            k.start_at_one(sp)
            for t, n in ((wq, "wq"), (wk, "wk"), (wv, "wv"), (wp, "wp"), (bp, "bp"), (krow, "krow")):
                sp.dma_start(t[:], d[n]).then_inc(s_w, 16)
            sp.wait_ge(s_w, after(96))

        @block.gpsimd
        def _(pool):
            nc.gpsimd.memset(mp[:], 0.0).then_inc(s_pre, 1)
            nc.gpsimd.memset(va[:], 1.0).then_inc(s_pre, 1)
            root_step(k, pool, s_var, s_root)
            pool.wait_ge(s_pre, after(2))

        @block.vector
        def _(dve):
            stats_of_h(k, dve, s_st, s_lk, s_var, s_root)
            dve.wait_ge(s_pre, after(2))
            with dve.Fori(0, B) as b:
                dve.wait_ge(s_xt, after(b))
                for t in range(NT):
                    nc.vector.tensor_scalar(xn[:, t, :], tile_of(k.h, b * NT + t), column_of(k.mean, b * NT + t),
                                            column_of(k.rstd, b * NT + t), ALU.subtract, ALU.mult).then_inc(s_xn, 1)
                dve.wait_ge(s_q, after(b + 1))
                for g in range(2):
                    nc.vector.tensor_scalar(qT[:, g, :], Gp[:, 2 + g, 0:NTOK], SCALE, None, ALU.mult).then_inc(s_qs, 1)
                dve.wait_ge(s_v, after(b + 1))
                nc.vector.tensor_copy(va[:, :, :, 0:DH0],
                                      S[:, 0:NT, 0:C].rearrange("p t (h c) -> p t h c", c=DH0)).then_inc(s_vs, 1)
                for n in range(6):
                    dve.wait_ge(s_s1, after(b * 6 + n + 1))
                    nc.vector.tensor_reduce(mp[:, n // 2, n % 2, :, 24:25], S[:, :, 0:NTOK], AX.X, ALU.max,
                                            negate=True).then_inc(s_mx, 1)
                for g in range(2):
                    dve.wait_ge(s_mt, after(b * 2 + g + 1))
                    nc.vector.tensor_tensor(qA[:, g, :], Gp[:, g, 0:NTOK], qT[:, g, :], ALU.add).then_inc(s_qa, 1)
                dve.wait_ge(s_pv, after(b + 1))
                for t in range(NT):
                    o = Gp[:, 2 + t // 2, (t % 2) * 256:(t % 2) * 256 + 256].rearrange("p (h c) -> p h c", c=32)
                    nc.vector.reciprocal(rec[:, t, :].rearrange("p (h a) -> p h a", a=1), o[:, :, DH0:DH0 + 1]).then_inc(s_rc, 1)
                for t in range(NT):
                    o = Gp[:, 2 + t // 2, (t % 2) * 256:(t % 2) * 256 + 256].rearrange("p (h c) -> p h c", c=32)
                    dve.wait_ge(s_rc, after(b * NT + t + 1))
                    nc.vector.tensor_tensor(at[:, t, :, :], o[:, :, 0:DH0],
                                            rec[:, t, :].rearrange("p (h a) -> p h a", a=1).broadcast_to([P, NH0, DH0]),
                                            ALU.mult).then_inc(s_at, 1)
                for t in range(NT):
                    dve.wait_ge(s_pj, after(b * NT + t + 1))
                    nc.vector.tensor_tensor(tile_of(k.h, b * NT + t), tile_of(k.h, b * NT + t), S[:, t, 0:C],
                                            ALU.add).then_inc(s_hs, 1)

        @block.tensor
        def _(pe):
            pe.wait_ge(s_w, after(96))
            with pe.Fori(0, B) as b:
                pe.wait_ge(s_xn, after(NT * b + NT))
                pe.wait_ge(s_tts, after(2 * b))
                for t in range(NT):
                    for i in range(2):
                        last = nc.tensor.transpose(Gp[0:KT, i, t * P:(t + 1) * P], xn[:, t, i * KT:(i + 1) * KT], k.ident[:])
                last.then_inc(s_xt, 1)
                pe.wait_ge(s_xts, after(2 * b + 2))
                pe.wait_ge(s_at, after(NT * b))
                for g in range(2):
                    for i in range(2):
                        last = nc.tensor.matmul(Gp[:, 2 + g, 0:NTOK], wq[:, i, g, :], xnT[:, i, :], start=i == 0, stop=i == 1)
                last.then_inc(s_q, 1)
                for g in range(2):
                    for i in range(2):
                        last = nc.tensor.matmul(Gp[:, g, 0:NTOK], wk[:, i, g, :], xnT[:, i, :], start=i == 0, stop=i == 1)
                last.then_inc(s_k, 1)
                pe.wait_ge(s_hs, after(NT * b))
                for t in range(NT):
                    for i in range(2):
                        last = nc.tensor.matmul(S[:, t, 0:C], xnT[:, i, t * P:(t + 1) * P], wv[:, i, :],
                                                start=i == 0, stop=i == 1)
                last.then_inc(s_v, 1)
                pe.wait_ge(s_qs, after(2 * b + 2))
                pe.wait_ge(s_ks, after(2 * b + 2))
                pe.wait_ge(s_vs, after(b + 1))
                for n in range(6):
                    t, g = n // 2, n % 2
                    if n:
                        pe.wait_ge(s_mx, after(b * 6 + n))
                    for j in range(4):
                        last = nc.tensor.matmul(S[:, j, 0:NTOK], qT[32 * j:32 * j + 32, g, t * P:(t + 1) * P],
                                                kT[32 * j:32 * j + 32, g, :], start=True, stop=True)
                    last.then_inc(s_s1, 1)
                pe.wait_ge(s_mx, after(b * 6 + 6))
                for g in range(2):
                    for t in range(NT):
                        last = nc.tensor.transpose(Gp[:, g, t * P:(t + 1) * P],
                                                   mp[:, t, g, :, :].rearrange("p h c -> p (h c)"), k.ident[:])
                    last.then_inc(s_mt, 1)
                for n in range(6):
                    t, g = n % NT, n // NT
                    if t == 0:
                        pe.wait_ge(s_qa, after(b * 2 + g + 1))
                    if n:
                        pe.wait_ge(s_ex, after(b * 6 + n))
                    for j in range(4):
                        last = nc.tensor.matmul(S[:, j, 0:NTOK], kT[32 * j:32 * j + 32, g, t * P:(t + 1) * P],
                                                qA[32 * j:32 * j + 32, g, :], start=True, stop=True)
                    last.then_inc(s_s2, 1)
                pe.wait_ge(s_ex, after(b * 6 + 6))
                for t in range(NT):
                    for h in range(NH0):
                        o = (t % 2) * 256 + h * 32
                        for kt in range(NT):
                            last = nc.tensor.matmul(Gp[:, 2 + t // 2, o:o + DH0 + 1], pT[:, kt, h // 4, h % 4, t * P:(t + 1) * P],
                                                    va[:, kt, h, :], start=kt == 0, stop=kt == NT - 1)
                last.then_inc(s_pv, 1)
                for t in range(NT):
                    pe.wait_ge(s_at, after(NT * b + t + 1))
                    flat = at[:, t, :, :].rearrange("p h c -> p (h c)")
                    for i in range(2):
                        last = nc.tensor.transpose(Gp[0:KT, i, t * P:(t + 1) * P], flat[:, i * KT:(i + 1) * KT], k.ident[:])
                last.then_inc(s_tt, 1)
                pe.wait_ge(s_tts, after(2 * b + 2))
                for t in range(NT):
                    for i in range(2):
                        nc.tensor.matmul(S[:, t, 0:C], aT[:, i, t * P:(t + 1) * P], wp[:, i, :], start=i == 0, stop=False)
                    nc.tensor.matmul(S[:, t, 0:C], k.ones[0:1, :], bp[:], start=False, stop=True).then_inc(s_pj, 1)

        @block.scalar
        def _(act):
            act.wait_ge(s_w, after(96))
            with act.Fori(0, B) as b:
                act.wait_ge(s_xt, after(b + 1))
                act.wait_ge(s_v, after(b))
                for i in range(2):
                    nc.scalar.activation(xnT[:, i, :], Gp[0:KT, i, 0:NTOK], ACT.Copy).then_inc(s_xts, 1)
                act.wait_ge(s_k, after(b + 1))
                act.wait_ge(s_s2, after(6 * b))
                for g in range(2):
                    nc.scalar.activation(kT[:, g, :], Gp[:, g, 0:NTOK], ACT.Identity, bias=krow[:]).then_inc(s_ks, 1)
                act.wait_ge(s_pv, after(b))
                for n in range(6):
                    act.wait_ge(s_s2, after(b * 6 + n + 1))
                    nc.scalar.activation(pT[:, n % NT, n // NT, :, :], S[:, :, 0:NTOK], ACT.Exp).then_inc(s_ex, 1)
                act.wait_ge(s_tt, after(b + 1))
                act.wait_ge(s_pj, after(NT * b))
                for i in range(2):
                    nc.scalar.activation(aT[:, i, :], Gp[0:KT, i, 0:NTOK], ACT.Copy).then_inc(s_tts, 1)


def route(k, tag, top, ntiles, gw, gb):
    nc, d = k.nc, k.d
    NC = top
    with ExitStack() as ctx:
        sb = lambda n, s, dt=F32: k.sb(tag + n, s, dt, ctx)
        w = sb("w", [KT, 2, E])
        bias = sb("bias", [1, E])
        tri = sb("tri", [P, P])
        rank8 = sb("rank8", [P, E])
        seg = sb("seg", [P, E, NC * G])
        starts = sb("starts", [1, ntiles])
        xb = sb("xb", [P, 4, C])
        xT = sb("xT", [KT, 2, 4 * P])
        lg = sb("lg", [P, G, E])
        pr = sb("pr", [P, G, E])
        key = sb("key", [P, G, E])
        oh = sb("oh", [P, E, NC, G])
        m1 = sb("m1", [P, 3, G])
        tot = sb("tot", [P, E, NC, G])
        inc = sb("inc", [P, E, NC, G])
        ne = sb("ne", [P, 3, E])
        nei = sb("nei", [P, E], I32)
        ends = sb("ends", [P, E])
        posf = sb("posf", [P, NC, G])
        cmp = sb("cmp", [1, ntiles, E])
        eidf = sb("eidf", [1, ntiles])
        xo = sb("xo", [P, 2, C])
        ib = sb("ib", [P, 2, NC], I32)
        pX = k.ps(tag + "pX", [P, 2, 512], ctx)
        pL = k.ps(tag + "pL", [P, 512], ctx)
        pC = k.ps(tag + "pC", [P, 512], ctx)
        pS = k.ps(tag + "pS", [P, 512], ctx)
        s_w, s_c, s_st, s_lk, s_xb, s_xt, s_xts, s_l, s_ls, s_d, s_oh, s_cnt, s_pos, s_xo = (
            k.sem(tag + n) for n in ("w", "c", "st", "lk", "xb", "xt", "xts", "l", "ls", "d", "oh", "cnt", "pos", "xo"))
        s_ib = k.plain_sem(tag + "ib")
        s_sc = [k.plain_sem(tag + f"sc{i}") for i in range(2)]
        s_var, s_root = k.sem(tag + "var"), k.sem(tag + "root")
        block = ctx.enter_context(nc.Block())

        def per_tile(t):
            return t.rearrange("p (g a) -> p g a", a=1).broadcast_to([P, G, E])

        @block.sync
        def _(sp):
            k.start_at_one(sp)
            for t, n in ((w, gw), (tri, "tri"), (rank8, "rank8")):
                sp.dma_start(t[:], d[n]).then_inc(s_w, 16)
            sp.dma_start(bias[:], d[gb]).then_inc(s_w, 16)
            sp.dma_start(starts[:], d["starts"][:, 0:ntiles]).then_inc(s_w, 16)
            sp.wait_ge(s_w, after(80))

        @block.gpsimd
        def _(pool):
            nc.gpsimd.memset(seg[:], 1.0).then_inc(s_c, 1)
            pool.wait_ge(s_c, after(1))
            nc.gpsimd.memset(seg[:, :, 0:1], 0.0).then_inc(s_c, 1)
            root_step(k, pool, s_var, s_root)
            pool.wait_ge(s_pos, after(1))
            if top == 2:
                pool.wait_ge(k.s_consts, after(16 * (N0 // 8)))
            def scatter(g, i, s):
                pool.sem_clear(s_ib)
                if type(g) is not int:
                    pool.wait_ge(s_sc[s], i * (16 * NC))
                pool.wait_ge(s_xo, after(g + 1))
                for c in range(NC):
                    nc.gpsimd.tensor_copy(ib[:, s, c:c + 1], k.pos[:, c, ds(g, 1)]).then_inc(s_ib, 1)
                pool.wait_ge(s_ib, NC)
                for c in range(NC):
                    nc.gpsimd.indirect_dma_start(k.xs, bass.IndirectOffsetOnAxis(ap=ib[:, s, c:c + 1], axis=0),
                                                 xo[:, s, :], None).then_inc(s_sc[s], 16)

            paired(pool, G, scatter)
            for s in range(2):
                pool.wait_ge(s_sc[s], 16 * NC * G // 2)

        @block.vector
        def _(dve):
            v = nc.vector
            stats_of_h(k, dve, s_st, s_lk, s_var, s_root)
            dve.wait_ge(s_w, after(80))
            dve.wait_ge(s_c, after(2))
            with dve.Fori(0, G // 4) as i:
                dve.wait_ge(s_xt, after(i))
                for t in range(4):
                    g = i * 4 + t
                    v.tensor_scalar(xb[:, t, :], tile_of(k.h, g), column_of(k.mean, g), column_of(k.rstd, g),
                                    ALU.subtract, ALU.mult).then_inc(s_xb, 1)
                dve.wait_ge(s_l, after(i + 1))
                v.tensor_copy(lg[:, ds(i * 4, 4), :], pL[:, 0:4 * E].rearrange("p (t e) -> p t e", e=E)).then_inc(s_ls, 1)
            dve.wait_ge(s_ls, after(G // 4))
            link = linker(dve, s_d)
            link(v.tensor_reduce(m1[:, 0, :], lg[:], AX.X, ALU.max))
            link(v.tensor_tensor(pr[:], lg[:], per_tile(m1[:, 0, :]), ALU.subtract))
            dve.sem_inc(s_oh, 1)
            dve.wait_ge(s_cnt, after(1))
            link(v.tensor_reduce(m1[:, 1, :], pr[:], AX.X, ALU.add))
            link(v.reciprocal(m1[:, 2, :], m1[:, 1, :]))
            link(v.tensor_tensor(pr[:], pr[:], per_tile(m1[:, 2, :]), ALU.mult))
            rank_b = rank8[:, :].rearrange("p (a e) -> p a e", a=1).broadcast_to([P, G, E])
            for c in range(NC):
                link(v.tensor_reduce(k.wtop[:, c, :], pr[:], AX.X, ALU.max))
                link(v.tensor_tensor(key[:], pr[:], per_tile(k.wtop[:, c, :]), ALU.is_equal))
                link(v.tensor_tensor(key[:], key[:], rank_b, ALU.mult))
                link(v.tensor_reduce(m1[:, 0, :], key[:], AX.X, ALU.max))
                ohc = oh[:, :, c, :].rearrange("p e g -> p g e")
                link(v.tensor_tensor(ohc, key[:], per_tile(m1[:, 0, :]), ALU.is_equal))
                if c + 1 < NC:
                    link(v.tensor_tensor(pr[:], pr[:], ohc, ALU.subtract))
            if NC == 2:
                link(v.tensor_tensor(m1[:, 0, :], k.wtop[:, 0, :], k.wtop[:, 1, :], ALU.add))
                link(v.reciprocal(m1[:, 1, :], m1[:, 0, :]))
                for c in range(2):
                    link(v.tensor_tensor(k.wtop[:, c, :], k.wtop[:, c, :], m1[:, 1, :], ALU.mult))
            dve.sem_inc(s_oh, 1)
            dve.wait_ge(s_cnt, after(2))
            n = E * NC * G
            flat = lambda t: t[:].rearrange("p e c g -> p (e c g)")
            link(v.tensor_copy(flat(tot), pS[:, 0:n]))
            link(v.tensor_tensor_scan(flat(inc), seg[:].rearrange("p e n -> p (e n)"), flat(tot), 0.0, ALU.mult, ALU.add))
            last = inc[:, :, NC - 1, G - 1]
            link(v.tensor_scalar(ne[:, 0, :], last, float(P - 1), None, ALU.add))
            link(v.tensor_copy(nei[:], ne[:, 0, :]))
            link(v.tensor_scalar(nei[:], nei[:], -P, None, ALU.bitwise_and))
            link(v.tensor_copy(ne[:, 2, :], nei[:]))
            link(v.tensor_tensor_scan(ends[:], k.ones[:, 0:E], ne[:, 2, :], 0.0, ALU.mult, ALU.add))
            link(v.tensor_tensor(ne[:, 0, :], ends[:], ne[:, 2, :], ALU.subtract))
            link(v.tensor_tensor(flat(inc), flat(inc), flat(tot), ALU.subtract))
            link(v.tensor_tensor(flat(inc), flat(inc), pC[:, 0:n], ALU.add))
            link(v.tensor_tensor(inc[:].rearrange("p e c g -> p e (c g)"), inc[:].rearrange("p e c g -> p e (c g)"),
                                 ne[:, 0, :].rearrange("p (e a) -> p e a", a=1).broadcast_to([P, E, NC * G]), ALU.add))
            link(v.tensor_tensor(flat(inc), flat(inc), flat(oh), ALU.mult))
            link(v.tensor_reduce(posf[:].rearrange("p c g -> p (c g)"), inc[:].rearrange("p e c g -> p (c g) e"),
                                 AX.X, ALU.add))
            link(v.tensor_copy(k.pos[:, 0:NC, :], posf[:]))
            dve.sem_inc(s_pos, 1)
            link(v.tensor_tensor(cmp[:], ends[0:1, :].rearrange("p (a e) -> p a e", a=1).broadcast_to([1, ntiles, E]),
                                 starts[:, :].rearrange("p (n a) -> p n a", a=1).broadcast_to([1, ntiles, E]), ALU.is_le))
            link(v.tensor_reduce(eidf[:], cmp[:], AX.X, ALU.add))
            link(v.tensor_scalar(eidf[:], eidf[:], float(E - 1), None, ALU.min))
            link(v.tensor_copy(k.eid[:, 0:ntiles], eidf[:]))

            def rows(g, i, s):
                if type(g) is not int:
                    dve.wait_ge(s_sc[s], i * (16 * NC))
                v.tensor_scalar(xo[:, s, :], tile_of(k.h, g), column_of(k.mean, g), column_of(k.rstd, g),
                                ALU.subtract, ALU.mult).then_inc(s_xo, 1)

            paired(dve, G, rows)

        @block.tensor
        def _(pe):
            pe.wait_ge(s_w, after(80))
            with pe.Fori(0, G // 4) as i:
                pe.wait_ge(s_xb, after(i * 4 + 4))
                pe.wait_ge(s_xts, after(i * 2))
                for t in range(4):
                    for c in range(2):
                        last = nc.tensor.transpose(pX[0:KT, c, t * P:(t + 1) * P], xb[:, t, c * KT:(c + 1) * KT], k.ident[:])
                last.then_inc(s_xt, 1)
                pe.wait_ge(s_xts, after(i * 2 + 2))
                pe.wait_ge(s_ls, after(i))
                for t in range(4):
                    for c in range(2):
                        nc.tensor.matmul(pL[:, t * E:(t + 1) * E], xT[:, c, t * P:(t + 1) * P], w[:, c, :], start=c == 0, stop=False)
                    last = nc.tensor.matmul(pL[:, t * E:(t + 1) * E], k.ones[0:1, :], bias[:], start=False, stop=True)
                last.then_inc(s_l, 1)
            pe.wait_ge(s_oh, after(2))
            n = E * NC * G
            oh_flat = oh[:].rearrange("p e c g -> p (e c g)")
            nc.tensor.matmul(pC[:, 0:n], tri[:], oh_flat, start=True, stop=True)
            nc.tensor.matmul(pS[:, 0:n], k.ones[:], oh_flat, start=True, stop=True).then_inc(s_cnt, 1)

        @block.scalar
        def _(act):
            with act.Fori(0, G // 4) as i:
                act.wait_ge(s_xt, after(i + 1))
                act.wait_ge(s_l, after(i))
                for c in range(2):
                    nc.scalar.activation(xT[:, c, :], pX[0:KT, c, :], ACT.Copy).then_inc(s_xts, 1)
            act.wait_ge(s_oh, after(1))
            nc.scalar.activation(pr[:].rearrange("p g e -> p (g e)"), pr[:].rearrange("p g e -> p (g e)"),
                                 ACT.Exp).then_inc(s_cnt, 1)


def paired(eng, tiles, step):
    for s in range(2):
        step(s, 0, s)
    with eng.Fori(1, tiles // 2) as i:
        for s in range(2):
            step(i * 2 + s, i, s)


def pipelined(eng, tiles, front, back):
    front(0, 0, 0)
    with eng.Fori(0, tiles // 2 - 1) as i:
        front(i * 2 + 1, i, 1)
        back(i * 2, i, 0)
        front(i * 2 + 2, i + 1, 0)
        back(i * 2 + 1, i, 1)
    front(tiles - 1, tiles // 2 - 1, 1)
    back(tiles - 2, tiles // 2 - 1, 0)
    back(tiles - 1, tiles // 2 - 1, 1)


def move_rows(sp, x, src, s_x, s_used, y, dst, s_st, s_ready, tiles):
    def load(n, s):
        sp.dma_start(x[:, s, :], src[ds(n * P, P), :] if type(n) is not int else src[n * P:(n + 1) * P, :]).then_inc(s_x[s], 16)

    def store(n, s):
        sp.wait_ge(s_ready, after(n + 1))
        sp.dma_start(dst[ds(n * P, P), :] if type(n) is not int else dst[n * P:(n + 1) * P, :], y[:, s, :]).then_inc(s_st[s], 16)

    load(0, 0)
    load(1, 1)
    with sp.Fori(0, tiles // 2 - 1) as i:
        for s in range(2):
            sp.wait_ge(s_used, after(i * 2 + s + 1))
            load(i * 2 + s + 2, s)
            store(i * 2 + s, s)
    for s in range(2):
        store(tiles - 2 + s, s)
    for s in range(2):
        sp.wait_ge(s_st[s], after(16 * tiles // 2))


def experts0(k):
    nc, d = k.nc, k.d
    NM = F0 // P
    HF = F0 // 2
    with ExitStack() as ctx:
        sb = lambda n, s, dt=F32: k.sb(n, s, dt, ctx)
        w1 = sb("e_w1", [KT + 1, 2, E, F0])
        w2 = sb("e_w2", [P, E, NM, C])
        b2 = sb("e_b2", [1, E, C])
        x = sb("e_x", [P, 2, C])
        xT = sb("e_xT", [KT + 1, 2, 2, P])
        hb = sb("e_h", [P, 2, 2, HF])
        hT = sb("e_hT", [P, 2, NM, P])
        y = sb("e_y", [P, 2, C])
        pX = k.ps("e_pX", [P, 512], ctx)
        pH = k.ps("e_pH", [P, 2, 2, 512], ctx)
        pT = k.ps("e_pT", [P, 2, 512], ctx)
        pY = k.ps("e_pY", [P, 512], ctx)
        s_w, s_on, s_xt, s_xts, s_h, s_hs, s_ht, s_hts, s_y, s_ys = (
            k.sem("e_" + n) for n in ("w", "on", "xt", "xts", "h", "hs", "ht", "hts", "y", "ys"))
        s_x = [k.sem(f"e_x{i}") for i in range(2)]
        s_st = [k.sem(f"e_st{i}") for i in range(2)]
        block = ctx.enter_context(nc.Block())

        @block.sync
        def _(sp):
            k.start_at_one(sp)
            for e in range(E):
                sp.dma_start(w1[:, :, e, :], d["e0w1"][:, :, e, :]).then_inc(s_w, 16)
                sp.dma_start(w2[:, e, :, :], d["e0w2"][:, e, :, :]).then_inc(s_w, 16)
            sp.dma_start(b2[:], d["e0b2"]).then_inc(s_w, 16)
            move_rows(sp, x, k.xs, s_x, s_xt, y, k.ys, s_st, s_ys, N0)

        @block.tensor
        def _(pe):
            pe.wait_ge(s_w, after(16 * (2 * E + 1)))
            pe.wait_ge(s_on, after(1))

            def front(n, i, s):
                e = pe.value_load(k.eid[0:1, ds(n, 1)], min_val=0, max_val=E - 1)
                pe.wait_ge(s_x[s], after(i * 16 + 16))
                pe.wait_ge(s_xts, after(n))
                for c in range(2):
                    last = nc.tensor.transpose(pX[0:KT, c * P:(c + 1) * P], x[:, s, c * KT:(c + 1) * KT], k.ident[:])
                last.then_inc(s_xt, 1)
                pe.wait_ge(s_xts, after(n + 1))
                if type(n) is not int or n > 1:
                    pe.wait_ge(s_hs, after(n - 1))
                for c in range(2):
                    for f in range(2):
                        last = nc.tensor.matmul(pH[:, s, f, 0:HF], xT[0:KT + c, s, c, :],
                                                w1[0:KT + c, c, ds(e, 1), f * HF:(f + 1) * HF].rearrange("p a f -> p (a f)"),
                                                start=c == 0, stop=c == 1)
                last.then_inc(s_h, 1)

            def back(n, i, s):
                e = pe.value_load(k.eid[0:1, ds(n, 1)], min_val=0, max_val=E - 1)
                pe.wait_ge(s_hs, after(n + 1))
                pe.wait_ge(s_hts, after(n))
                for m in range(NM):
                    last = nc.tensor.transpose(pT[:, m // 3, (m % 3) * P:(m % 3 + 1) * P],
                                               hb[:, s, m // 3, (m % 3) * P:(m % 3 + 1) * P], k.ident[:])
                last.then_inc(s_ht, 1)
                pe.wait_ge(s_hts, after(n + 1))
                pe.wait_ge(s_ys, after(n))
                for m in range(NM):
                    nc.tensor.matmul(pY[:, 0:C], hT[:, s, m, :], w2[:, ds(e, 1), m, :].rearrange("p a c -> p (a c)"),
                                     start=m == 0, stop=False)
                nc.tensor.matmul(pY[:, 0:C], k.ones[0:1, :], b2[:, ds(e, 1), :].rearrange("p a c -> p (a c)"),
                                 start=False, stop=True).then_inc(s_y, 1)

            pipelined(pe, N0, front, back)

        @block.scalar
        def _(act):
            act.preload_act_table(ACT.Gelu)

            def front(n, i, s):
                act.wait_ge(s_h, after(n + 1))
                if type(n) is not int or n > 1:
                    act.wait_ge(s_ht, after(n - 1))
                nc.scalar.activation(hb[:, s, :, :], pH[:, s, :, 0:HF], ACT.Gelu).then_inc(s_hs, 1)

            def back(n, i, s):
                act.wait_ge(s_st[s], after(i * 16))
                act.wait_ge(s_y, after(n + 1))
                nc.scalar.activation(y[:, s, :], pY[:, 0:C], ACT.Copy).then_inc(s_ys, 1)

            pipelined(act, N0, front, back)

        @block.vector
        def _(dve):
            nc.vector.memset(xT[KT:KT + 1, :, :, :], 1.0).then_inc(s_on, 1)

            def front(n, i, s):
                dve.wait_ge(s_xt, after(n + 1))
                nc.vector.tensor_copy(xT[0:KT, s, :, :],
                                      pX[0:KT, 0:2 * P].rearrange("p (c t) -> p c t", c=2)).then_inc(s_xts, 1)

            def back(n, i, s):
                dve.wait_ge(s_ht, after(n + 1))
                nc.vector.tensor_copy(hT[:, s, :, :].rearrange("p (a m) t -> p a (m t)", a=2),
                                      pT[:, :, 0:3 * P]).then_inc(s_hts, 1)

            pipelined(dve, N0, front, back)


def combine0(k):
    nc = k.nc
    with ExitStack() as ctx:
        ya = k.sb("cb_y", [P, 2, 2, C], F32, ctx)
        ib = k.sb("cb_i", [P, 2, 2], I32, ctx)
        s_a, s_h = k.sem("cb_a"), k.sem("cb_h")
        s_ib = k.plain_sem("cb_ib")
        s_g = [k.plain_sem(f"cb_g{i}") for i in range(2)]
        block = ctx.enter_context(nc.Block())

        @block.sync
        def _(sp):
            k.start_at_one(sp)

        @block.gpsimd
        def _(pool):
            def gather(g, i, s):
                pool.sem_clear(s_ib)
                if type(g) is not int:
                    pool.wait_ge(s_g[s], i * 32)
                pool.wait_ge(s_h, after(i * 2))
                for c in range(2):
                    nc.gpsimd.tensor_copy(ib[:, s, c:c + 1], k.pos[:, c, ds(g, 1)]).then_inc(s_ib, 1)
                pool.wait_ge(s_ib, 2)
                for c in range(2):
                    nc.gpsimd.indirect_dma_start(ya[:, s, c, :], None, k.ys,
                                                 bass.IndirectOffsetOnAxis(ap=ib[:, s, c:c + 1], axis=0)).then_inc(s_g[s], 16)

            paired(pool, G, gather)

        @block.vector
        def _(dve):
            with dve.Fori(0, G // 2) as i:
                for s in range(2):
                    g = i * 2 + s
                    dve.wait_ge(s_g[s], i * 32 + 32)
                    nc.vector.scalar_tensor_tensor(out=tile_of(k.h, g), in0=ya[:, s, 0, :], scalar=k.wtop[:, 0, ds(g, 1)],
                                                   in1=tile_of(k.h, g), op0=ALU.mult, op1=ALU.add).then_inc(s_a, 1)
                    dve.wait_ge(s_a, after(g + 1))
                    nc.vector.scalar_tensor_tensor(out=tile_of(k.h, g), in0=ya[:, s, 1, :], scalar=k.wtop[:, 1, ds(g, 1)],
                                                   in1=tile_of(k.h, g), op0=ALU.mult, op1=ALU.add).then_inc(s_h, 1)


def experts1(k):
    nc, d = k.nc, k.d
    NM = F1 // P
    with ExitStack() as ctx:
        sb = lambda n, s, dt=F32: k.sb(n, s, dt, ctx)
        w1 = sb("f_w1", [KT, 2, E, F1])
        w2 = sb("f_w2", [KT, 2, E, F1])
        w3 = sb("f_w3", [P, E, NM, C])
        x = sb("f_x", [P, 2, C])
        xT = sb("f_xT", [KT, 2, 2, P])
        sl = sb("f_sl", [P, 2, F1])
        hb = sb("f_h", [P, 2, F1])
        hT = sb("f_hT", [P, 2, NM, P])
        y = sb("f_y", [P, 2, C], BF16)
        pX = k.ps("f_pX", [P, 512], ctx)
        pA = k.ps("f_pA", [P, 2, 512], ctx)
        pB = k.ps("f_pB", [P, 2, 512], ctx)
        pT = k.ps("f_pT", [P, 512], ctx)
        pY = k.ps("f_pY", [P, 512], ctx)
        s_w, s_xt, s_xts, s_h, s_sl, s_hs, s_ht, s_hts, s_y, s_ys = (
            k.sem("f_" + n) for n in ("w", "xt", "xts", "h", "sl", "hs", "ht", "hts", "y", "ys"))
        s_x = [k.sem(f"f_x{i}") for i in range(2)]
        s_st = [k.sem(f"f_st{i}") for i in range(2)]
        block = ctx.enter_context(nc.Block())

        @block.sync
        def _(sp):
            k.start_at_one(sp)
            for e in range(E):
                sp.dma_start(w1[:, :, e, :], d["e1w1"][:, :, e, :]).then_inc(s_w, 16)
                sp.dma_start(w2[:, :, e, :], d["e1w2"][:, :, e, :]).then_inc(s_w, 16)
                sp.dma_start(w3[:, e, :, :], d["e1w3"][:, e, :, :]).then_inc(s_w, 16)
            move_rows(sp, x, k.xs, s_x, s_xt, y, k.ys1, s_st, s_ys, N1)

        @block.tensor
        def _(pe):
            pe.wait_ge(s_w, after(16 * 3 * E))

            def front(n, i, s):
                e = pe.value_load(k.eid[0:1, ds(n, 1)], min_val=0, max_val=E - 1)
                pe.wait_ge(s_x[s], after(i * 16 + 16))
                pe.wait_ge(s_xts, after(n))
                for c in range(2):
                    last = nc.tensor.transpose(pX[0:KT, c * P:(c + 1) * P], x[:, s, c * KT:(c + 1) * KT], k.ident[:])
                last.then_inc(s_xt, 1)
                pe.wait_ge(s_xts, after(n + 1))
                if type(n) is not int or n > 1:
                    pe.wait_ge(s_hs, after(n - 1))
                for c in range(2):
                    for p, w in ((pA, w1), (pB, w2)):
                        last = nc.tensor.matmul(p[:, s, :], xT[:, s, c, :],
                                                w[:, c, ds(e, 1), :].rearrange("p a f -> p (a f)"),
                                                start=c == 0, stop=c == 1)
                last.then_inc(s_h, 1)

            def back(n, i, s):
                e = pe.value_load(k.eid[0:1, ds(n, 1)], min_val=0, max_val=E - 1)
                pe.wait_ge(s_hs, after(n + 1))
                pe.wait_ge(s_hts, after(n))
                for m in range(NM):
                    last = nc.tensor.transpose(pT[:, m * P:(m + 1) * P], hb[:, s, m * P:(m + 1) * P], k.ident[:])
                last.then_inc(s_ht, 1)
                pe.wait_ge(s_hts, after(n + 1))
                pe.wait_ge(s_ys, after(n))
                for m in range(NM):
                    last = nc.tensor.matmul(pY[:, 0:C], hT[:, s, m, :], w3[:, ds(e, 1), m, :].rearrange("p a c -> p (a c)"),
                                            start=m == 0, stop=m == NM - 1)
                last.then_inc(s_y, 1)

            pipelined(pe, N1, front, back)

        @block.scalar
        def _(act):
            act.preload_act_table(ACT.Silu)

            def front(n, i, s):
                act.wait_ge(s_h, after(n + 1))
                if type(n) is not int or n > 1:
                    act.wait_ge(s_hs, after(n - 1))
                nc.scalar.activation(sl[:, s, :], pA[:, s, :], ACT.Silu).then_inc(s_sl, 1)

            def back(n, i, s):
                act.wait_ge(s_ht, after(n + 1))
                nc.scalar.activation(hT[:, s, :, :].rearrange("p m t -> p (m t)"), pT[:, :], ACT.Copy).then_inc(s_hts, 1)
                act.wait_ge(s_st[s], after(i * 16))
                act.wait_ge(s_y, after(n + 1))
                nc.scalar.activation(y[:, s, :], pY[:, 0:C], ACT.Copy).then_inc(s_ys, 1)

            pipelined(act, N1, front, back)

        @block.vector
        def _(dve):
            def front(n, i, s):
                dve.wait_ge(s_xt, after(n + 1))
                nc.vector.tensor_copy(xT[:, s, :, :],
                                      pX[0:KT, 0:2 * P].rearrange("p (c t) -> p c t", c=2)).then_inc(s_xts, 1)
                dve.wait_ge(s_sl, after(n + 1))
                if type(n) is not int or n > 1:
                    dve.wait_ge(s_ht, after(n - 1))
                nc.vector.tensor_tensor(hb[:, s, :], pB[:, s, :], sl[:, s, :], ALU.mult).then_inc(s_hs, 1)

            pipelined(dve, N1, front, lambda n, i, s: None)


def finish(k):
    nc, d = k.nc, k.d
    with ExitStack() as ctx:
        ya = k.sb("fi_y", [P, 2, C], BF16, ctx)
        ib = k.sb("fi_i", [P, 2], I32, ctx)
        s_h, s_o = k.sem("fi_h"), k.sem("fi_o")
        s_ib = k.plain_sem("fi_ib")
        s_g = [k.plain_sem(f"fi_g{i}") for i in range(2)]
        block = ctx.enter_context(nc.Block())

        @block.gpsimd
        def _(pool):
            def gather(g, i, s):
                pool.sem_clear(s_ib)
                if type(g) is not int:
                    pool.wait_ge(s_g[s], i * 16)
                pool.wait_ge(s_h, after(i * 2))
                nc.gpsimd.tensor_copy(ib[:, s:s + 1], k.pos[:, 0, ds(g, 1)]).then_inc(s_ib, 1)
                pool.wait_ge(s_ib, 1)
                nc.gpsimd.indirect_dma_start(ya[:, s, :], None, k.ys1,
                                             bass.IndirectOffsetOnAxis(ap=ib[:, s:s + 1], axis=0)).then_inc(s_g[s], 16)

            paired(pool, G, gather)

        @block.vector
        def _(dve):
            with dve.Fori(0, G // 2) as i:
                for s in range(2):
                    g = i * 2 + s
                    dve.wait_ge(s_g[s], i * 16 + 16)
                    nc.vector.scalar_tensor_tensor(out=tile_of(k.h, g), in0=ya[:, s, :], scalar=k.wtop[:, 0, ds(g, 1)],
                                                   in1=tile_of(k.h, g), op0=ALU.mult, op1=ALU.add).then_inc(s_h, 1)

        @block.sync
        def _(sp):
            k.start_at_one(sp)
            store_result(sp, k, s_o, lambda b: sp.wait_ge(s_h, after(b * NT + NT)))


def store_result(sp, k, s_o, ready=lambda b: None):
    out = k.d["out"]
    with sp.Fori(0, B) as b:
        ready(b)
        for t in range(NT):
            sp.dma_start(out[ds(b, 1), t * P:(t + 1) * P, :].rearrange("a p c -> p (a c)"),
                         tile_of(k.h, b * NT + t)).then_inc(s_o, 16)
    sp.wait_ge(s_o, after(16 * G))


def dump(k):
    with ExitStack() as ctx:
        s_o = k.sem("dump")
        block = ctx.enter_context(k.nc.Block())

        @block.sync
        def _(sp):
            k.start_at_one(sp)
            store_result(sp, k, s_o)


def second_stats(k):
    nc = k.nc
    with ExitStack() as ctx:
        xa = k.sb("ss_x", [P, 4, C], F32, ctx)
        s_st, s_lk, s_var, s_root, s_x, s_b, s_c = (k.sem("ss_" + n) for n in ("st", "lk", "var", "root", "x", "b", "c"))
        block = ctx.enter_context(nc.Block())

        @block.sync
        def _(sp):
            k.start_at_one(sp)

        @block.gpsimd
        def _(pool):
            root_step(k, pool, s_var, s_root)
            pool.wait_ge(s_var, after(2))
            nc.gpsimd.tensor_tensor(k.rstd2[:], k.vare[:], k.half[:, 0:G], ALU.pow).then_inc(s_root, 1)

        @block.vector
        def _(dve):
            stats_of_h(k, dve, s_st, s_lk, s_var, s_root)
            with dve.Fori(0, G // 4) as i:
                dve.wait_ge(s_b, after(i * 4))
                for t in range(4):
                    g = i * 4 + t
                    nc.vector.tensor_scalar(xa[:, t, :], tile_of(k.h, g), column_of(k.mean, g), column_of(k.rstd, g),
                                            ALU.subtract, ALU.mult).then_inc(s_x, 1)
                dve.wait_ge(s_x, after(i * 4 + 4))
                for t in range(4):
                    nc.vector.bn_stats(tile_of(k.stats, i * 4 + t), xa[:, t, :]).then_inc(s_b, 1)
            dve.wait_ge(s_b, after(G))
            nc.vector.tensor_copy(k.mean1[:], k.mean[:]).then_inc(s_c, 1)
            dve.wait_ge(s_c, after(1))
            finish_stats(k, linker(dve, s_lk, 7)).then_inc(s_var, 1)
            dve.wait_ge(s_root, after(2))


def memory(k):
    nc, d = k.nc, k.d
    with ExitStack() as mctx:
        k.mean1 = k.sb("mean1", [P, G], F32, mctx)
        k.rstd2 = k.sb("rstd2", [P, G], F32, mctx)
        y = k.sb("m_y", [P, G, C], F32, mctx)
        second_stats(k)
        fast_weights(k, y)
        gate(k, y)


def fast_weights(k, y):
    nc, d = k.nc, k.d
    HF = PW // 2
    with ExitStack() as ctx:
        sb = lambda n, s, dt=F32: k.sb("m_" + n, s, dt, ctx)
        wa = sb("wa", [P, 3, PW])
        wb = sb("wb", [KB, 3, PW])
        ma = sb("ma", [P, 3, MOD])
        mb = sb("mb", [P, 3, MOD])
        mbias = sb("mbias", [64 + MOD, 3])
        lin = sb("lin", [P, 2, C])
        gb = sb("gb", [P, 3, 2, HD])
        lr = sb("lr", [P, 4, H])
        gv = sb("gv", [P, 2, H, HD])
        beta = sb("beta", [P, H, HD])
        up = sb("up", [P, P])
        maskA = sb("maskA", [P, H, P])
        up0 = sb("up0", [P, P])
        corner = sb("corner", [P, LEVELS, P], I32)
        wm = sb("wm", [P, 3 * H])
        woT = sb("woT", [P, H // 2, C])
        xf = sb("xf", [P, 4, 256])
        x0 = sb("x0", [P, P])
        x1 = sb("x1", [P, P])
        xk = sb("xk", [P, 3, P])
        zc = sb("zc", [P, PW])
        sq = sb("sq", [P, PW])
        sm = sb("sm", [P, 4, H])
        z = sb("z", [P, 3, PW])
        dummy = sb("dummy", [1, LEVELS * NG])
        kb = sb("kb", [P, PW])
        kq = sb("kq", [P, H // 2, 2, P])
        kz = sb("kz", [P, H, P])
        AT = sb("AT", [P, H, P])
        PT = sb("PT", [P, H, P])
        T = sb("T", [P, H, P])
        U = sb("U", [P, H, P])
        X = sb("X", [P, H, P])
        R = sb("R", [P, NG, 4 * HD + 32])
        D = sb("D", [P, PW])
        oT = sb("oT", [P, H // 2, P])
        S = sb("S", [P, H // 2, 2, HD])
        pj = k.ps("m_pj", [P, 2, 512], ctx)
        pg = k.ps("m_pg", [P, 2 * NG, 512], ctx)
        names = ("w c lk var root xf xt xts hd hds pj pjs z1 sq ss rt z2 z3 tr trs kz kk kks "
                 "u0 t1 t1s mx mxs my mys mu mus ks r dd dds ot ots su st yo yos").split()
        s = {n: k.sem("m_" + n) for n in names}
        block = ctx.enter_context(nc.Block())
        heads = lambda t: t.rearrange("p (h c) -> p h c", c=HD)
        per_head = lambda t: t.rearrange("p (h a) -> p h a", a=1).broadcast_to([P, H, HD])
        all_heads = lambda t: t.rearrange("p (a c) -> p a c", a=1).broadcast_to([P, H, HD])
        quad = lambda t, g: t[:, 4 * g:4 * g + 4, :].rearrange("p h c -> p (h c)")
        a_ = lambda g: pg[:, 2 * g, :]
        b_ = lambda g: pg[:, 2 * g + 1, :]

        @block.sync
        def _(sp):
            k.start_at_one(sp)
            for t, n in ((wa, "wa"), (wb, "wb"), (ma, "ma"), (mb, "mb"), (up, "up"), (up0, "up0"), (corner, "corner"),
                         (woT, "woT")):
                sp.dma_start(t[:], d[n]).then_inc(s["w"], 16)
            sp.dma_start(mbias[64:64 + MOD, :], d["mbias"]).then_inc(s["w"], 16)
            sp.dma_start(lin[:], d["lin"].broadcast_to([P, 2, C])).then_inc(s["w"], 16)
            sp.dma_start(gb[:], d["gb"].broadcast_to([P, 3, 2, HD])).then_inc(s["w"], 16)
            sp.dma_start(lr[:, 0, :], d["lr_scale"].broadcast_to([P, H])).then_inc(s["w"], 16)
            sp.wait_ge(s["w"], after(16 * 12))

        @block.gpsimd
        def _(pool):
            gp = nc.gpsimd
            for t in (xf, kz, R, S):
                gp.memset(t[:], 0.0)
            gp.memset(xk[:], 1.0).then_inc(s["c"], 1)

            def tile(n):
                for m in range(3):
                    pool.wait_ge(s["var"], after(n * 4 + (m if m == 0 else m + 1) + 1))
                    gp.tensor_tensor(sm[:, 1, :], sm[:, 0, :], k.half[:, 0:H], ALU.pow).then_inc(s["root"], 1)
                    pool.wait_ge(s["z1"], after(n * 3 + m + 1))
                    zm = heads(z[:, m, :])
                    gp.tensor_tensor(zm, zm, gv[:, 0, :, :] if m == 1 else all_heads(gb[:, m, 0, :]),
                                     ALU.mult).then_inc(s["z2"], 1)
                    pool.wait_ge(s["z2"], after(n * 3 + m + 1))
                    gp.tensor_tensor(zm, zm, gv[:, 1, :, :] if m == 1 else all_heads(gb[:, m, 1, :]),
                                     ALU.add).then_inc(s["z3"], 1)
                    if m == 0:
                        pool.wait_ge(s["var"], after(n * 4 + 2))
                        gp.tensor_tensor(sm[:, 1, :], sm[:, 0, :], k.half2[:, 0:H], ALU.pow).then_inc(s["root"], 1)

            with pool.Fori(0, B) as b:
                for c in range(NT):
                    tile(b * NT + c)

        @block.vector
        def _(dve):
            v = nc.vector
            dve.wait_ge(s["w"], after(16 * 12))
            dve.wait_ge(s["c"], after(1))
            lkn = [0]

            def link(ins):
                lkn[0] += 1
                ins.then_inc(s["lk"], 1)
                dve.wait_ge(s["lk"], after(lkn[0]))
            link(v.tensor_scalar(wb[64:KB, :, :], wb[64:KB, :, :], 0.1, None, ALU.mult))
            for w, n in ((wa, P), (wb, KB)):
                w3 = w[:, :, :].rearrange("p m (h c) -> p (m h) c", c=HD)
                link(v.tensor_reduce(wm[0:n, :], w3, AX.X, ALU.add))
                link(v.tensor_scalar(wm[0:n, :], wm[0:n, :], 1.0 / HD, None, ALU.mult))
                link(v.tensor_tensor(w3, w3, wm[0:n, :].rearrange("p (h a) -> p h a", a=1).broadcast_to([n, 3 * H, HD]),
                                     ALU.subtract))
            dve.wait_ge(s["hds"], after(1))
            link(v.tensor_scalar(lr[:, 1, :], lr[:, 1, :], 1.0, None, ALU.add))
            link(v.reciprocal(lr[:, 0, :], lr[:, 1, :]))
            link(v.tensor_scalar(lr[:, 1, :], lr[:, 0, :], 0.2, None, ALU.mult))
            link(v.tensor_scalar(lr[:, 2, :], lr[:, 1, :], 1.0, None, ALU.add))
            link(v.reciprocal(lr[:, 0, :], lr[:, 2, :]))
            link(v.scalar_tensor_tensor(out=lr[:, 3, :], in0=lr[:, 1, :], scalar=-1.0, in1=lr[:, 0, :], op0=ALU.mult,
                                        op1=ALU.mult))
            for i in range(2):
                link(v.tensor_tensor(gv[:, i, :, :], all_heads(gb[:, 1, i, :]), per_head(lr[:, 3, :]), ALU.mult))
            link(v.tensor_scalar(lr[:, 1, :], lr[:, 2, :], -1.0, None, ALU.mult))
            link(v.tensor_copy(beta[:], per_head(lr[:, 2, :])))
            link(v.tensor_tensor(maskA[:], up[:, :].rearrange("p (a c) -> p a c", a=1).broadcast_to([P, H, P]),
                                 lr[:, 1, :].rearrange("p (h a) -> p h a", a=1).broadcast_to([P, H, P]), ALU.mult))

            def tile(g, n, c, first):
                dve.wait_ge(s["xt"], after(n))
                steps = [v.tensor_scalar(xf[:, 0, 0:C], tile_of(k.h, g), column_of(k.mean1, g), column_of(k.rstd, g),
                                         ALU.subtract, ALU.mult),
                         lambda: v.tensor_scalar(xf[:, 1, 0:C], xf[:, 0, 0:C], column_of(k.mean, g), column_of(k.rstd2, g),
                                                 ALU.subtract, ALU.mult),
                         lambda: v.tensor_tensor(xf[:, 2, 0:C], xf[:, 1, 0:C], lin[:, 0, :], ALU.mult),
                         lambda: v.tensor_tensor(xf[:, 3, 0:C], xf[:, 2, 0:C], lin[:, 1, :], ALU.add)]
                for j, st in enumerate(steps):
                    (st() if j else st).then_inc(s["xf"], 1)
                    dve.wait_ge(s["xf"], after(n * 4 + j + 1))
                vc, zs = 0, 0
                for m in range(3):
                    dve.wait_ge(s["sq"], after(n * 4 + (m if m == 0 else m + 1) + 1))
                    v.tensor_reduce(sm[:, 2, :], heads(sq[:]), AX.X, ALU.add).then_inc(s["ss"], 1)
                    dve.wait_ge(s["ss"], after(n * 3 + m + 1))
                    v.tensor_scalar(sm[:, 0, :], sm[:, 2, :], 1.0 / HD, EPS, ALU.mult, ALU.add).then_inc(s["var"], 1)
                    dve.wait_ge(s["root"], after(n * 4 + (m if m == 0 else m + 1) + 1))
                    if m == 2:
                        dve.wait_ge(s["tr"], after(n))
                    v.tensor_tensor(heads(z[:, m, :]), heads(zc[:]), per_head(sm[:, 1, :]), ALU.mult).then_inc(s["z1"], 1)
                    if m == 0:
                        dve.wait_ge(s["sq"], after(n * 4 + 2))
                        v.tensor_reduce(sm[:, 0, :], heads(sq[:]), AX.X, ALU.add).then_inc(s["var"], 1)
                        dve.wait_ge(s["root"], after(n * 4 + 2))
                        v.tensor_scalar(sm[:, 2, :], sm[:, 1, :], 1e-6, None, ALU.add).then_inc(s["rt"], 1)
                        dve.wait_ge(s["rt"], after(n * 4 + 1))
                        v.reciprocal(sm[:, 3, :], sm[:, 2, :]).then_inc(s["rt"], 1)
                        dve.wait_ge(s["rt"], after(n * 4 + 2))
                        v.tensor_tensor(heads(z[:, 0, :]), heads(z[:, 0, :]), per_head(sm[:, 3, :]), ALU.mult).then_inc(s["rt"], 1)
                        dve.wait_ge(s["rt"], after(n * 4 + 3))
                        v.tensor_tensor(heads(kb[:]), heads(z[:, 0, :]), beta[:], ALU.mult).then_inc(s["rt"], 1)
                for p3 in range(2):
                    dve.wait_ge(s["trs"], after(n * 4 + p3 + 1))
                    for o in (0, 64):
                        v.tensor_copy(kz[o:o + 64, p3 * 6 + o // 64:p3 * 6 + 6:2, :],
                                      kq[o:o + 64, 3 * p3:3 * p3 + 3, 0, :]).then_inc(s["kz"], 1)
                for g3 in range(NG):
                    dve.wait_ge(s["kk"], after(n * NG + g3 + 1))
                    for half in range(2):
                        pair = pg[:, 2 * g3 + half, :].rearrange("p (h a t) -> p h a t", h=2, a=2)
                        h = 4 * g3 + 2 * half
                        v.tensor_tensor(AT[:, h:h + 2, :], pair[:, :, 0, :], maskA[:, h:h + 2, :], ALU.mult).then_inc(s["kks"], 1)
                        v.tensor_tensor(PT[:, h:h + 2, :], pair[:, :, 1, :], maskA[:, h:h + 2, :], ALU.mult).then_inc(s["kks"], 1)
                three = lambda t: t.rearrange("p (a c) -> p a c", a=1).broadcast_to([P, 4, P])
                for g3 in range(NG):
                    q4 = slice(4 * g3, 4 * g3 + 4)
                    dve.wait_ge(s["kks"], after(n * 12 + 4 * g3 + 3))
                    v.tensor_tensor(X[:, q4, :], AT[:, q4, :], three(up0[:]), ALU.mult).then_inc(s["u0"], 1)
                    dve.wait_ge(s["u0"], after(n * 6 + 2 * g3 + 1))
                    v.tensor_tensor(U[:, q4, :], X[:, q4, :], three(k.ident[:]), ALU.add).then_inc(s["u0"], 1)
                for lv in range(1, LEVELS):
                    for g3 in range(NG):
                        q4 = slice(4 * g3, 4 * g3 + 4)
                        dve.wait_ge(s["my"], after(n * 18 + (lv - 1) * NG + g3 + 1))
                        v.memset(dummy[:, lv * NG + g3:lv * NG + g3 + 1], 0.0)
                        v.copy_predicated(T[:, q4, :], three(corner[:, lv, :]),
                                          b_(g3).rearrange("p (h t) -> p h t", t=P)).then_inc(s["mys"], 1)
                for g3 in range(NG):
                    if first:
                        v.tensor_copy(R[:, g3, 0:256], z[:, 1, 256 * g3:256 * g3 + 256]).then_inc(s["r"], 1)
                    else:
                        dve.wait_ge(s["ks"], after(n * NG + g3 + 1))
                        v.tensor_tensor(R[:, g3, 0:256], a_(g3)[:, 0:256], z[:, 1, 256 * g3:256 * g3 + 256],
                                        ALU.add).then_inc(s["r"], 1)
                for g3 in range(NG):
                    if c < NT - 1:
                        dve.wait_ge(s["su"], after(n * NG + g3 + 1))
                        src = b_(g3)[:, 256:512].rearrange("p (q a c) -> p q a c", q=2, a=2)
                        for o in (0, 64):
                            dst = S[o:o + 64, 2 * g3:2 * g3 + 2, o // 64, :]
                            if first:
                                v.tensor_scalar(dst, src[o:o + 64, :, o // 64, :], -1.0, None, ALU.mult).then_inc(s["st"], 1)
                            else:
                                v.tensor_tensor(dst, dst, src[o:o + 64, :, o // 64, :], ALU.subtract).then_inc(s["st"], 1)
                    else:
                        dve.sem_inc(s["st"], 2)
                dve.wait_ge(s["yo"], after(n + 1))
                v.tensor_copy(tile_of(y, g), pj[:, 0, 0:C]).then_inc(s["yos"], 1)

            with dve.Fori(0, B) as b:
                for c in range(NT):
                    tile(b * NT + c, b * NT + c, c, c == 0)

        @block.tensor
        def _(pe):
            mm = nc.tensor.matmul
            pe.wait_ge(s["w"], after(16 * 12))
            pe.wait_ge(s["lk"], after(7))

            def tile(n, c, first):
                pe.wait_ge(s["xf"], after(n * 4 + 4))
                pe.wait_ge(s["yos"], after(n))
                for i in range(2):
                    last = nc.tensor.transpose(pj[:, 0, i * P:(i + 1) * P], xf[:, 3, i * P:(i + 1) * P], k.ident[:])
                last.then_inc(s["xt"], 1)
                pe.wait_ge(s["xts"], after(n * 3 + 3))
                for m in range(3):
                    mm(pj[64:64 + MOD, 1, m * P:(m + 1) * P], ma[:, m, :], x0[:], start=True, stop=False)
                    last = mm(pj[64:64 + MOD, 1, m * P:(m + 1) * P], mb[:, m, :], x1[:], start=False, stop=True)
                last.then_inc(s["hd"], 1)
                pe.wait_ge(s["hds"], after(n * 3 + 4))
                for m in range(3):
                    pe.wait_ge(s["pjs"], after(n * 3 + m))
                    for f in range(2):
                        mm(pj[:, f, 0:HF], x0[:], wa[:, m, f * HF:(f + 1) * HF], start=True, stop=False)
                        last = mm(pj[:, f, 0:HF], xk[0:KB, m, :], wb[:, m, f * HF:(f + 1) * HF], start=False, stop=True)
                    last.then_inc(s["pj"], 1)
                pe.wait_ge(s["pjs"], after(n * 3 + 3))
                for m, src in ((0, 0), (1, 2)):
                    pe.wait_ge(s["z3"], after(n * 3 + src + 1))
                    if m == 0:
                        pe.wait_ge(s["rt"], after(n * 4 + 3))
                    for f in range(2):
                        if m == 1:
                            pe.wait_ge(s["trs"], after(n * 4 + f + 1))
                        for q in range(3):
                            last = nc.tensor.transpose(pj[:, f, q * P:(q + 1) * P], z[:, src, (3 * f + q) * P:(3 * f + q + 1) * P],
                                                       k.ident[:])
                        last.then_inc(s["tr"], 1)
                pe.wait_ge(s["trs"], after(n * 4 + 4))
                pe.wait_ge(s["kz"], after(n * 4 + 4))
                pe.wait_ge(s["dds"], after(n * 3))
                pe.wait_ge(s["ots"], after(n * 3))
                pe.wait_ge(s["st"], after(n * 6))
                for g3 in range(NG):
                    for hh in range(4):
                        h = 4 * g3 + hh
                        last = mm(pg[:, 2 * g3 + hh // 2, (hh % 2) * 256:(hh % 2) * 256 + 256], kz[:, h, :],
                                  kq[:, h // 2, :, :].rearrange("p a t -> p (a t)"), start=True, stop=True)
                    last.then_inc(s["kk"], 1)
                for g3 in range(NG):
                    pe.wait_ge(s["u0"], after(n * 6 + 2 * g3 + 2))
                    pe.wait_ge(s["kks"], after(n * 12 + 4 * g3 + 4))
                    for hh in range(4):
                        last = nc.tensor.transpose(a_(g3)[:, hh * P:(hh + 1) * P], U[:, 4 * g3 + hh, :], k.ident[:])
                    last.then_inc(s["t1"], 1)
                for lv in range(1, LEVELS):
                    j = n * 18 + (lv - 1) * NG
                    for g3 in range(NG):
                        if lv == 1:
                            pe.wait_ge(s["t1s"], after(n * NG + g3 + 1))
                        else:
                            pe.wait_ge(s["mus"], after(j - NG + g3 + 1))
                        for hh in range(4):
                            h = 4 * g3 + hh
                            last = mm(a_(g3)[:, hh * P:(hh + 1) * P], AT[:, h, :], T[:, h, :], start=True, stop=True)
                        last.then_inc(s["mx"], 1)
                    for g3 in range(NG):
                        pe.wait_ge(s["mxs"], after(j + g3 + 1))
                        for hh in range(4):
                            h = 4 * g3 + hh
                            last = mm(b_(g3)[:, hh * P:(hh + 1) * P], U[:, h, :], X[:, h, :], start=True, stop=True)
                        last.then_inc(s["my"], 1)
                    for g3 in range(NG):
                        pe.wait_ge(s["mys"], after(j + g3 + 1))
                        for hh in range(4):
                            last = nc.tensor.transpose(a_(g3)[:, hh * P:(hh + 1) * P], T[:, 4 * g3 + hh, :], k.ident[:])
                        last.then_inc(s["mu"], 1)
                for g3 in range(NG if not first else 0):
                    pe.wait_ge(s["mus"], after(n * 18 + 15 + g3 + 1))
                    if not first:
                        for q in range(2):
                            pr = 2 * g3 + q
                            last = mm(a_(g3)[:, q * P:(q + 1) * P], kq[:, pr, 0, :], S[:, pr, :, :].rearrange("p a c -> p (a c)"),
                                      start=True, stop=True)
                        last.then_inc(s["ks"], 1)
                if first:
                    pe.wait_ge(s["mus"], after(n * 18 + 18))
                    pe.sem_inc(s["ks"], 3)
                for g3 in range(NG):
                    pe.wait_ge(s["r"], after(n * NG + g3 + 1))
                    for hh in range(4):
                        h = 4 * g3 + hh
                        last = mm(b_(g3)[:, hh * P:hh * P + 96], U[:, h, :], R[:, g3, hh * HD:hh * HD + 96], start=True, stop=True)
                    last.then_inc(s["dd"], 1)
                for g3 in range(NG):
                    pe.wait_ge(s["dds"], after(n * NG + g3 + 1))
                    for q in range(2):
                        pr = 2 * g3 + q
                        o = a_(g3)[:, q * P:(q + 1) * P]
                        if not first:
                            mm(o, S[:, pr, :, :].rearrange("p a c -> p (a c)"), kq[:, pr, 1, :], start=True, stop=False,
                               skip_group_check=True)
                        for e in range(2):
                            h = 2 * pr + e
                            last = mm(a_(g3)[64 * e:64 * e + 64, q * P:(q + 1) * P], D[:, h * HD:(h + 1) * HD], PT[:, h, :],
                                      start=first, stop=True, skip_group_check=True)
                    last.then_inc(s["ot"], 1)
                    if c < NT - 1:
                        for q in range(2):
                            pr = 2 * g3 + q
                            last = mm(b_(g3)[:, 256 + q * P:256 + (q + 1) * P], kb[:, pr * P:(pr + 1) * P],
                                      D[:, pr * P:(pr + 1) * P], start=True, stop=True)
                        last.then_inc(s["su"], 1)
                if c == NT - 1:
                    pe.sem_inc(s["su"], 3)
                pe.wait_ge(s["ots"], after(n * NG + 3))
                for q in range(H // 2):
                    last = mm(pj[:, 0, 0:C], oT[:, q, :], woT[:, q, :], start=q == 0, stop=q == H // 2 - 1)
                last.then_inc(s["yo"], 1)

            with pe.Fori(0, B) as b:
                for c in range(NT):
                    tile(b * NT + c, c, c == 0)

        @block.scalar
        def _(act):
            A = nc.scalar.activation
            act.wait_ge(s["w"], after(16 * 12))
            A(lr[:, 1, :], lr[:, 0, :], ACT.Exp, scale=-1.0).then_inc(s["hds"], 1)
            act.preload_act_table(ACT.Gelu)

            def tile(n, c, first):
                act.wait_ge(s["xt"], after(n + 1))
                act.wait_ge(s["pj"], after(n * 3))
                A(x0[:], pj[:, 0, 0:P], ACT.Copy).then_inc(s["xts"], 1)
                A(x1[:], pj[:, 0, P:2 * P], ACT.Copy).then_inc(s["xts"], 1)
                A(xk[0:64, :, :], pj[0:64, 0, P:2 * P].rearrange("p (a t) -> p a t", a=1).broadcast_to([64, 3, P]),
                  ACT.Copy).then_inc(s["xts"], 1)
                act.wait_ge(s["hd"], after(n + 1))
                for m in range(3):
                    A(xk[64:64 + MOD, m, :], pj[64:64 + MOD, 1, m * P:(m + 1) * P], ACT.Gelu,
                      bias=mbias[64:64 + MOD, m:m + 1]).then_inc(s["hds"], 1)
                for m in range(3):
                    act.wait_ge(s["pj"], after(n * 3 + m + 1))
                    act.wait_ge(s["z1"], after(n * 3 + m))
                    if m == 1:
                        act.wait_ge(s["var"], after(n * 4 + 2))
                    A(zc[:].rearrange("p (f c) -> p f c", f=2), pj[:, :, 0:HF], ACT.Copy).then_inc(s["pjs"], 1) if False else \
                        A(zc[:].rearrange("p (f c) -> p f c", f=2), pj[:, :, 0:HF], ACT.Copy)
                    A(sq[:].rearrange("p (f c) -> p f c", f=2), pj[:, :, 0:HF], ACT.Square).then_inc(s["sq"], 1)
                    act.wait_ge(s["sq"], after(n * 4 + (m if m == 0 else m + 1) + 1))
                    act.sem_inc(s["pjs"], 1)
                    if m == 0:
                        act.wait_ge(s["z3"], after(n * 3 + 1))
                        act.wait_ge(s["var"], after(n * 4 + 1))
                        A(sq[:], z[:, 0, :], ACT.Square).then_inc(s["sq"], 1)
                for m in range(2):
                    for f in range(2):
                        act.wait_ge(s["tr"], after(n * 4 + 2 * m + f + 1))
                        A(kq[:, 3 * f:3 * f + 3, m, :], pj[:, f, 0:3 * P].rearrange("p (h t) -> p h t", t=P),
                          ACT.Copy).then_inc(s["trs"], 1)
                for g3 in range(NG):
                    act.wait_ge(s["t1"], after(n * NG + g3 + 1))
                    A(quad(T, g3), a_(g3), ACT.Copy).then_inc(s["t1s"], 1)
                for lv in range(1, LEVELS):
                    j = n * 18 + (lv - 1) * NG
                    for g3 in range(NG):
                        act.wait_ge(s["mx"], after(j + g3 + 1))
                        A(quad(X, g3), a_(g3), ACT.Copy).then_inc(s["mxs"], 1)
                    for g3 in range(NG):
                        act.wait_ge(s["mu"], after(j + g3 + 1))
                        A(quad(U, g3), a_(g3), ACT.Copy).then_inc(s["mus"], 1)
                for g3 in range(NG):
                    act.wait_ge(s["dd"], after(n * NG + g3 + 1))
                    act.wait_ge(s["su"], after(n * NG))
                    A(heads(D[:, 256 * g3:256 * g3 + 256]), b_(g3).rearrange("p (h t) -> p h t", t=P)[:, :, 0:HD],
                      ACT.Copy).then_inc(s["dds"], 1)
                act.wait_ge(s["yo"], after(n))
                for g3 in range(NG):
                    act.wait_ge(s["ot"], after(n * NG + g3 + 1))
                    A(oT[:, 2 * g3:2 * g3 + 2, :].rearrange("p q t -> p (q t)"), a_(g3)[:, 0:256], ACT.Copy).then_inc(s["ots"], 1)

            with act.Fori(0, B) as b:
                for c in range(NT):
                    tile(b * NT + c, c, c == 0)


def gate(k, y):
    nc, d = k.nc, k.d
    with ExitStack() as ctx:
        sb = lambda n, s, dt=F32: k.sb("g_" + n, s, dt, ctx)
        wg = sb("wg", [KT + 1, 2, C])
        xb = sb("xb", [P, 2, C])
        xT = sb("xT", [KT + 1, 2, 2 * P])
        sg = sb("sg", [P, 2, C])
        pX = k.ps("g_pX", [P, 2, 512], ctx)
        pG = k.ps("g_pG", [P, 512], ctx)
        s_w, s_on, s_x, s_xt, s_xts, s_g, s_sg, s_m, s_h = (k.sem("g_" + n) for n in ("w", "on", "x", "xt", "xts", "g", "sg", "m", "h"))
        block = ctx.enter_context(nc.Block())

        @block.sync
        def _(sp):
            k.start_at_one(sp)
            sp.dma_start(wg[:], d["wg"]).then_inc(s_w, 16)
            sp.wait_ge(s_w, after(16))

        @block.vector
        def _(dve):
            nc.vector.memset(xT[KT:KT + 1, :, :], 1.0).then_inc(s_on, 1)
            with dve.Fori(0, G // 2) as i:
                dve.wait_ge(s_xt, after(i))
                for t in range(2):
                    g = i * 2 + t
                    nc.vector.tensor_scalar(xb[:, t, :], tile_of(k.h, g), column_of(k.mean1, g), column_of(k.rstd, g),
                                            ALU.subtract, ALU.mult).then_inc(s_x, 1)
                dve.wait_ge(s_sg, after(i + 1))
                for t in range(2):
                    nc.vector.tensor_tensor(sg[:, t, :], sg[:, t, :], tile_of(y, i * 2 + t), ALU.mult).then_inc(s_m, 1)
                dve.wait_ge(s_m, after(i * 2 + 2))
                for t in range(2):
                    nc.vector.tensor_tensor(tile_of(k.h, i * 2 + t), tile_of(k.h, i * 2 + t), sg[:, t, :], ALU.add).then_inc(s_h, 1)

        @block.tensor
        def _(pe):
            pe.wait_ge(s_w, after(16))
            pe.wait_ge(s_on, after(1))
            with pe.Fori(0, G // 2) as i:
                pe.wait_ge(s_x, after(i * 2 + 2))
                pe.wait_ge(s_xts, after(i * 2))
                for t in range(2):
                    for c in range(2):
                        last = nc.tensor.transpose(pX[0:KT, c, t * P:(t + 1) * P], xb[:, t, c * KT:(c + 1) * KT], k.ident[:])
                last.then_inc(s_xt, 1)
                pe.wait_ge(s_xts, after(i * 2 + 2))
                pe.wait_ge(s_sg, after(i))
                for t in range(2):
                    for c in range(2):
                        last = nc.tensor.matmul(pG[:, t * C:(t + 1) * C], xT[0:KT + c, c, t * P:(t + 1) * P], wg[0:KT + c, c, :],
                                                start=c == 0, stop=c == 1)
                last.then_inc(s_g, 1)

        @block.scalar
        def _(act):
            act.preload_act_table(ACT.Sigmoid)
            with act.Fori(0, G // 2) as i:
                act.wait_ge(s_xt, after(i + 1))
                for c in range(2):
                    nc.scalar.activation(xT[0:KT, c, :], pX[0:KT, c, 0:2 * P], ACT.Copy).then_inc(s_xts, 1)
                act.wait_ge(s_g, after(i + 1))
                act.wait_ge(s_h, after(i * 2))
                nc.scalar.activation(sg[:].rearrange("p t c -> p (t c)"), pG[:, 0:2 * C], ACT.Sigmoid).then_inc(s_sg, 1)


def build(nc, d, stop=99):
    with ExitStack() as ctx:
        k = Core(nc, ctx, d)
        stages = [tokenizer, attention,
                  lambda k: route(k, "r0", 2, N0, "gate0_w", "gate0_b"), experts0, combine0,
                  lambda k: (k.recycle(), memory(k)),
                  lambda k: route(k, "r1", 1, N1, "gate1_w", "gate1_b"), experts1, finish]
        for f in stages[:stop]:
            f(k)
        if stop < len(stages):
            dump(k)


def hostprep(inputs):
    f = lambda n: np.asarray(inputs[n])
    a = {}
    x = f("x")
    for lv, p in enumerate((1, 2, 4)):
        n = 64 // p
        a[f"x{lv}r"] = x.reshape(B, 3, n, p, n, p).transpose(2, 4, 0, 3, 5, 1).reshape(n * n, B * p * p * 3)
        a[f"idx{lv}"] = f(f"L0_tok_idx{lv}")
    w0 = np.zeros((P, 64), np.float32)
    w0[0:48] = f("L0_tok_W0").T
    w0[64:112] = f("L0_tok_W0").T
    a["w0T"] = w0
    a["w1T"] = f("L0_tok_W1").T.reshape(2, KT, 64).transpose(1, 0, 2)
    a["w2T"] = f("L0_tok_W2").T.reshape(6, P, 64).transpose(1, 0, 2)
    a["wfT"] = f("L0_tok_Wf").T.reshape(3, 64, C).transpose(1, 0, 2)
    a["lb"] = np.stack([f("L0_tok_b0"), f("L0_tok_b1"), f("L0_tok_b2")], 1)
    a["bf"] = f("L0_tok_bf")[None]
    a["txt"] = f("txt")
    for name, n in (("up1", 64), ("up2", 16)):
        m = np.zeros((n, 256), np.float32)
        at = np.clip((np.arange(256, dtype=np.float32) + np.float32(0.5)) * np.float32(n / 256) - np.float32(0.5), 0, n - 1)
        lo = np.floor(at).astype(int)
        for t in range(256):
            m[lo[t], t] += 1 - (at[t] - lo[t])
            m[min(lo[t] + 1, n - 1), t] += at[t] - lo[t]
        a[name] = m
    w = f("L0_attn_w_qkv")

    def heads(w):
        o = np.zeros((2, KT, NH0, 32), np.float32)
        o[..., 0:DH0] = w.reshape(2, KT, NH0, DH0)
        return o.reshape(2, KT, 2, P).transpose(1, 0, 2, 3)
    tiles = lambda w: w.reshape(2, KT, -1).transpose(1, 0, 2)
    a["wq"], a["wk"], a["wv"] = heads(w[:, 0:C]), heads(w[:, C:2 * C]), tiles(w[:, 2 * C:])
    a["wp"], a["bp"] = tiles(f("L0_attn_w_proj")), f("L0_attn_b_proj")[None]
    kr = np.zeros((P, 1), np.float32)
    kr[DH0::32] = 1
    a["krow"] = kr
    a["gate0_w"], a["gate0_b"] = tiles(f("L0_ffn_gate_w")), f("L0_ffn_gate_b")[None]
    a["gate1_w"], a["gate1_b"] = tiles(f("L1_ffn_router_w")), f("L1_ffn_router_b")[None]
    a["tri"] = np.triu(np.ones((P, P), np.float32), 1)
    a["rank8"] = np.tile(np.arange(E, 0, -1, dtype=np.float32), (P, 1))
    a["starts"] = (np.arange(N0, dtype=np.float32) * P)[None]
    w1 = np.zeros((KT + 1, 2, E, F0), np.float32)
    w1[0:KT] = f("L0_ffn_w1").reshape(E, 2, KT, F0).transpose(2, 1, 0, 3)
    w1[KT, 1] = f("L0_ffn_b1")
    a["e0w1"] = w1
    a["e0w2"] = f("L0_ffn_w2").reshape(E, F0 // P, P, C).transpose(2, 0, 1, 3)
    a["e0b2"] = f("L0_ffn_b2")[None]
    a["e1w1"] = f("L1_ffn_w1").reshape(E, 2, KT, F1).transpose(2, 1, 0, 3)
    a["e1w2"] = f("L1_ffn_w2").reshape(E, 2, KT, F1).transpose(2, 1, 0, 3)
    a["e1w3"] = f("L1_ffn_w3").reshape(E, F1 // P, P, C).transpose(2, 0, 1, 3)
    wa = np.zeros((P, 3, PW), np.float32)
    wb = np.zeros((KB, 3, PW), np.float32)
    ma = np.zeros((P, 3, MOD), np.float32)
    mb = np.zeros((P, 3, MOD), np.float32)
    for m, n in enumerate("kvq"):
        w, m1 = f(f"L1_attn_W{n}").T, f(f"L1_attn_{n}m_w1").T
        wa[:, m], wb[0:64, m] = w[0:P], w[P:]
        wb[64:64 + MOD, m], wb[64 + MOD, m] = f(f"L1_attn_{n}m_w2").T, f(f"L1_attn_{n}m_b2")
        ma[:, m], mb[0:64, m] = m1[0:P], m1[P:]
    a["wa"], a["wb"], a["ma"], a["mb"] = wa, wb, ma, mb
    a["mbias"] = np.stack([f(f"L1_attn_{n}m_b1") for n in "kvq"], 1)
    a["lin"] = np.stack([f("L1_attn_ln_in_g"), f("L1_attn_ln_in_b")])[None]
    a["gb"] = np.stack([np.stack([f(f"L1_attn_ln{n}_g"), f(f"L1_attn_ln{n}_b")]) for n in "kvq"])[None]
    a["lr_scale"] = f("L1_attn_lr_scale")[None]
    a["up"] = np.triu(np.ones((P, P), np.float32), 1)
    t, s = np.arange(P)[:, None], np.arange(P)[None, :]
    corner = np.zeros((P, LEVELS, P), np.int32)
    for lv in range(LEVELS):
        corner[:, lv] = (t >> (lv + 1) == s >> (lv + 1)) & ((t >> lv) & 1 == 1) & ((s >> lv) & 1 == 0)
    a["corner"] = corner
    a["up0"] = corner[:, 0].T.astype(np.float32)
    a["woT"] = f("L1_attn_Wo").T.reshape(H // 2, P, C).transpose(1, 0, 2)
    wg = np.zeros((KT + 1, 2, C), np.float32)
    wg[0:KT] = tiles(f("L1_attn_Wg").T)
    wg[KT, 1] = f("L1_attn_bg")
    a["wg"] = wg
    return {n: np.ascontiguousarray(v) for n, v in a.items()}


STOP = 99


def kernel(**inputs):
    import concourse.bacc as bacc
    from concourse.bass_utils import run_bass_kernel_spmd

    arrays = hostprep(inputs)
    nc = bacc.Bacc("TRN2", target_bir_lowering=False, num_devices=1)
    d = {n: nc.dram_tensor("in_" + n, v.shape, mybir.dt.from_np(v.dtype), kind="ExternalInput").ap()
         for n, v in arrays.items()}
    d["out"] = nc.dram_tensor("out", (B, NTOK, C), F32, kind="ExternalOutput").ap()
    build(nc, d, STOP)
    r = run_bass_kernel_spmd(nc, [{"in_" + n: v for n, v in arrays.items()}], core_ids=[0])
    return r.results[0]["out"]
```

```python
from contextlib import ExitStack

import numpy as np
import concourse.bass as bass
from concourse import mybir

F32 = mybir.dt.float32
BF16 = mybir.dt.bfloat16
I32 = mybir.dt.int32
ACT = mybir.ActivationFunctionType
ALU = mybir.AluOpType
AX = mybir.AxisListType

P = 128
B = 8
C = 192
KT = 96
NT = 3
G = B * NT
NTOK = NT * P
EPS = 1e-5
E = 8
NH0, DH0 = 8, 24
SCALE = DH0 ** -0.5
F0, F1 = 768, 512
N0 = 56
N1 = 32
H, HD = 12, 64
PW = H * HD
MOD = 48
KB = 64 + MOD + 1
NG = 3
BLK = 16
NBLK = P // BLK
UNITS = NBLK * H
LEVELS = 3
SUB = 2 * BLK - 1


def ds(start, size):
    return bass.ds(start, size)


def after(n):
    return n + 1


class Core:

    def __init__(self, nc, ctx, d):
        self.nc, self.ctx, self.d = nc, ctx, d
        self.fresh, self.used = [], []
        self.h = self.sb("h", [P, G, C])
        self.ident = self.sb("ident", [P, P])
        self.ones = self.sb("ones", [P, P])
        self.stats = self.sb("stats", [P, G, 6])
        self.tmp24 = self.sb("tmp24", [P, 4, G])
        self.mean = self.sb("mean", [P, G])
        self.rstd = self.sb("rstd", [P, G])
        self.vare = self.sb("vare", [P, G])
        self.half2 = self.sb("half2", [P, G])
        self.half = self.sb("half", [P, 2 * G])
        self.wtop = self.sb("wtop", [P, 2, G])
        self.pos = self.sb("pos", [P, 2, G], I32)
        self.eid = self.sb("eid", [1, N0], I32)
        self.xs = nc.dram_tensor("xs", (N0 * P, C), F32, kind="Internal").ap()
        self.ys = nc.dram_tensor("ys", (N0 * P, C), F32, kind="Internal").ap()
        self.ys1 = nc.dram_tensor("ys1", (N1 * P, C), BF16, kind="Internal").ap()
        self.s_consts = self.sem("s_consts")

    def sb(self, name, shape, dt=F32, ctx=None):
        return (ctx or self.ctx).enter_context(self.nc.sbuf_tensor(name, shape, dt))

    def ps(self, name, shape, ctx, dt=F32):
        return ctx.enter_context(self.nc.psum_tensor(name, shape, dt))

    def sem(self, name):
        self.fresh.append(self.plain_sem(name))
        return self.fresh[-1]

    def plain_sem(self, name):
        self.used.append(self.nc.alloc_semaphore(name))
        return self.used[-1]

    def recycle(self):
        self.nc.clear_and_free_semaphores(self.used)
        self.nc.all_engine_barrier()
        self.used = []

    def start_at_one(self, eng):
        for s in self.fresh:
            eng.sem_inc(s, 1)
        self.fresh = []


def linker(eng, sem, base=0):
    n = [0]

    def link(ins):
        n[0] += 1
        ins.then_inc(sem, 1)
        eng.wait_ge(sem, after(base + n[0]))
    return link


def root_step(k, pool, s_var, s_root):
    pool.wait_ge(s_var, after(1))
    k.nc.gpsimd.tensor_tensor(k.rstd[:], k.vare[:], k.half[:, 0:G], ALU.pow).then_inc(s_root, 1)


def finish_stats(k, link):
    v = k.nc.vector
    me, mo = k.stats[:, :, 1], k.stats[:, :, 4]
    ve, vo = k.stats[:, :, 2], k.stats[:, :, 5]
    a, b, c = k.tmp24[:, 0, :], k.tmp24[:, 1, :], k.tmp24[:, 2, :]
    link(v.tensor_tensor(a, me, mo, ALU.add))
    link(v.tensor_scalar(k.mean[:, :], a, 0.5, None, ALU.mult))
    link(v.tensor_tensor(b, me, mo, ALU.subtract))
    link(v.tensor_tensor(a, b, b, ALU.mult))
    link(v.tensor_tensor(c, ve, vo, ALU.add))
    link(v.tensor_scalar(b, c, 1.0 / C, None, ALU.mult))
    link(v.scalar_tensor_tensor(out=c, in0=a, scalar=0.25, in1=b, op0=ALU.mult, op1=ALU.add))
    return v.tensor_scalar(k.vare[:], c, EPS, None, ALU.add)


def stats_of_h(k, dve, s_st, s_link, s_var, s_root):
    with dve.Fori(0, G) as g:
        k.nc.vector.bn_stats(k.stats[:, ds(g, 1), :].rearrange("p a b -> p (a b)"),
                             k.h[:, ds(g, 1), :].rearrange("p a b -> p (a b)")).then_inc(s_st, 1)
    dve.wait_ge(s_st, after(G))
    finish_stats(k, linker(dve, s_link)).then_inc(s_var, 1)
    dve.wait_ge(s_root, after(1))


def tile_of(t, g):
    return t[:, g, :] if type(g) is int else t[:, ds(g, 1), :].rearrange("p a b -> p (a b)")


def column_of(t, g):
    return t[:, g:g + 1] if type(g) is int else t[:, ds(g, 1)]


def tokenizer(k):
    nc, d = k.nc, k.d
    with ExitStack() as ctx:
        sb = lambda n, s, dt=F32: k.sb(n, s, dt, ctx)
        ix0 = sb("ix0", [P, 2, 16], I32)
        ix1 = sb("ix1", [64, 16], I32)
        ix2 = sb("ix2", [16, 16], I32)
        g0 = sb("g0", [P, 2, 16, 3 * B])
        g1 = sb("g1", [64, 16, 12 * B])
        g2 = sb("g2", [16, 16, 48 * B])
        c0 = sb("c0", [P, 2, 64])
        c1 = sb("c1", [64, 16, 12])
        c2 = sb("c2", [16, 16, 48])
        t0T = sb("t0T", [P, P])
        t1T = sb("t1T", [KT, 2, 64])
        t2T = sb("t2T", [P, 6, 16])
        w0T = sb("w0T", [P, 64])
        w1T = sb("w1T", [KT, 2, 64])
        w2T = sb("w2T", [P, 6, 64])
        wfT = sb("wfT", [64, 3, C])
        lb = sb("lb", [64, 3])
        bf = sb("bf", [P, C])
        up1 = sb("up1", [64, 256])
        up2 = sb("up2", [16, 256])
        o1 = sb("o1", [64, 64])
        o2 = sb("o2", [16, 64])
        yT = sb("yT", [64, 3, 256])
        zero = sb("zero", [P, C])
        pT0 = k.ps("pT0", [P, 512], ctx)
        pT1 = k.ps("pT1", [P, 512], ctx)
        pY = k.ps("pY", [P, 2, 512], ctx)
        pO = k.ps("pO", [P, 512], ctx)
        pU = k.ps("pU", [P, 512], ctx)
        pH = k.ps("pH", [P, 512], ctx)
        s_ix, s_w, s_id, s_c0 = (k.sem("t_" + n) for n in ("ix", "w", "id", "c0"))
        s_g = k.plain_sem("t_g")
        s_cut, s_tr, s_trs, s_lv, s_lvs, s_up, s_y, s_h, s_hs, s_z = (
            k.sem("t_" + n) for n in ("cut", "tr", "trs", "lv", "lvs", "up", "y", "h", "hs", "z"))
        block = ctx.enter_context(nc.Block())

        @block.sync
        def _(sp):
            k.start_at_one(sp)
            sp.dma_start(ix0[:], d["idx0"].rearrange("(t p j) -> p t j", t=2, j=16)).then_inc(s_ix, 16)
            sp.dma_start(ix1[:], d["idx1"].rearrange("(p j) -> p j", j=16)).then_inc(s_ix, 16)
            sp.dma_start(ix2[:], d["idx2"].rearrange("(p j) -> p j", j=16)).then_inc(s_ix, 16)
            for t, name in ((w0T, "w0T"), (w1T, "w1T"), (w2T, "w2T"), (wfT, "wfT"), (lb, "lb"),
                            (up1, "up1"), (up2, "up2")):
                sp.dma_start(t[:], d[name]).then_inc(s_w, 16)
            sp.dma_start(bf[:], d["bf"].broadcast_to([P, C])).then_inc(s_w, 16)
            sp.dma_start(k.h[:, :, :].rearrange("p (b t) c -> p b t c", t=NT)[:, :, 2, :],
                         d["txt"].rearrange("b p c -> p b c")).then_inc(s_w, 16)
            sp.wait_ge(s_z, after(1))
            for n in range(0, N0, 8):
                sp.dma_start(k.xs[n * P:(n + 8) * P, :].rearrange("(n p) c -> p n c", p=P),
                             zero[:, :].rearrange("p (a c) -> p a c", a=1).broadcast_to([P, 8, C])).then_inc(k.s_consts, 16)
            sp.wait_ge(s_w, after(16 * 9))

        @block.gpsimd
        def _(pool):
            nc.gpsimd.memset(k.ident[:], 0.0).then_inc(s_id, 1)
            nc.gpsimd.memset(k.half[:], -0.5)
            nc.gpsimd.memset(k.half2[:], 0.5)
            nc.gpsimd.memset(k.ones[:], 1.0).then_inc(s_id, 1)
            pool.wait_ge(s_id, after(2))
            nc.gpsimd.affine_select(out=k.ident[:], in_=k.ident[:], compare_op=ALU.not_equal, fill=1.0, base=0,
                                    pattern=[[-1, P]], channel_multiplier=1).then_inc(s_id, 1)
            pool.wait_ge(s_ix, after(48))
            for j in range(16):
                for t in range(2):
                    nc.gpsimd.indirect_dma_start(g0[:, t, j, :], None, d["x0r"],
                                                 bass.IndirectOffsetOnAxis(ap=ix0[:, t, j:j + 1], axis=0)).then_inc(s_g, 16)
                nc.gpsimd.indirect_dma_start(g1[:, j, :], None, d["x1r"],
                                             bass.IndirectOffsetOnAxis(ap=ix1[:, j:j + 1], axis=0)).then_inc(s_g, 16)
                nc.gpsimd.indirect_dma_start(g2[:, j, :], None, d["x2r"],
                                             bass.IndirectOffsetOnAxis(ap=ix2[:, j:j + 1], axis=0)).then_inc(s_g, 16)

        @block.vector
        def _(dve):
            nc.vector.memset(zero[:], 0.0).then_inc(s_z, 1)
            nc.vector.memset(c0[:], 0.0).then_inc(s_c0, 1)
            dve.wait_ge(s_c0, after(1))
            dve.wait_ge(s_g, 64 * 16)
            dve.wait_ge(s_w, after(16 * 9))
            with dve.Fori(0, B) as b:
                dve.wait_ge(s_tr, after(b))
                nc.vector.tensor_copy(c0[:, :, 0:48].rearrange("p t (j c) -> p t j c", c=3),
                                      g0[:, :, :, ds(b * 3, 3)])
                nc.vector.tensor_copy(c1[:], g1[:, :, ds(b * 12, 12)])
                nc.vector.tensor_copy(c2[:], g2[:, :, ds(b * 48, 48)]).then_inc(s_cut, 1)
                dve.wait_ge(s_h, after(b + 1))
                for t in range(2):
                    nc.vector.tensor_tensor(tile_of(k.h, b * NT + t), pH[:, t * C:(t + 1) * C], bf[:],
                                            ALU.add).then_inc(s_hs, 1)

        @block.tensor
        def _(pe):
            pe.wait_ge(s_id, after(3))
            pe.wait_ge(s_w, after(16 * 9))
            with pe.Fori(0, B) as b:
                pe.wait_ge(s_cut, after(b + 1))
                pe.wait_ge(s_trs, after(3 * b))
                nc.tensor.transpose(pT0[:, 0:P], c0[:, :, :].rearrange("p t c -> p (t c)"), k.ident[:])
                for i in range(2):
                    nc.tensor.transpose(pT1[0:KT, i * 64:(i + 1) * 64],
                                        c1[:, i * 8:(i + 1) * 8, :].rearrange("p j c -> p (j c)"), k.ident[0:64, 0:64])
                flat2 = c2[:, :, :].rearrange("p j c -> p (j c)")
                for i in range(6):
                    last = nc.tensor.transpose(pT1[:, P + i * 16:P + (i + 1) * 16], flat2[:, i * P:(i + 1) * P],
                                               k.ident[0:16, 0:16])
                last.then_inc(s_tr, 1)
                pe.wait_ge(s_trs, after(3 * b + 3))
                pe.wait_ge(s_y, after(5 * b))
                pe.wait_ge(s_lvs, after(2 * b))
                for i in range(6):
                    nc.tensor.matmul(pO[0:16, 64:128], t2T[:, i, :], w2T[:, i, :], start=i == 0, stop=i == 5)
                for i in range(2):
                    nc.tensor.matmul(pO[0:64, 0:64], t1T[:, i, :], w1T[:, i, :], start=i == 0, stop=i == 1)
                for t in range(2):
                    last = nc.tensor.matmul(pY[0:64, t, 0:P], w0T[64 * t:64 * t + 48, :], t0T[64 * t:64 * t + 48, :],
                                            start=True, stop=True)
                last.then_inc(s_lv, 1)
                pe.wait_ge(s_lvs, after(2 * b + 2))
                nc.tensor.matmul(pU[0:64, 256:512], o2[:], up2[:], start=True, stop=True)
                nc.tensor.matmul(pU[0:64, 0:256], o1[:], up1[:], start=True, stop=True).then_inc(s_up, 1)
                pe.wait_ge(s_y, after(5 * b + 5))
                pe.wait_ge(s_hs, after(2 * b))
                for t in range(2):
                    for i in range(3):
                        last = nc.tensor.matmul(pH[:, t * C:(t + 1) * C], yT[:, i, t * P:(t + 1) * P], wfT[:, i, :],
                                                start=i == 0, stop=i == 2)
                last.then_inc(s_h, 1)

        @block.scalar
        def _(act):
            act.wait_ge(s_w, after(16 * 9))
            with act.Fori(0, B) as b:
                act.wait_ge(s_tr, after(b + 1))
                act.wait_ge(s_lv, after(b))
                nc.scalar.activation(t0T[:], pT0[:, 0:P], ACT.Copy).then_inc(s_trs, 1)
                nc.scalar.activation(t1T[:].rearrange("p i t -> p (i t)"), pT1[0:KT, 0:128], ACT.Copy).then_inc(s_trs, 1)
                nc.scalar.activation(t2T[:].rearrange("p i t -> p (i t)"), pT1[:, 128:224], ACT.Copy).then_inc(s_trs, 1)
                act.wait_ge(s_lv, after(b + 1))
                act.wait_ge(s_up, after(b))
                nc.scalar.activation(o1[:], pO[0:64, 0:64], ACT.Copy).then_inc(s_lvs, 1)
                nc.scalar.activation(o2[:], pO[0:16, 64:128], ACT.Copy).then_inc(s_lvs, 1)
                act.wait_ge(s_h, after(b))
                for t in range(2):
                    nc.scalar.activation(yT[:, 0, t * P:(t + 1) * P], pY[0:64, t, 0:P], ACT.Identity,
                                         bias=lb[:, 0:1]).then_inc(s_y, 1)
                act.wait_ge(s_up, after(b + 1))
                for i in (1, 2):
                    nc.scalar.activation(yT[:, i, :], pU[0:64, (i - 1) * 256:i * 256], ACT.Identity,
                                         bias=lb[:, i:i + 1]).then_inc(s_y, 1)
                act.wait_ge(s_y, after(5 * b + 4))
                act.sem_inc(s_y, 1)


def attention(k):
    nc, d = k.nc, k.d
    NU = NT * NH0
    with ExitStack() as ctx:
        sb = lambda n, s, dt=F32: k.sb(n, s, dt, ctx)
        wq = sb("wq", [KT, 2, 2, P])
        wk = sb("wk", [KT, 2, 2, P])
        wv = sb("wv", [KT, 2, C])
        wp = sb("wp", [P, 2, C])
        dsel = sb("dsel", [P, P])
        xn = sb("xn", [P, NT, C])
        xnT = sb("xnT", [KT, 2, NTOK])
        qT = sb("qT", [P, 2, NTOK])
        kz = sb("kz", [P, 2, 4, NTOK])
        va = sb("va", [P, NT, NH0, 32])
        mx = sb("mx", [P, NU])
        pm = sb("pm", [P, 2, 4, NTOK])
        pT = sb("pT", [P, NT, NH0, NTOK])
        oR = sb("oR", [P, 2, NTOK])
        rec = sb("rec", [P, 2, NTOK])
        oN = sb("oN", [P, 2, NTOK])
        S = k.ps("aS", [P, 4, 512], ctx)
        Gp = k.ps("aG", [P, 4, 512], ctx)
        names = ("w", "st", "lk", "var", "root", "pre", "xn", "xt", "xts", "q", "k", "v", "qs", "ks", "vs", "sc", "mx", "ex",
                 "pt", "pa", "pd", "pv", "or", "dn", "rc", "on", "pj", "hs")
        (s_w, s_st, s_lk, s_var, s_root, s_pre, s_xn, s_xt, s_xts, s_q, s_k, s_v, s_qs, s_ks, s_vs, s_sc, s_mx, s_ex,
         s_pt, s_pa, s_pd, s_pv, s_or, s_dn, s_rc, s_on, s_pj, s_hs) = (k.sem("a_" + n) for n in names)
        block = ctx.enter_context(nc.Block())

        def evacuator(n, kt):
            on_act = kt == 1 or (kt == 2 and n % 2)
            order = [(m, t) for m in range(6) for t in range(NT) if (t == 1 or (t == 2 and m % 2)) == on_act]
            return on_act, order.index((n, kt)), len(order)

        @block.sync
        def _(sp):
            k.start_at_one(sp)
            for t, n in ((wq, "wq"), (wk, "wk"), (wv, "wv"), (wp, "wp"), (dsel, "dsel")):
                sp.dma_start(t[:], d[n]).then_inc(s_w, 16)
            sp.wait_ge(s_w, after(80))

        @block.gpsimd
        def _(pool):
            nc.gpsimd.memset(kz[:], 0.0).then_inc(s_pre, 1)
            nc.gpsimd.memset(va[:], 1.0).then_inc(s_pre, 1)
            root_step(k, pool, s_var, s_root)
            pool.wait_ge(s_pre, after(2))

        @block.vector
        def _(dve):
            v = nc.vector
            stats_of_h(k, dve, s_st, s_lk, s_var, s_root)
            dve.wait_ge(s_pre, after(2))
            with dve.Fori(0, B) as b:
                dve.wait_ge(s_xt, after(b))
                for t in range(NT):
                    v.tensor_scalar(xn[:, t, :], tile_of(k.h, b * NT + t), column_of(k.mean, b * NT + t),
                                    column_of(k.rstd, b * NT + t), ALU.subtract, ALU.mult).then_inc(s_xn, 1)
                dve.wait_ge(s_xt, after(b + 1))
                v.tensor_copy(xnT[:, 1, :], Gp[0:KT, 1, 0:NTOK]).then_inc(s_xts, 1)
                dve.wait_ge(s_q, after(b + 1))
                for g in range(2):
                    v.tensor_scalar(qT[:, g, :], Gp[:, 2 + g, 0:NTOK], SCALE, None, ALU.mult).then_inc(s_qs, 1)
                dve.wait_ge(s_k, after(b + 1))
                for j in range(4):
                    v.tensor_copy(kz[32 * j:32 * j + 32, 1, j, :], Gp[32 * j:32 * j + 32, 1, 0:NTOK]).then_inc(s_ks, 1)
                dve.wait_ge(s_v, after(b + 1))
                v.tensor_copy(va[:, :, :, 0:DH0],
                              S[:, 0:NT, 0:C].rearrange("p t (h c) -> p t h c", c=DH0)).then_inc(s_vs, 1)

                def maxima(n):
                    for j in range(4):
                        u = 4 * n + j
                        dve.wait_ge(s_sc, after(b * NU + u + 1))
                        v.tensor_reduce(mx[:, u:u + 1], S[:, j, 0:NTOK], AX.X, ALU.max, negate=True).then_inc(s_mx, 1)

                def keys(n):
                    for kt in range(NT):
                        if not evacuator(n, kt)[0]:
                            dve.wait_ge(s_pt, after(b * 18 + n * NT + kt + 1))
                            v.tensor_copy(pT[:, kt, 4 * (n % 2):4 * (n % 2) + 4, (n // 2) * P:(n // 2 + 1) * P],
                                          Gp[:, kt, :].rearrange("p (h t) -> p h t", t=P)).then_inc(s_pd, 1)
                maxima(0)
                for n in range(1, 6):
                    maxima(n)
                    keys(n - 1)
                keys(5)
                for g in range(2):
                    dve.wait_ge(s_dn, after(b * 2 + g + 1))
                    v.reciprocal(rec[:, g, :], Gp[:, g, 0:NTOK]).then_inc(s_rc, 1)
                for g in range(2):
                    dve.wait_ge(s_rc, after(b * 2 + g + 1))
                    v.tensor_tensor(oN[:, g, :], oR[:, g, :], rec[:, g, :], ALU.mult).then_inc(s_on, 1)
                for t in range(NT):
                    dve.wait_ge(s_pj, after(b * NT + t + 1))
                    v.tensor_tensor(tile_of(k.h, b * NT + t), tile_of(k.h, b * NT + t), S[:, t, 0:C],
                                    ALU.add).then_inc(s_hs, 1)

        @block.tensor
        def _(pe):
            mm = nc.tensor.matmul
            pe.wait_ge(s_w, after(80))
            with pe.Fori(0, B) as b:
                pe.wait_ge(s_xn, after(NT * b + NT))
                pe.wait_ge(s_rc, after(2 * b))
                for i in range(2):
                    for t in range(NT):
                        last = nc.tensor.transpose(Gp[0:KT, i, t * P:(t + 1) * P], xn[:, t, i * KT:(i + 1) * KT], k.ident[:])
                last.then_inc(s_xt, 1)
                pe.wait_ge(s_xts, after(2 * b + 2))
                pe.wait_ge(s_or, after(2 * b))
                for g in range(2):
                    for i in range(2):
                        last = mm(Gp[:, 2 + g, 0:NTOK], wq[:, i, g, :], xnT[:, i, :], start=i == 0, stop=i == 1)
                last.then_inc(s_q, 1)
                for g in range(2):
                    for i in range(2):
                        last = mm(Gp[:, g, 0:NTOK], wk[:, i, g, :], xnT[:, i, :], start=i == 0, stop=i == 1)
                last.then_inc(s_k, 1)
                pe.wait_ge(s_hs, after(NT * b))
                for t in range(NT):
                    for i in range(2):
                        last = mm(S[:, t, 0:C], xnT[:, i, t * P:(t + 1) * P], wv[:, i, :], start=i == 0, stop=i == 1)
                last.then_inc(s_v, 1)
                pe.wait_ge(s_qs, after(2 * b + 2))
                pe.wait_ge(s_ks, after(8 * b + 8))
                pe.wait_ge(s_vs, after(b + 1))

                def scores(n):
                    for j in range(4):
                        u = 4 * n + j
                        if n:
                            pe.wait_ge(s_ex, after(b * NU + u - 3))
                        mm(S[:, j, 0:NTOK], qT[:, n % 2, (n // 2) * P:(n // 2 + 1) * P], kz[:, n % 2, j, :],
                           start=True, stop=True).then_inc(s_sc, 1)

                def turn(n):
                    pe.wait_ge(s_ex, after(b * NU + 4 * n + 4))
                    for kt in range(NT):
                        if n:
                            on_act, at, of = evacuator(n - 1, kt)
                            pe.wait_ge(s_pa if on_act else s_pd, after(b * of + at + 1))
                        for j in range(4):
                            last = nc.tensor.transpose(Gp[:, kt, j * P:(j + 1) * P], pm[:, n % 2, j, kt * P:(kt + 1) * P], k.ident[:])
                        last.then_inc(s_pt, 1)
                scores(0)
                for n in range(1, 6):
                    scores(n)
                    turn(n - 1)
                turn(5)
                pe.wait_ge(s_pa, after(b * 9 + 9))
                pe.wait_ge(s_pd, after(b * 9 + 9))
                for g in range(2):
                    for j in range(4):
                        for kt in range(NT):
                            last = mm(Gp[32 * j:32 * j + 32, 2 + g, 0:NTOK], va[:, kt, 4 * g + j, :], pT[:, kt, 4 * g + j, :],
                                      start=kt == 0, stop=kt == NT - 1)
                    last.then_inc(s_pv, 1)
                for g in range(2):
                    pe.wait_ge(s_or, after(2 * b + g + 1))
                    mm(Gp[:, g, 0:NTOK], dsel[:], oR[:, g, :], start=True, stop=True).then_inc(s_dn, 1)
                pe.wait_ge(s_on, after(2 * b + 2))
                for t in range(NT):
                    for g in range(2):
                        last = mm(S[:, t, 0:C], oN[:, g, t * P:(t + 1) * P], wp[:, g, :], start=g == 0, stop=g == 1)
                    last.then_inc(s_pj, 1)

        @block.scalar
        def _(act):
            A = nc.scalar.activation
            act.preload_act_table(ACT.Exp)
            act.wait_ge(s_pre, after(2))
            with act.Fori(0, B) as b:
                act.wait_ge(s_xt, after(b + 1))
                A(xnT[:, 0, :], Gp[0:KT, 0, 0:NTOK], ACT.Copy).then_inc(s_xts, 1)
                act.wait_ge(s_k, after(b + 1))
                for j in range(4):
                    A(kz[32 * j:32 * j + 32, 0, j, :], Gp[32 * j:32 * j + 32, 0, 0:NTOK], ACT.Copy).then_inc(s_ks, 1)

                def exps(n):
                    if n >= 2:
                        act.wait_ge(s_pt, after(b * 18 + (n - 2) * NT + NT))
                    for j in range(4):
                        u = 4 * n + j
                        act.wait_ge(s_mx, after(b * NU + u + 1))
                        A(pm[:, n % 2, j, :], S[:, j, 0:NTOK], ACT.Exp, bias=mx[:, u:u + 1]).then_inc(s_ex, 1)

                def keys(n):
                    for kt in range(NT):
                        if evacuator(n, kt)[0]:
                            act.wait_ge(s_pt, after(b * 18 + n * NT + kt + 1))
                            A(pT[:, kt, 4 * (n % 2):4 * (n % 2) + 4, (n // 2) * P:(n // 2 + 1) * P],
                              Gp[:, kt, :].rearrange("p (h t) -> p h t", t=P), ACT.Copy).then_inc(s_pa, 1)
                exps(0)
                for n in range(1, 6):
                    exps(n)
                    keys(n - 1)
                keys(5)
                for g in range(2):
                    act.wait_ge(s_pv, after(b * 2 + g + 1))
                    A(oR[:, g, :], Gp[:, 2 + g, 0:NTOK], ACT.Copy).then_inc(s_or, 1)


def route(k, tag, top, ntiles, gw, gb):
    nc, d = k.nc, k.d
    NC = top
    with ExitStack() as ctx:
        sb = lambda n, s, dt=F32: k.sb(tag + n, s, dt, ctx)
        w = sb("w", [KT, 2, E])
        bias = sb("bias", [1, E])
        tri = sb("tri", [P, P])
        rank8 = sb("rank8", [P, E])
        seg = sb("seg", [P, E, NC * G])
        starts = sb("starts", [1, ntiles])
        xb = sb("xb", [P, 4, C])
        xT = sb("xT", [KT, 2, 4 * P])
        lg = sb("lg", [P, G, E])
        pr = sb("pr", [P, G, E])
        key = sb("key", [P, G, E])
        oh = sb("oh", [P, E, NC, G])
        m1 = sb("m1", [P, 3, G])
        tot = sb("tot", [P, E, NC, G])
        inc = sb("inc", [P, E, NC, G])
        ne = sb("ne", [P, 3, E])
        nei = sb("nei", [P, E], I32)
        ends = sb("ends", [P, E])
        posf = sb("posf", [P, NC, G])
        cmp = sb("cmp", [1, ntiles, E])
        eidf = sb("eidf", [1, ntiles])
        xo = sb("xo", [P, 2, C])
        ib = sb("ib", [P, 2, NC], I32)
        pX = k.ps(tag + "pX", [P, 2, 512], ctx)
        pL = k.ps(tag + "pL", [P, 512], ctx)
        pC = k.ps(tag + "pC", [P, 512], ctx)
        pS = k.ps(tag + "pS", [P, 512], ctx)
        s_w, s_c, s_st, s_lk, s_xb, s_xt, s_xts, s_l, s_ls, s_d, s_oh, s_cnt, s_pos, s_xo = (
            k.sem(tag + n) for n in ("w", "c", "st", "lk", "xb", "xt", "xts", "l", "ls", "d", "oh", "cnt", "pos", "xo"))
        s_ib = k.plain_sem(tag + "ib")
        s_sc = [k.plain_sem(tag + f"sc{i}") for i in range(2)]
        s_var, s_root = k.sem(tag + "var"), k.sem(tag + "root")
        block = ctx.enter_context(nc.Block())

        def per_tile(t):
            return t.rearrange("p (g a) -> p g a", a=1).broadcast_to([P, G, E])

        @block.sync
        def _(sp):
            k.start_at_one(sp)
            for t, n in ((w, gw), (tri, "tri"), (rank8, "rank8")):
                sp.dma_start(t[:], d[n]).then_inc(s_w, 16)
            sp.dma_start(bias[:], d[gb]).then_inc(s_w, 16)
            sp.dma_start(starts[:], d["starts"][:, 0:ntiles]).then_inc(s_w, 16)
            sp.wait_ge(s_w, after(80))

        @block.gpsimd
        def _(pool):
            nc.gpsimd.memset(seg[:], 1.0).then_inc(s_c, 1)
            pool.wait_ge(s_c, after(1))
            nc.gpsimd.memset(seg[:, :, 0:1], 0.0).then_inc(s_c, 1)
            root_step(k, pool, s_var, s_root)
            pool.wait_ge(s_pos, after(1))
            if top == 2:
                pool.wait_ge(k.s_consts, after(16 * (N0 // 8)))
            def scatter(g, i, s):
                pool.sem_clear(s_ib)
                if type(g) is not int:
                    pool.wait_ge(s_sc[s], i * (16 * NC))
                pool.wait_ge(s_xo, after(g + 1))
                for c in range(NC):
                    nc.gpsimd.tensor_copy(ib[:, s, c:c + 1], k.pos[:, c, ds(g, 1)]).then_inc(s_ib, 1)
                pool.wait_ge(s_ib, NC)
                for c in range(NC):
                    nc.gpsimd.indirect_dma_start(k.xs, bass.IndirectOffsetOnAxis(ap=ib[:, s, c:c + 1], axis=0),
                                                 xo[:, s, :], None).then_inc(s_sc[s], 16)

            paired(pool, G, scatter)
            for s in range(2):
                pool.wait_ge(s_sc[s], 16 * NC * G // 2)

        @block.vector
        def _(dve):
            v = nc.vector
            stats_of_h(k, dve, s_st, s_lk, s_var, s_root)
            dve.wait_ge(s_w, after(80))
            dve.wait_ge(s_c, after(2))
            with dve.Fori(0, G // 4) as i:
                dve.wait_ge(s_xt, after(i))
                for t in range(4):
                    g = i * 4 + t
                    v.tensor_scalar(xb[:, t, :], tile_of(k.h, g), column_of(k.mean, g), column_of(k.rstd, g),
                                    ALU.subtract, ALU.mult).then_inc(s_xb, 1)
                dve.wait_ge(s_l, after(i + 1))
                v.tensor_copy(lg[:, ds(i * 4, 4), :], pL[:, 0:4 * E].rearrange("p (t e) -> p t e", e=E)).then_inc(s_ls, 1)
            dve.wait_ge(s_ls, after(G // 4))
            link = linker(dve, s_d)
            link(v.tensor_reduce(m1[:, 0, :], lg[:], AX.X, ALU.max))
            link(v.tensor_tensor(pr[:], lg[:], per_tile(m1[:, 0, :]), ALU.subtract))
            dve.sem_inc(s_oh, 1)
            dve.wait_ge(s_cnt, after(1))
            link(v.tensor_reduce(m1[:, 1, :], pr[:], AX.X, ALU.add))
            link(v.reciprocal(m1[:, 2, :], m1[:, 1, :]))
            link(v.tensor_tensor(pr[:], pr[:], per_tile(m1[:, 2, :]), ALU.mult))
            rank_b = rank8[:, :].rearrange("p (a e) -> p a e", a=1).broadcast_to([P, G, E])
            for c in range(NC):
                link(v.tensor_reduce(k.wtop[:, c, :], pr[:], AX.X, ALU.max))
                link(v.tensor_tensor(key[:], pr[:], per_tile(k.wtop[:, c, :]), ALU.is_equal))
                link(v.tensor_tensor(key[:], key[:], rank_b, ALU.mult))
                link(v.tensor_reduce(m1[:, 0, :], key[:], AX.X, ALU.max))
                ohc = oh[:, :, c, :].rearrange("p e g -> p g e")
                link(v.tensor_tensor(ohc, key[:], per_tile(m1[:, 0, :]), ALU.is_equal))
                if c + 1 < NC:
                    link(v.tensor_tensor(pr[:], pr[:], ohc, ALU.subtract))
            if NC == 2:
                link(v.tensor_tensor(m1[:, 0, :], k.wtop[:, 0, :], k.wtop[:, 1, :], ALU.add))
                link(v.reciprocal(m1[:, 1, :], m1[:, 0, :]))
                for c in range(2):
                    link(v.tensor_tensor(k.wtop[:, c, :], k.wtop[:, c, :], m1[:, 1, :], ALU.mult))
            dve.sem_inc(s_oh, 1)
            dve.wait_ge(s_cnt, after(2))
            n = E * NC * G
            flat = lambda t: t[:].rearrange("p e c g -> p (e c g)")
            link(v.tensor_copy(flat(tot), pS[:, 0:n]))
            link(v.tensor_tensor_scan(flat(inc), seg[:].rearrange("p e n -> p (e n)"), flat(tot), 0.0, ALU.mult, ALU.add))
            last = inc[:, :, NC - 1, G - 1]
            link(v.tensor_scalar(ne[:, 0, :], last, float(P - 1), None, ALU.add))
            link(v.tensor_copy(nei[:], ne[:, 0, :]))
            link(v.tensor_scalar(nei[:], nei[:], -P, None, ALU.bitwise_and))
            link(v.tensor_copy(ne[:, 2, :], nei[:]))
            link(v.tensor_tensor_scan(ends[:], k.ones[:, 0:E], ne[:, 2, :], 0.0, ALU.mult, ALU.add))
            link(v.tensor_tensor(ne[:, 0, :], ends[:], ne[:, 2, :], ALU.subtract))
            link(v.tensor_tensor(flat(inc), flat(inc), flat(tot), ALU.subtract))
            link(v.tensor_tensor(flat(inc), flat(inc), pC[:, 0:n], ALU.add))
            link(v.tensor_tensor(inc[:].rearrange("p e c g -> p e (c g)"), inc[:].rearrange("p e c g -> p e (c g)"),
                                 ne[:, 0, :].rearrange("p (e a) -> p e a", a=1).broadcast_to([P, E, NC * G]), ALU.add))
            link(v.tensor_tensor(flat(inc), flat(inc), flat(oh), ALU.mult))
            link(v.tensor_reduce(posf[:].rearrange("p c g -> p (c g)"), inc[:].rearrange("p e c g -> p (c g) e"),
                                 AX.X, ALU.add))
            link(v.tensor_copy(k.pos[:, 0:NC, :], posf[:]))
            dve.sem_inc(s_pos, 1)
            link(v.tensor_tensor(cmp[:], ends[0:1, :].rearrange("p (a e) -> p a e", a=1).broadcast_to([1, ntiles, E]),
                                 starts[:, :].rearrange("p (n a) -> p n a", a=1).broadcast_to([1, ntiles, E]), ALU.is_le))
            link(v.tensor_reduce(eidf[:], cmp[:], AX.X, ALU.add))
            link(v.tensor_scalar(eidf[:], eidf[:], float(E - 1), None, ALU.min))
            link(v.tensor_copy(k.eid[:, 0:ntiles], eidf[:]))

            def rows(g, i, s):
                if type(g) is not int:
                    dve.wait_ge(s_sc[s], i * (16 * NC))
                v.tensor_scalar(xo[:, s, :], tile_of(k.h, g), column_of(k.mean, g), column_of(k.rstd, g),
                                ALU.subtract, ALU.mult).then_inc(s_xo, 1)

            paired(dve, G, rows)

        @block.tensor
        def _(pe):
            pe.wait_ge(s_w, after(80))
            with pe.Fori(0, G // 4) as i:
                pe.wait_ge(s_xb, after(i * 4 + 4))
                pe.wait_ge(s_xts, after(i * 2))
                for t in range(4):
                    for c in range(2):
                        last = nc.tensor.transpose(pX[0:KT, c, t * P:(t + 1) * P], xb[:, t, c * KT:(c + 1) * KT], k.ident[:])
                last.then_inc(s_xt, 1)
                pe.wait_ge(s_xts, after(i * 2 + 2))
                pe.wait_ge(s_ls, after(i))
                for t in range(4):
                    for c in range(2):
                        nc.tensor.matmul(pL[:, t * E:(t + 1) * E], xT[:, c, t * P:(t + 1) * P], w[:, c, :], start=c == 0, stop=False)
                    last = nc.tensor.matmul(pL[:, t * E:(t + 1) * E], k.ones[0:1, :], bias[:], start=False, stop=True)
                last.then_inc(s_l, 1)
            pe.wait_ge(s_oh, after(2))
            n = E * NC * G
            oh_flat = oh[:].rearrange("p e c g -> p (e c g)")
            nc.tensor.matmul(pC[:, 0:n], tri[:], oh_flat, start=True, stop=True)
            nc.tensor.matmul(pS[:, 0:n], k.ones[:], oh_flat, start=True, stop=True).then_inc(s_cnt, 1)

        @block.scalar
        def _(act):
            with act.Fori(0, G // 4) as i:
                act.wait_ge(s_xt, after(i + 1))
                act.wait_ge(s_l, after(i))
                for c in range(2):
                    nc.scalar.activation(xT[:, c, :], pX[0:KT, c, :], ACT.Copy).then_inc(s_xts, 1)
            act.wait_ge(s_oh, after(1))
            nc.scalar.activation(pr[:].rearrange("p g e -> p (g e)"), pr[:].rearrange("p g e -> p (g e)"),
                                 ACT.Exp).then_inc(s_cnt, 1)


def paired(eng, tiles, step):
    for s in range(2):
        step(s, 0, s)
    with eng.Fori(1, tiles // 2) as i:
        for s in range(2):
            step(i * 2 + s, i, s)


def pipelined(eng, tiles, front, back):
    front(0, 0, 0)
    with eng.Fori(0, tiles // 2 - 1) as i:
        front(i * 2 + 1, i, 1)
        back(i * 2, i, 0)
        front(i * 2 + 2, i + 1, 0)
        back(i * 2 + 1, i, 1)
    front(tiles - 1, tiles // 2 - 1, 1)
    back(tiles - 2, tiles // 2 - 1, 0)
    back(tiles - 1, tiles // 2 - 1, 1)


def move_rows(sp, x, src, s_x, s_used, y, dst, s_st, s_ready, tiles):
    def load(n, s):
        sp.dma_start(x[:, s, :], src[ds(n * P, P), :] if type(n) is not int else src[n * P:(n + 1) * P, :]).then_inc(s_x[s], 16)

    def store(n, s):
        sp.wait_ge(s_ready, after(n + 1))
        sp.dma_start(dst[ds(n * P, P), :] if type(n) is not int else dst[n * P:(n + 1) * P, :], y[:, s, :]).then_inc(s_st[s], 16)

    load(0, 0)
    load(1, 1)
    with sp.Fori(0, tiles // 2 - 1) as i:
        for s in range(2):
            sp.wait_ge(s_used, after(i * 2 + s + 1))
            load(i * 2 + s + 2, s)
            store(i * 2 + s, s)
    for s in range(2):
        store(tiles - 2 + s, s)
    for s in range(2):
        sp.wait_ge(s_st[s], after(16 * tiles // 2))


def experts0(k):
    nc, d = k.nc, k.d
    NM = F0 // P
    HF = F0 // 2
    with ExitStack() as ctx:
        sb = lambda n, s, dt=F32: k.sb(n, s, dt, ctx)
        w1 = sb("e_w1", [KT + 1, 2, E, F0])
        w2 = sb("e_w2", [P, E, NM, C])
        b2 = sb("e_b2", [1, E, C])
        x = sb("e_x", [P, 2, C])
        xT = sb("e_xT", [KT + 1, 2, 2, P])
        hb = sb("e_h", [P, 2, 2, HF])
        hT = sb("e_hT", [P, 2, NM, P])
        y = sb("e_y", [P, 2, C])
        pX = k.ps("e_pX", [P, 512], ctx)
        pH = k.ps("e_pH", [P, 2, 2, 512], ctx)
        pT = k.ps("e_pT", [P, 2, 512], ctx)
        pY = k.ps("e_pY", [P, 512], ctx)
        s_w, s_on, s_xt, s_xts, s_h, s_hs, s_ht, s_hts, s_y, s_ys = (
            k.sem("e_" + n) for n in ("w", "on", "xt", "xts", "h", "hs", "ht", "hts", "y", "ys"))
        s_x = [k.sem(f"e_x{i}") for i in range(2)]
        s_st = [k.sem(f"e_st{i}") for i in range(2)]
        block = ctx.enter_context(nc.Block())

        @block.sync
        def _(sp):
            k.start_at_one(sp)
            for e in range(E):
                sp.dma_start(w1[:, :, e, :], d["e0w1"][:, :, e, :]).then_inc(s_w, 16)
                sp.dma_start(w2[:, e, :, :], d["e0w2"][:, e, :, :]).then_inc(s_w, 16)
            sp.dma_start(b2[:], d["e0b2"]).then_inc(s_w, 16)
            move_rows(sp, x, k.xs, s_x, s_xt, y, k.ys, s_st, s_ys, N0)

        @block.tensor
        def _(pe):
            pe.wait_ge(s_w, after(16 * (2 * E + 1)))
            pe.wait_ge(s_on, after(1))

            def front(n, i, s):
                e = pe.value_load(k.eid[0:1, ds(n, 1)], min_val=0, max_val=E - 1)
                pe.wait_ge(s_x[s], after(i * 16 + 16))
                pe.wait_ge(s_xts, after(n))
                for c in range(2):
                    last = nc.tensor.transpose(pX[0:KT, c * P:(c + 1) * P], x[:, s, c * KT:(c + 1) * KT], k.ident[:])
                last.then_inc(s_xt, 1)
                pe.wait_ge(s_xts, after(n + 1))
                if type(n) is not int or n > 1:
                    pe.wait_ge(s_hs, after(n - 1))
                for c in range(2):
                    for f in range(2):
                        last = nc.tensor.matmul(pH[:, s, f, 0:HF], xT[0:KT + c, s, c, :],
                                                w1[0:KT + c, c, ds(e, 1), f * HF:(f + 1) * HF].rearrange("p a f -> p (a f)"),
                                                start=c == 0, stop=c == 1)
                last.then_inc(s_h, 1)

            def back(n, i, s):
                e = pe.value_load(k.eid[0:1, ds(n, 1)], min_val=0, max_val=E - 1)
                pe.wait_ge(s_hs, after(n + 1))
                pe.wait_ge(s_hts, after(n))
                for m in range(NM):
                    last = nc.tensor.transpose(pT[:, m // 3, (m % 3) * P:(m % 3 + 1) * P],
                                               hb[:, s, m // 3, (m % 3) * P:(m % 3 + 1) * P], k.ident[:])
                last.then_inc(s_ht, 1)
                pe.wait_ge(s_hts, after(n + 1))
                pe.wait_ge(s_ys, after(n))
                for m in range(NM):
                    nc.tensor.matmul(pY[:, 0:C], hT[:, s, m, :], w2[:, ds(e, 1), m, :].rearrange("p a c -> p (a c)"),
                                     start=m == 0, stop=False)
                nc.tensor.matmul(pY[:, 0:C], k.ones[0:1, :], b2[:, ds(e, 1), :].rearrange("p a c -> p (a c)"),
                                 start=False, stop=True).then_inc(s_y, 1)

            pipelined(pe, N0, front, back)

        @block.scalar
        def _(act):
            act.preload_act_table(ACT.Gelu)

            def front(n, i, s):
                act.wait_ge(s_h, after(n + 1))
                if type(n) is not int or n > 1:
                    act.wait_ge(s_ht, after(n - 1))
                nc.scalar.activation(hb[:, s, :, :], pH[:, s, :, 0:HF], ACT.Gelu).then_inc(s_hs, 1)

            def back(n, i, s):
                act.wait_ge(s_st[s], after(i * 16))
                act.wait_ge(s_y, after(n + 1))
                nc.scalar.activation(y[:, s, :], pY[:, 0:C], ACT.Copy).then_inc(s_ys, 1)

            pipelined(act, N0, front, back)

        @block.vector
        def _(dve):
            nc.vector.memset(xT[KT:KT + 1, :, :, :], 1.0).then_inc(s_on, 1)

            def front(n, i, s):
                dve.wait_ge(s_xt, after(n + 1))
                nc.vector.tensor_copy(xT[0:KT, s, :, :],
                                      pX[0:KT, 0:2 * P].rearrange("p (c t) -> p c t", c=2)).then_inc(s_xts, 1)

            def back(n, i, s):
                dve.wait_ge(s_ht, after(n + 1))
                nc.vector.tensor_copy(hT[:, s, :, :].rearrange("p (a m) t -> p a (m t)", a=2),
                                      pT[:, :, 0:3 * P]).then_inc(s_hts, 1)

            pipelined(dve, N0, front, back)


def combine0(k):
    nc = k.nc
    with ExitStack() as ctx:
        ya = k.sb("cb_y", [P, 2, 2, C], F32, ctx)
        ib = k.sb("cb_i", [P, 2, 2], I32, ctx)
        s_a, s_h = k.sem("cb_a"), k.sem("cb_h")
        s_ib = k.plain_sem("cb_ib")
        s_g = [k.plain_sem(f"cb_g{i}") for i in range(2)]
        block = ctx.enter_context(nc.Block())

        @block.sync
        def _(sp):
            k.start_at_one(sp)

        @block.gpsimd
        def _(pool):
            def gather(g, i, s):
                pool.sem_clear(s_ib)
                if type(g) is not int:
                    pool.wait_ge(s_g[s], i * 32)
                pool.wait_ge(s_h, after(i * 2))
                for c in range(2):
                    nc.gpsimd.tensor_copy(ib[:, s, c:c + 1], k.pos[:, c, ds(g, 1)]).then_inc(s_ib, 1)
                pool.wait_ge(s_ib, 2)
                for c in range(2):
                    nc.gpsimd.indirect_dma_start(ya[:, s, c, :], None, k.ys,
                                                 bass.IndirectOffsetOnAxis(ap=ib[:, s, c:c + 1], axis=0)).then_inc(s_g[s], 16)

            paired(pool, G, gather)

        @block.vector
        def _(dve):
            with dve.Fori(0, G // 2) as i:
                for s in range(2):
                    g = i * 2 + s
                    dve.wait_ge(s_g[s], i * 32 + 32)
                    nc.vector.scalar_tensor_tensor(out=tile_of(k.h, g), in0=ya[:, s, 0, :], scalar=k.wtop[:, 0, ds(g, 1)],
                                                   in1=tile_of(k.h, g), op0=ALU.mult, op1=ALU.add).then_inc(s_a, 1)
                    dve.wait_ge(s_a, after(g + 1))
                    nc.vector.scalar_tensor_tensor(out=tile_of(k.h, g), in0=ya[:, s, 1, :], scalar=k.wtop[:, 1, ds(g, 1)],
                                                   in1=tile_of(k.h, g), op0=ALU.mult, op1=ALU.add).then_inc(s_h, 1)


def experts1(k):
    nc, d = k.nc, k.d
    NM = F1 // P
    with ExitStack() as ctx:
        sb = lambda n, s, dt=F32: k.sb(n, s, dt, ctx)
        w1 = sb("f_w1", [KT, 2, E, F1])
        w2 = sb("f_w2", [KT, 2, E, F1])
        w3 = sb("f_w3", [P, E, NM, C])
        x = sb("f_x", [P, 2, C])
        xT = sb("f_xT", [KT, 2, 2, P])
        sl = sb("f_sl", [P, 2, F1])
        hb = sb("f_h", [P, 2, F1])
        hT = sb("f_hT", [P, 2, NM, P])
        y = sb("f_y", [P, 2, C], BF16)
        pX = k.ps("f_pX", [P, 512], ctx)
        pA = k.ps("f_pA", [P, 2, 512], ctx)
        pB = k.ps("f_pB", [P, 2, 512], ctx)
        pT = k.ps("f_pT", [P, 512], ctx)
        pY = k.ps("f_pY", [P, 512], ctx)
        s_w, s_xt, s_xts, s_h, s_sl, s_hs, s_ht, s_hts, s_y, s_ys = (
            k.sem("f_" + n) for n in ("w", "xt", "xts", "h", "sl", "hs", "ht", "hts", "y", "ys"))
        s_x = [k.sem(f"f_x{i}") for i in range(2)]
        s_st = [k.sem(f"f_st{i}") for i in range(2)]
        block = ctx.enter_context(nc.Block())

        @block.sync
        def _(sp):
            k.start_at_one(sp)
            for e in range(E):
                sp.dma_start(w1[:, :, e, :], d["e1w1"][:, :, e, :]).then_inc(s_w, 16)
                sp.dma_start(w2[:, :, e, :], d["e1w2"][:, :, e, :]).then_inc(s_w, 16)
                sp.dma_start(w3[:, e, :, :], d["e1w3"][:, e, :, :]).then_inc(s_w, 16)
            move_rows(sp, x, k.xs, s_x, s_xt, y, k.ys1, s_st, s_ys, N1)

        @block.tensor
        def _(pe):
            pe.wait_ge(s_w, after(16 * 3 * E))

            def front(n, i, s):
                e = pe.value_load(k.eid[0:1, ds(n, 1)], min_val=0, max_val=E - 1)
                pe.wait_ge(s_x[s], after(i * 16 + 16))
                pe.wait_ge(s_xts, after(n))
                for c in range(2):
                    last = nc.tensor.transpose(pX[0:KT, c * P:(c + 1) * P], x[:, s, c * KT:(c + 1) * KT], k.ident[:])
                last.then_inc(s_xt, 1)
                pe.wait_ge(s_xts, after(n + 1))
                if type(n) is not int or n > 1:
                    pe.wait_ge(s_hs, after(n - 1))
                for c in range(2):
                    for p, w in ((pA, w1), (pB, w2)):
                        last = nc.tensor.matmul(p[:, s, :], xT[:, s, c, :],
                                                w[:, c, ds(e, 1), :].rearrange("p a f -> p (a f)"),
                                                start=c == 0, stop=c == 1)
                last.then_inc(s_h, 1)

            def back(n, i, s):
                e = pe.value_load(k.eid[0:1, ds(n, 1)], min_val=0, max_val=E - 1)
                pe.wait_ge(s_hs, after(n + 1))
                pe.wait_ge(s_hts, after(n))
                for m in range(NM):
                    last = nc.tensor.transpose(pT[:, m * P:(m + 1) * P], hb[:, s, m * P:(m + 1) * P], k.ident[:])
                last.then_inc(s_ht, 1)
                pe.wait_ge(s_hts, after(n + 1))
                pe.wait_ge(s_ys, after(n))
                for m in range(NM):
                    last = nc.tensor.matmul(pY[:, 0:C], hT[:, s, m, :], w3[:, ds(e, 1), m, :].rearrange("p a c -> p (a c)"),
                                            start=m == 0, stop=m == NM - 1)
                last.then_inc(s_y, 1)

            pipelined(pe, N1, front, back)

        @block.scalar
        def _(act):
            act.preload_act_table(ACT.Silu)

            def front(n, i, s):
                act.wait_ge(s_h, after(n + 1))
                if type(n) is not int or n > 1:
                    act.wait_ge(s_hs, after(n - 1))
                nc.scalar.activation(sl[:, s, :], pA[:, s, :], ACT.Silu).then_inc(s_sl, 1)

            def back(n, i, s):
                act.wait_ge(s_ht, after(n + 1))
                nc.scalar.activation(hT[:, s, :, :].rearrange("p m t -> p (m t)"), pT[:, :], ACT.Copy).then_inc(s_hts, 1)
                act.wait_ge(s_st[s], after(i * 16))
                act.wait_ge(s_y, after(n + 1))
                nc.scalar.activation(y[:, s, :], pY[:, 0:C], ACT.Copy).then_inc(s_ys, 1)

            pipelined(act, N1, front, back)

        @block.vector
        def _(dve):
            def front(n, i, s):
                dve.wait_ge(s_xt, after(n + 1))
                nc.vector.tensor_copy(xT[:, s, :, :],
                                      pX[0:KT, 0:2 * P].rearrange("p (c t) -> p c t", c=2)).then_inc(s_xts, 1)
                dve.wait_ge(s_sl, after(n + 1))
                if type(n) is not int or n > 1:
                    dve.wait_ge(s_ht, after(n - 1))
                nc.vector.tensor_tensor(hb[:, s, :], pB[:, s, :], sl[:, s, :], ALU.mult).then_inc(s_hs, 1)

            pipelined(dve, N1, front, lambda n, i, s: None)


def finish(k):
    nc, d = k.nc, k.d
    with ExitStack() as ctx:
        ya = k.sb("fi_y", [P, 2, C], BF16, ctx)
        ib = k.sb("fi_i", [P, 2], I32, ctx)
        s_h, s_o = k.sem("fi_h"), k.sem("fi_o")
        s_ib = k.plain_sem("fi_ib")
        s_g = [k.plain_sem(f"fi_g{i}") for i in range(2)]
        block = ctx.enter_context(nc.Block())

        @block.gpsimd
        def _(pool):
            def gather(g, i, s):
                pool.sem_clear(s_ib)
                if type(g) is not int:
                    pool.wait_ge(s_g[s], i * 16)
                pool.wait_ge(s_h, after(i * 2))
                nc.gpsimd.tensor_copy(ib[:, s:s + 1], k.pos[:, 0, ds(g, 1)]).then_inc(s_ib, 1)
                pool.wait_ge(s_ib, 1)
                nc.gpsimd.indirect_dma_start(ya[:, s, :], None, k.ys1,
                                             bass.IndirectOffsetOnAxis(ap=ib[:, s:s + 1], axis=0)).then_inc(s_g[s], 16)

            paired(pool, G, gather)

        @block.vector
        def _(dve):
            with dve.Fori(0, G // 2) as i:
                for s in range(2):
                    g = i * 2 + s
                    dve.wait_ge(s_g[s], i * 16 + 16)
                    nc.vector.scalar_tensor_tensor(out=tile_of(k.h, g), in0=ya[:, s, :], scalar=k.wtop[:, 0, ds(g, 1)],
                                                   in1=tile_of(k.h, g), op0=ALU.mult, op1=ALU.add).then_inc(s_h, 1)

        @block.sync
        def _(sp):
            k.start_at_one(sp)
            store_result(sp, k, s_o, lambda b: sp.wait_ge(s_h, after(b * NT + NT)))


def store_result(sp, k, s_o, ready=lambda b: None):
    out = k.d["out"]
    with sp.Fori(0, B) as b:
        ready(b)
        for t in range(NT):
            sp.dma_start(out[ds(b, 1), t * P:(t + 1) * P, :].rearrange("a p c -> p (a c)"),
                         tile_of(k.h, b * NT + t)).then_inc(s_o, 16)
    sp.wait_ge(s_o, after(16 * G))


def dump(k):
    with ExitStack() as ctx:
        s_o = k.sem("dump")
        block = ctx.enter_context(k.nc.Block())

        @block.sync
        def _(sp):
            k.start_at_one(sp)
            store_result(sp, k, s_o)


def second_stats(k):
    nc = k.nc
    with ExitStack() as ctx:
        xa = k.sb("ss_x", [P, 4, C], F32, ctx)
        s_st, s_lk, s_var, s_root, s_x, s_b, s_c = (k.sem("ss_" + n) for n in ("st", "lk", "var", "root", "x", "b", "c"))
        block = ctx.enter_context(nc.Block())

        @block.sync
        def _(sp):
            k.start_at_one(sp)

        @block.gpsimd
        def _(pool):
            root_step(k, pool, s_var, s_root)
            pool.wait_ge(s_var, after(2))
            nc.gpsimd.tensor_tensor(k.rstd2[:], k.vare[:], k.half[:, 0:G], ALU.pow).then_inc(s_root, 1)

        @block.vector
        def _(dve):
            stats_of_h(k, dve, s_st, s_lk, s_var, s_root)
            with dve.Fori(0, G // 4) as i:
                dve.wait_ge(s_b, after(i * 4))
                for t in range(4):
                    g = i * 4 + t
                    nc.vector.tensor_scalar(xa[:, t, :], tile_of(k.h, g), column_of(k.mean, g), column_of(k.rstd, g),
                                            ALU.subtract, ALU.mult).then_inc(s_x, 1)
                dve.wait_ge(s_x, after(i * 4 + 4))
                for t in range(4):
                    nc.vector.bn_stats(tile_of(k.stats, i * 4 + t), xa[:, t, :]).then_inc(s_b, 1)
            dve.wait_ge(s_b, after(G))
            nc.vector.tensor_copy(k.mean1[:], k.mean[:]).then_inc(s_c, 1)
            dve.wait_ge(s_c, after(1))
            finish_stats(k, linker(dve, s_lk, 7)).then_inc(s_var, 1)
            dve.wait_ge(s_root, after(2))


def memory(k):
    nc, d = k.nc, k.d
    with ExitStack() as mctx:
        k.mean1 = k.sb("mean1", [P, G], F32, mctx)
        k.rstd2 = k.sb("rstd2", [P, G], F32, mctx)
        y = nc.dram_tensor("m_y", (NTOK * B, C), F32, kind="Internal").ap()
        blocks = [nc.dram_tensor("m_blocks%d" % i, (NBLK, H, BLK, BLK), F32, kind="Internal").ap() for i in range(2)]
        second_stats(k)
        fast_weights(k, y, blocks)
        gate(k, y)


def fast_weights(k, y, blocks):
    nc, d = k.nc, k.d
    HF = PW // 2
    with ExitStack() as ctx:
        sb = lambda n, s, dt=F32: k.sb("m_" + n, s, dt, ctx)
        wa = sb("wa", [P, 3, PW])
        wb = sb("wb", [KB, 3, PW])
        ma = sb("ma", [P, 3, MOD])
        mb = sb("mb", [P, 3, MOD])
        mbias = sb("mbias", [64 + MOD, 3])
        lin = sb("lin", [P, 2, C])
        gb = sb("gb", [P, 3, 2, HD])
        lr = sb("lr", [P, 4, H])
        gv = sb("gv", [P, 2, H, HD])
        up = sb("up", [P, P])
        maskA = sb("maskA", [P, H, P])
        eye = sb("eye", [UNITS, BLK, BLK])
        Ab = sb("Ab", [UNITS, BLK, BLK])
        Ub = sb("Ub", [UNITS, BLK, BLK])
        prod = sb("prod", [UNITS, BLK, BLK])
        U0 = sb("U0", [P, H, P])
        yb = sb("yb", [P, NT, C])
        corner = sb("corner", [P, LEVELS, P], I32)
        wm = sb("wm", [P, 3 * H])
        woT = sb("woT", [P, H // 2, C])
        xf = sb("xf", [P, 4, 256])
        x0 = sb("x0", [P, P])
        x1 = sb("x1", [P, P])
        xk = sb("xk", [P, 3, P])
        zc = sb("zc", [P, PW])
        sq = sb("sq", [P, PW])
        zsq = sb("zsq", [P, PW])
        sm = sb("sm", [P, 4, H])
        z = sb("z", [P, 2, PW])
        nv = sb("nv", [P, NT, PW])
        dummy = sb("dummy", [1, LEVELS * NG])
        kb = sb("kb", [P, NT, PW])
        kq = sb("kq", [P, NT, H // 2, 2, P])
        kz = sb("kz", [P, H, P])
        AT = sb("AT", [P, NT, H, P])
        PT = sb("PT", [P, H, P])
        T = sb("T", [P, H, P])
        U = sb("U", [P, H, P])
        X = sb("X", [P, H, P])
        R = sb("R", [P, NG, 4 * HD + 32])
        D = sb("D", [P, PW])
        oT = sb("oT", [P, H // 2, P])
        S = sb("S", [P, H // 2, 2, HD])
        pj = k.ps("m_pj", [P, 2, 512], ctx)
        pg = k.ps("m_pg", [P, 2 * NG, 512], ctx)
        names = ("w c lk var root xf xt xts hd hds pj z1 sq ss rt z2 z3 zq tr trs kz kk kks "
                 "ka kas ao ai sub uo ui t1 t1s mx mxs my mys mu mus ks r dd dds ot ots su st yo yos ys").split()
        s = {n: k.sem("m_" + n) for n in names}
        block = ctx.enter_context(nc.Block())
        heads = lambda t: t.rearrange("p (h c) -> p h c", c=HD)
        per_head = lambda t: t.rearrange("p (h a) -> p h a", a=1).broadcast_to([P, H, HD])
        all_heads = lambda t: t.rearrange("p (a c) -> p a c", a=1).broadcast_to([P, H, HD])
        quad = lambda t, g: t[:, 4 * g:4 * g + 4, :].rearrange("p h c -> p (h c)")
        a_ = lambda g: pg[:, 2 * g, :]
        b_ = lambda g: pg[:, 2 * g + 1, :]

        @block.sync
        def _(sp):
            k.start_at_one(sp)
            for t, n in ((wa, "wa"), (wb, "wb"), (ma, "ma"), (mb, "mb"), (up, "up"), (eye, "eye"), (corner, "corner"),
                         (woT, "woT")):
                sp.dma_start(t[:], d[n]).then_inc(s["w"], 16)
            sp.dma_start(mbias[64:64 + MOD, :], d["mbias"]).then_inc(s["w"], 16)
            sp.dma_start(lin[:], d["lin"].broadcast_to([P, 2, C])).then_inc(s["w"], 16)
            sp.dma_start(gb[:], d["gb"].broadcast_to([P, 3, 2, HD])).then_inc(s["w"], 16)
            sp.dma_start(lr[:, 0, :], d["lr_scale"].broadcast_to([P, H])).then_inc(s["w"], 16)
            sp.wait_ge(s["w"], after(16 * 12))
            sp.wait_ge(s["c"], after(1))
            at, ut = blocks
            with sp.Fori(0, B) as b:
                for c in range(NT):
                    n = b * NT + c
                    sp.wait_ge(s["kas"], after(n * NG + 3))
                    for i in range(NBLK):
                        o = slice(i * BLK, (i + 1) * BLK)
                        sp.dma_start(at[i].rearrange("h s t -> s h t"), AT[o, c, :, o]).then_inc(s["ao"], 16)
                    sp.wait_ge(s["ao"], after(n * (16 * NBLK) + 16 * NBLK))
                    sp.dma_start(Ab[:], at.rearrange("i h s t -> (i h) s t")).then_inc(s["ai"], 16)
                    sp.wait_ge(s["sub"], after(n * SUB + SUB))
                    sp.dma_start(ut.rearrange("i h s t -> (i h) s t"), Ub[:]).then_inc(s["uo"], 16)
                    sp.wait_ge(s["uo"], after(n * 16 + 16))
                    for i in range(NBLK):
                        o = slice(i * BLK, (i + 1) * BLK)
                        sp.dma_start(U0[o, :, o], ut[i].rearrange("h s t -> s h t")).then_inc(s["ui"], 16)
            sp.wait_ge(s["ys"], after(16 * G))

        @block.gpsimd
        def _(pool):
            gp = nc.gpsimd
            for t in (xf, kz, R, S, U0):
                gp.memset(t[:], 0.0)
            gp.memset(xk[:], 1.0).then_inc(s["c"], 1)

            def norms(n, c):
                for m in range(3):
                    pool.wait_ge(s["var"], after(n * 4 + (m + 1 if m else 0) + 1))
                    gp.tensor_tensor(sm[:, 1, :], sm[:, 0, :], k.half[:, 0:H], ALU.pow).then_inc(s["root"], 1)
                    pool.wait_ge(s["z1"], after(n * 3 + m + 1))
                    zm = heads(nv[:, c, :] if m == 1 else z[:, m // 2, :])
                    gp.tensor_tensor(zm, zm, gv[:, 0, :, :] if m == 1 else all_heads(gb[:, m, 0, :]),
                                     ALU.mult).then_inc(s["z2"], 1)
                    pool.wait_ge(s["z2"], after(n * 3 + m + 1))
                    gp.tensor_tensor(zm, zm, gv[:, 1, :, :] if m == 1 else all_heads(gb[:, m, 1, :]),
                                     ALU.add).then_inc(s["z3"], 1)
                    if m == 0:
                        pool.wait_ge(s["z3"], after(n * 3 + 1))
                        gp.tensor_tensor(zsq[:], z[:, 0, :], z[:, 0, :], ALU.mult).then_inc(s["zq"], 1)
                        pool.wait_ge(s["var"], after(n * 4 + 2))
                        gp.tensor_tensor(sm[:, 1, :], sm[:, 0, :], k.half2[:, 0:H], ALU.pow).then_inc(s["root"], 1)

            def substitute(n):
                pool.wait_ge(s["ai"], after(n * 16 + 16))
                gp.tensor_tensor(Ub[:], eye[:], eye[:], ALU.mult).then_inc(s["sub"], 1)
                for j in range(BLK - 1):
                    shape = [UNITS, j + 1, BLK - 1 - j]
                    o = prod[:, 0:j + 1, j + 1:BLK]
                    pool.wait_ge(s["sub"], after(n * SUB + 2 * j + 1))
                    gp.tensor_tensor(o, Ub[:, 0:j + 1, j:j + 1].broadcast_to(shape),
                                     Ab[:, j:j + 1, j + 1:BLK].broadcast_to(shape), ALU.mult).then_inc(s["sub"], 1)
                    pool.wait_ge(s["sub"], after(n * SUB + 2 * j + 2))
                    gp.tensor_tensor(Ub[:, 0:j + 1, j + 1:BLK], Ub[:, 0:j + 1, j + 1:BLK], o, ALU.add).then_inc(s["sub"], 1)

            pool.wait_ge(s["w"], after(16 * 12))
            norms(0, 0)
            substitute(0)
            norms(1, 1)
            with pool.Fori(0, B - 1) as b:
                for c in range(NT):
                    substitute(b * NT + c + 1)
                    norms(b * NT + c + 2, (c + 2) % NT)
            substitute(G - 2)
            norms(G - 1, NT - 1)
            substitute(G - 1)

        @block.vector
        def _(dve):
            v = nc.vector
            dve.wait_ge(s["w"], after(16 * 12))
            dve.wait_ge(s["c"], after(1))
            lkn = [0]

            def link(ins):
                lkn[0] += 1
                ins.then_inc(s["lk"], 1)
                dve.wait_ge(s["lk"], after(lkn[0]))
            link(v.tensor_scalar(wb[64:KB, :, :], wb[64:KB, :, :], 0.1, None, ALU.mult))
            for w, n in ((wa, P), (wb, KB)):
                w3 = w[:, :, :].rearrange("p m (h c) -> p (m h) c", c=HD)
                link(v.tensor_reduce(wm[0:n, :], w3, AX.X, ALU.add))
                link(v.tensor_scalar(wm[0:n, :], wm[0:n, :], 1.0 / HD, None, ALU.mult))
                link(v.tensor_tensor(w3, w3, wm[0:n, :].rearrange("p (h a) -> p h a", a=1).broadcast_to([n, 3 * H, HD]),
                                     ALU.subtract))
            dve.wait_ge(s["hds"], after(1))
            link(v.tensor_scalar(lr[:, 1, :], lr[:, 1, :], 1.0, None, ALU.add))
            link(v.reciprocal(lr[:, 0, :], lr[:, 1, :]))
            link(v.tensor_scalar(lr[:, 1, :], lr[:, 0, :], 0.2, None, ALU.mult))
            link(v.tensor_scalar(lr[:, 2, :], lr[:, 1, :], 1.0, None, ALU.add))
            link(v.reciprocal(lr[:, 0, :], lr[:, 2, :]))
            link(v.scalar_tensor_tensor(out=lr[:, 3, :], in0=lr[:, 1, :], scalar=-1.0, in1=lr[:, 0, :], op0=ALU.mult,
                                        op1=ALU.mult))
            for i in range(2):
                link(v.tensor_tensor(gv[:, i, :, :], all_heads(gb[:, 1, i, :]), per_head(lr[:, 3, :]), ALU.mult))
            link(v.tensor_scalar(lr[:, 1, :], lr[:, 2, :], -1.0, None, ALU.mult))
            link(v.tensor_tensor(maskA[:], up[:, :].rearrange("p (a c) -> p a c", a=1).broadcast_to([P, H, P]),
                                 lr[:, 1, :].rearrange("p (h a) -> p h a", a=1).broadcast_to([P, H, P]), ALU.mult))

            def inputs(n):
                g = n
                dve.wait_ge(s["xt"], after(n))
                dst = [xf[:, j, 0:C] for j in range(4)]
                v.tensor_scalar(dst[0], tile_of(k.h, g), column_of(k.mean1, g), column_of(k.rstd, g),
                                ALU.subtract, ALU.mult).then_inc(s["xf"], 1)
                dve.wait_ge(s["xf"], after(n * 4 + 1))
                v.tensor_scalar(dst[1], dst[0], column_of(k.mean, g), column_of(k.rstd2, g),
                                ALU.subtract, ALU.mult).then_inc(s["xf"], 1)
                dve.wait_ge(s["xf"], after(n * 4 + 2))
                v.tensor_tensor(dst[2], dst[1], lin[:, 0, :], ALU.mult).then_inc(s["xf"], 1)
                dve.wait_ge(s["xf"], after(n * 4 + 3))
                v.tensor_tensor(dst[3], dst[2], lin[:, 1, :], ALU.add).then_inc(s["xf"], 1)

            def head_norm(n, m, c):
                i = n * 4 + (m + 1 if m else 0) + 1
                dve.wait_ge(s["sq"], after(n * 3 + m + 1))
                v.tensor_reduce(sm[:, 2, :], heads(sq[:]), AX.X, ALU.add).then_inc(s["ss"], 1)
                dve.wait_ge(s["ss"], after(n * 3 + m + 1))
                v.tensor_scalar(sm[:, 0, :], sm[:, 2, :], 1.0 / HD, EPS, ALU.mult, ALU.add).then_inc(s["var"], 1)
                if m != 1:
                    dve.wait_ge(s["tr"], after(n * 4))
                dve.wait_ge(s["root"], after(i))
                v.tensor_tensor(heads(nv[:, c, :] if m == 1 else z[:, m // 2, :]), heads(zc[:]), per_head(sm[:, 1, :]),
                                ALU.mult).then_inc(s["z1"], 1)

            def unit_keys(n, c):
                dve.wait_ge(s["zq"], after(n + 1))
                v.tensor_reduce(sm[:, 0, :], heads(zsq[:]), AX.X, ALU.add).then_inc(s["var"], 1)
                dve.wait_ge(s["root"], after(n * 4 + 2))
                v.tensor_scalar(sm[:, 2, :], sm[:, 1, :], 1e-6, None, ALU.add).then_inc(s["rt"], 1)
                dve.wait_ge(s["rt"], after(n * 4 + 1))
                v.reciprocal(sm[:, 3, :], sm[:, 2, :]).then_inc(s["rt"], 1)
                dve.wait_ge(s["rt"], after(n * 4 + 2))
                v.tensor_tensor(heads(z[:, 0, :]), heads(z[:, 0, :]), per_head(sm[:, 3, :]), ALU.mult).then_inc(s["rt"], 1)
                dve.wait_ge(s["rt"], after(n * 4 + 3))
                v.tensor_tensor(heads(kb[:, c, :]), heads(z[:, 0, :]), per_head(lr[:, 2, :]), ALU.mult).then_inc(s["rt"], 1)

            def single_keys(n, c):
                dve.wait_ge(s["kk"], after(n * NG))
                for p3 in range(2):
                    dve.wait_ge(s["trs"], after(n * 4 + p3 + 1))
                    for o in (0, 64):
                        v.tensor_copy(kz[o:o + 64, p3 * 6 + o // 64:p3 * 6 + 6:2, :],
                                      kq[o:o + 64, c, 3 * p3:3 * p3 + 3, 0, :]).then_inc(s["kz"], 1)

            three = lambda t: t.rearrange("p (a c) -> p a c", a=1).broadcast_to([P, 4, P])

            def decays(n, c):
                for g3 in range(NG):
                    q4 = slice(4 * g3, 4 * g3 + 4)
                    dve.wait_ge(s["ka"], after(n * NG + g3 + 1))
                    v.tensor_tensor(AT[:, c, q4, :], pj[:, g3 % 2, :].rearrange("p (h t) -> p h t", t=P), maskA[:, q4, :],
                                    ALU.mult).then_inc(s["kas"], 1)

            def chunk(n, c, more, next_=True):
                first, m, cm = c == 0, n + 2, (c + 2) % NT
                for g3 in range(NG):
                    q4 = slice(4 * g3, 4 * g3 + 4)
                    dve.wait_ge(s["kk"], after(n * NG + g3 + 1))
                    v.tensor_tensor(PT[:, q4, :], b_(g3).rearrange("p (h t) -> p h t", t=P), maskA[:, q4, :],
                                    ALU.mult).then_inc(s["kks"], 1)
                if next_:
                    single_keys(n + 1, (c + 1) % NT)
                if more:
                    inputs(m)
                for lv in range(LEVELS):
                    for g3 in range(NG):
                        q4 = slice(4 * g3, 4 * g3 + 4)
                        dve.wait_ge(s["my"], after(n * (LEVELS * NG) + lv * NG + g3 + 1))
                        v.memset(dummy[:, lv * NG + g3:lv * NG + g3 + 1], 0.0)
                        v.copy_predicated(T[:, q4, :], three(corner[:, lv, :]),
                                          b_(g3).rearrange("p (h t) -> p h t", t=P)).then_inc(s["mys"], 1)
                    if next_ and lv == 0:
                        decays(n + 1, (c + 1) % NT)
                    if more and lv == 1:
                        head_norm(m, 0, cm)
                    if more and lv == 2:
                        unit_keys(m, cm)
                        head_norm(m, 1, cm)
                for g3 in range(NG):
                    if first:
                        v.tensor_copy(R[:, g3, 0:256], nv[:, c, 256 * g3:256 * g3 + 256]).then_inc(s["r"], 1)
                    else:
                        dve.wait_ge(s["ks"], after(n * NG + g3 + 1))
                        v.tensor_tensor(R[:, g3, 0:256], a_(g3)[:, 0:256], nv[:, c, 256 * g3:256 * g3 + 256],
                                        ALU.add).then_inc(s["r"], 1)
                if more:
                    head_norm(m, 2, cm)
                for g3 in range(NG):
                    if c < NT - 1:
                        dve.wait_ge(s["su"], after(n * NG + g3 + 1))
                        src = b_(g3)[:, 256:512].rearrange("p (q a c) -> p q a c", q=2, a=2)
                        for o in (0, 64):
                            dst = S[o:o + 64, 2 * g3:2 * g3 + 2, o // 64, :]
                            if first:
                                v.tensor_scalar(dst, src[o:o + 64, :, o // 64, :], -1.0, None, ALU.mult).then_inc(s["st"], 1)
                            else:
                                v.tensor_tensor(dst, dst, src[o:o + 64, :, o // 64, :], ALU.subtract).then_inc(s["st"], 1)
                    else:
                        dve.sem_inc(s["st"], 2)
                dve.wait_ge(s["yo"], after(n + 1))
                dve.wait_ge(s["ys"], after(n * 16))
                v.tensor_copy(yb[:, c, :], a_(0)[:, 256:256 + C]).then_inc(s["yos"], 1)

            for n in range(2):
                inputs(n)
                head_norm(n, 0, n)
                unit_keys(n, n)
                head_norm(n, 1, n)
                head_norm(n, 2, n)
                if n == 0:
                    single_keys(0, 0)
                    decays(0, 0)
            with dve.Fori(0, B - 1) as b:
                for c in range(NT):
                    chunk(b * NT + c, c, True)
            for c in range(NT):
                chunk(G - NT + c, c, c == 0, c < NT - 1)

        @block.tensor
        def _(pe):
            mm = nc.tensor.matmul
            pe.wait_ge(s["w"], after(16 * 12))
            pe.wait_ge(s["lk"], after(7))

            def ahead(step, n, c):
                if step == 0:
                    pe.wait_ge(s["xf"], after(n * 4 + 4))
                    pe.wait_ge(s["trs"], after(n * 4))
                    pe.wait_ge(s["kas"], after(n * NG))
                    for i in range(2):
                        last = nc.tensor.transpose(pj[:, 0, i * P:(i + 1) * P], xf[:, 3, i * P:(i + 1) * P], k.ident[:])
                    last.then_inc(s["xt"], 1)
                if step == 1:
                    pe.wait_ge(s["xts"], after(n * 3 + 3))
                    for m in range(3):
                        mm(pj[64:64 + MOD, 1, m * P:(m + 1) * P], ma[:, m, :], x0[:], start=True, stop=False)
                        last = mm(pj[64:64 + MOD, 1, m * P:(m + 1) * P], mb[:, m, :], x1[:], start=False, stop=True)
                    last.then_inc(s["hd"], 1)
                if step in (2, 3, 4):
                    m = step - 2
                    if m == 0:
                        pe.wait_ge(s["hds"], after(n * 3 + 4))
                    else:
                        pe.wait_ge(s["sq"], after(n * 3 + m))
                    for f in range(2):
                        mm(pj[:, f, 0:HF], x0[:], wa[:, m, f * HF:(f + 1) * HF], start=True, stop=False)
                        last = mm(pj[:, f, 0:HF], xk[0:KB, m, :], wb[:, m, f * HF:(f + 1) * HF], start=False, stop=True)
                    last.then_inc(s["pj"], 1)
                if step in (5, 6):
                    m = step - 5
                    if m == 0:
                        pe.wait_ge(s["sq"], after(n * 3 + 3))
                        pe.wait_ge(s["rt"], after(n * 4 + 3))
                    else:
                        pe.wait_ge(s["z3"], after(n * 3 + 3))
                    for f in range(2):
                        if m == 1:
                            pe.wait_ge(s["trs"], after(n * 4 + f + 1))
                        for q in range(3):
                            last = nc.tensor.transpose(pj[:, f, q * P:(q + 1) * P], z[:, m, (3 * f + q) * P:(3 * f + q + 1) * P],
                                                       k.ident[:])
                        last.then_inc(s["tr"], 1)

            def decays(n, c):
                pe.wait_ge(s["trs"], after(n * 4 + 4))
                pe.wait_ge(s["kz"], after(n * 4 + 4))
                for g3 in range(NG):
                    if g3 == 2:
                        pe.wait_ge(s["kas"], after(n * NG + 1))
                    for hh in range(4):
                        h = 4 * g3 + hh
                        last = mm(pj[:, g3 % 2, hh * P:(hh + 1) * P], kz[:, h, :], kq[:, c, h // 2, 0, :], start=True, stop=True)
                    last.then_inc(s["ka"], 1)

            def chunk(n, c, more, next_=True):
                first, m, cm = c == 0, n + 2, (c + 2) % NT
                pe.wait_ge(s["dds"], after(n * 3))
                pe.wait_ge(s["ots"], after(n * 3))
                pe.wait_ge(s["st"], after(n * 6))
                pe.wait_ge(s["yos"], after(n))
                for g3 in range(NG):
                    for hh in range(4):
                        h = 4 * g3 + hh
                        last = mm(b_(g3)[:, hh * P:(hh + 1) * P], kz[:, h, :], kq[:, c, h // 2, 1, :], start=True, stop=True)
                    last.then_inc(s["kk"], 1)
                pe.wait_ge(s["ui"], after(n * (16 * NBLK) + 16 * NBLK))
                for g3 in range(NG):
                    for hh in range(4):
                        last = nc.tensor.transpose(a_(g3)[:, hh * P:(hh + 1) * P], U0[:, 4 * g3 + hh, :], k.ident[:])
                    last.then_inc(s["t1"], 1)
                for lv in range(LEVELS):
                    j = n * (LEVELS * NG) + lv * NG
                    for g3 in range(NG):
                        if lv == 0:
                            pe.wait_ge(s["t1s"], after(n * NG + g3 + 1))
                        else:
                            pe.wait_ge(s["mus"], after(j - NG + g3 + 1))
                        for hh in range(4):
                            h = 4 * g3 + hh
                            last = mm(a_(g3)[:, hh * P:(hh + 1) * P], AT[:, c, h, :], T[:, h, :], start=True, stop=True)
                        last.then_inc(s["mx"], 1)
                    if more and lv == 1:
                        ahead(1, m, cm)
                    for g3 in range(NG):
                        pe.wait_ge(s["mxs"], after(j + g3 + 1))
                        if lv == 0:
                            pe.wait_ge(s["kks"], after(n * NG + g3 + 1))
                        for hh in range(4):
                            h = 4 * g3 + hh
                            last = mm(b_(g3)[:, hh * P:(hh + 1) * P], (U0 if lv == 0 else U)[:, h, :], X[:, h, :],
                                      start=True, stop=True)
                        last.then_inc(s["my"], 1)
                    if next_ and lv == 0:
                        decays(n + 1, (c + 1) % NT)
                    if more and lv == 2:
                        ahead(3, m, cm)
                    for g3 in range(NG):
                        pe.wait_ge(s["mys"], after(j + g3 + 1))
                        for hh in range(4):
                            last = nc.tensor.transpose(a_(g3)[:, hh * P:(hh + 1) * P], T[:, 4 * g3 + hh, :], k.ident[:])
                        last.then_inc(s["mu"], 1)
                    if more and lv < 2:
                        ahead(2 * lv, m, cm)
                if first:
                    pe.wait_ge(s["mus"], after(n * (LEVELS * NG) + LEVELS * NG))
                    pe.sem_inc(s["ks"], 3)
                else:
                    for g3 in range(NG):
                        pe.wait_ge(s["mus"], after(n * (LEVELS * NG) + (LEVELS - 1) * NG + g3 + 1))
                        for q in range(2):
                            pr = 2 * g3 + q
                            last = mm(a_(g3)[:, q * P:(q + 1) * P], kq[:, c, pr, 0, :],
                                      S[:, pr, :, :].rearrange("p a c -> p (a c)"), start=True, stop=True)
                        last.then_inc(s["ks"], 1)
                if more:
                    ahead(4, m, cm)
                for g3 in range(NG):
                    pe.wait_ge(s["r"], after(n * NG + g3 + 1))
                    for hh in range(4):
                        h = 4 * g3 + hh
                        last = mm(b_(g3)[:, hh * P:hh * P + 96], U[:, h, :], R[:, g3, hh * HD:hh * HD + 96], start=True, stop=True)
                    last.then_inc(s["dd"], 1)
                for g3 in range(NG):
                    pe.wait_ge(s["dds"], after(n * NG + g3 + 1))
                    for q in range(2):
                        pr = 2 * g3 + q
                        o = a_(g3)[:, q * P:(q + 1) * P]
                        if not first:
                            mm(o, S[:, pr, :, :].rearrange("p a c -> p (a c)"), kq[:, c, pr, 1, :], start=True, stop=False,
                               skip_group_check=True)
                        for e in range(2):
                            h = 2 * pr + e
                            last = mm(a_(g3)[64 * e:64 * e + 64, q * P:(q + 1) * P], D[:, h * HD:(h + 1) * HD], PT[:, h, :],
                                      start=first, stop=True, skip_group_check=True)
                    last.then_inc(s["ot"], 1)
                    if c < NT - 1:
                        for q in range(2):
                            pr = 2 * g3 + q
                            last = mm(b_(g3)[:, 256 + q * P:256 + (q + 1) * P], kb[:, c, pr * P:(pr + 1) * P],
                                      D[:, pr * P:(pr + 1) * P], start=True, stop=True)
                        last.then_inc(s["su"], 1)
                if c == NT - 1:
                    pe.sem_inc(s["su"], 3)
                if more:
                    ahead(5, m, cm)
                pe.wait_ge(s["ots"], after(n * NG + 3))
                for q in range(H // 2):
                    last = mm(a_(0)[:, 256:256 + C], oT[:, q, :], woT[:, q, :], start=q == 0, stop=q == H // 2 - 1)
                last.then_inc(s["yo"], 1)
                if more:
                    ahead(6, m, cm)

            for step in range(7):
                ahead(step, 0, 0)
            decays(0, 0)
            for step in range(7):
                ahead(step, 1, 1)
            with pe.Fori(0, B - 1) as b:
                for c in range(NT):
                    chunk(b * NT + c, c, True)
            for c in range(NT):
                chunk(G - NT + c, c, c == 0, c < NT - 1)

        @block.scalar
        def _(act):
            A = nc.scalar.activation
            act.wait_ge(s["w"], after(16 * 12))
            A(lr[:, 1, :], lr[:, 0, :], ACT.Exp, scale=-1.0).then_inc(s["hds"], 1)
            act.preload_act_table(ACT.Gelu)

            def ahead(step, n, c):
                if step == 0:
                    act.wait_ge(s["xt"], after(n + 1))
                    act.wait_ge(s["pj"], after(n * 3))
                    A(x0[:], pj[:, 0, 0:P], ACT.Copy).then_inc(s["xts"], 1)
                    A(x1[:], pj[:, 0, P:2 * P], ACT.Copy).then_inc(s["xts"], 1)
                    A(xk[0:64, :, :], pj[0:64, 0, P:2 * P].rearrange("p (a t) -> p a t", a=1).broadcast_to([64, 3, P]),
                      ACT.Copy).then_inc(s["xts"], 1)
                if step == 1:
                    act.wait_ge(s["hd"], after(n + 1))
                    for m in range(3):
                        A(xk[64:64 + MOD, m, :], pj[64:64 + MOD, 1, m * P:(m + 1) * P], ACT.Gelu,
                          bias=mbias[64:64 + MOD, m:m + 1]).then_inc(s["hds"], 1)
                if step in (2, 3, 4):
                    m = step - 2
                    act.wait_ge(s["pj"], after(n * 3 + m + 1))
                    act.wait_ge(s["z1"], after(n * 3 + m))
                    A(zc[:].rearrange("p (f c) -> p f c", f=2), pj[:, :, 0:HF], ACT.Copy)
                    A(sq[:].rearrange("p (f c) -> p f c", f=2), pj[:, :, 0:HF], ACT.Square).then_inc(s["sq"], 1)
                if step in (5, 6):
                    m = step - 5
                    for f in range(2):
                        act.wait_ge(s["tr"], after(n * 4 + 2 * m + f + 1))
                        A(kq[:, c, 3 * f:3 * f + 3, m, :], pj[:, f, 0:3 * P].rearrange("p (h t) -> p h t", t=P),
                          ACT.Copy).then_inc(s["trs"], 1)

            def chunk(n, c, more):
                m, cm = n + 2, (c + 2) % NT
                for g3 in range(NG):
                    act.wait_ge(s["t1"], after(n * NG + g3 + 1))
                    A(quad(T, g3), a_(g3), ACT.Copy).then_inc(s["t1s"], 1)
                for lv in range(LEVELS):
                    j = n * (LEVELS * NG) + lv * NG
                    for g3 in range(NG):
                        act.wait_ge(s["mx"], after(j + g3 + 1))
                        A(quad(X, g3), a_(g3), ACT.Copy).then_inc(s["mxs"], 1)
                    if more and lv > 0:
                        ahead(2 * lv - 1, m, cm)
                    for g3 in range(NG):
                        act.wait_ge(s["mu"], after(j + g3 + 1))
                        A(quad(U, g3), a_(g3), ACT.Copy).then_inc(s["mus"], 1)
                    if more and lv < 2:
                        ahead(2 * lv, m, cm)
                if more:
                    ahead(4, m, cm)
                for g3 in range(NG):
                    act.wait_ge(s["dd"], after(n * NG + g3 + 1))
                    act.wait_ge(s["su"], after(n * NG))
                    A(heads(D[:, 256 * g3:256 * g3 + 256]), b_(g3).rearrange("p (h t) -> p h t", t=P)[:, :, 0:HD],
                      ACT.Copy).then_inc(s["dds"], 1)
                act.wait_ge(s["yo"], after(n))
                for g3 in range(NG):
                    act.wait_ge(s["ot"], after(n * NG + g3 + 1))
                    A(oT[:, 2 * g3:2 * g3 + 2, :].rearrange("p q t -> p (q t)"), a_(g3)[:, 0:256], ACT.Copy).then_inc(s["ots"], 1)
                if more:
                    ahead(5, m, cm)
                    ahead(6, m, cm)
                act.wait_ge(s["yos"], after(n + 1))
                act.dma_start(y[ds(n * P, P), :], yb[:, c, :]).then_inc(s["ys"], 16)

            for n in range(2):
                for step in range(7):
                    ahead(step, n, n)
            with act.Fori(0, B - 1) as b:
                for c in range(NT):
                    chunk(b * NT + c, c, True)
            for c in range(NT):
                chunk(G - NT + c, c, c == 0)


def gate(k, y):
    nc, d = k.nc, k.d
    with ExitStack() as ctx:
        sb = lambda n, s, dt=F32: k.sb("g_" + n, s, dt, ctx)
        wg = sb("wg", [KT + 1, 2, C])
        xb = sb("xb", [P, 2, C])
        xT = sb("xT", [KT + 1, 2, 2 * P])
        sg = sb("sg", [P, 2, C])
        ym = sb("ym", [P, G, C])
        pX = k.ps("g_pX", [P, 2, 512], ctx)
        pG = k.ps("g_pG", [P, 512], ctx)
        s_w, s_y, s_on, s_x, s_xt, s_xts, s_g, s_sg, s_m, s_h = (k.sem("g_" + n) for n in ("w", "y", "on", "x", "xt", "xts", "g", "sg", "m", "h"))
        block = ctx.enter_context(nc.Block())

        @block.sync
        def _(sp):
            k.start_at_one(sp)
            sp.dma_start(wg[:], d["wg"]).then_inc(s_w, 16)
            sp.dma_start(ym[:], y.rearrange("(g p) c -> p g c", p=P)).then_inc(s_y, 16)
            sp.wait_ge(s_w, after(16))

        @block.vector
        def _(dve):
            nc.vector.memset(xT[KT:KT + 1, :, :], 1.0).then_inc(s_on, 1)
            dve.wait_ge(s_y, after(16))
            with dve.Fori(0, G // 2) as i:
                dve.wait_ge(s_xt, after(i))
                for t in range(2):
                    g = i * 2 + t
                    nc.vector.tensor_scalar(xb[:, t, :], tile_of(k.h, g), column_of(k.mean1, g), column_of(k.rstd, g),
                                            ALU.subtract, ALU.mult).then_inc(s_x, 1)
                dve.wait_ge(s_sg, after(i + 1))
                for t in range(2):
                    nc.vector.tensor_tensor(sg[:, t, :], sg[:, t, :], tile_of(ym, i * 2 + t), ALU.mult).then_inc(s_m, 1)
                dve.wait_ge(s_m, after(i * 2 + 2))
                for t in range(2):
                    nc.vector.tensor_tensor(tile_of(k.h, i * 2 + t), tile_of(k.h, i * 2 + t), sg[:, t, :], ALU.add).then_inc(s_h, 1)

        @block.tensor
        def _(pe):
            pe.wait_ge(s_w, after(16))
            pe.wait_ge(s_on, after(1))
            with pe.Fori(0, G // 2) as i:
                pe.wait_ge(s_x, after(i * 2 + 2))
                pe.wait_ge(s_xts, after(i * 2))
                for t in range(2):
                    for c in range(2):
                        last = nc.tensor.transpose(pX[0:KT, c, t * P:(t + 1) * P], xb[:, t, c * KT:(c + 1) * KT], k.ident[:])
                last.then_inc(s_xt, 1)
                pe.wait_ge(s_xts, after(i * 2 + 2))
                pe.wait_ge(s_sg, after(i))
                for t in range(2):
                    for c in range(2):
                        last = nc.tensor.matmul(pG[:, t * C:(t + 1) * C], xT[0:KT + c, c, t * P:(t + 1) * P], wg[0:KT + c, c, :],
                                                start=c == 0, stop=c == 1)
                last.then_inc(s_g, 1)

        @block.scalar
        def _(act):
            act.preload_act_table(ACT.Sigmoid)
            with act.Fori(0, G // 2) as i:
                act.wait_ge(s_xt, after(i + 1))
                for c in range(2):
                    nc.scalar.activation(xT[0:KT, c, :], pX[0:KT, c, 0:2 * P], ACT.Copy).then_inc(s_xts, 1)
                act.wait_ge(s_g, after(i + 1))
                act.wait_ge(s_h, after(i * 2))
                nc.scalar.activation(sg[:].rearrange("p t c -> p (t c)"), pG[:, 0:2 * C], ACT.Sigmoid).then_inc(s_sg, 1)


def build(nc, d, stop=99):
    with ExitStack() as ctx:
        k = Core(nc, ctx, d)
        stages = [tokenizer, attention,
                  lambda k: route(k, "r0", 2, N0, "gate0_w", "gate0_b"), experts0, combine0,
                  lambda k: (k.recycle(), memory(k)),
                  lambda k: route(k, "r1", 1, N1, "gate1_w", "gate1_b"), experts1, finish]
        for f in stages[:stop]:
            f(k)
        if stop < len(stages):
            dump(k)


def hostprep(inputs):
    f = lambda n: np.asarray(inputs[n])
    a = {}
    x = f("x")
    for lv, p in enumerate((1, 2, 4)):
        n = 64 // p
        a[f"x{lv}r"] = x.reshape(B, 3, n, p, n, p).transpose(2, 4, 0, 3, 5, 1).reshape(n * n, B * p * p * 3)
        a[f"idx{lv}"] = f(f"L0_tok_idx{lv}")
    w0 = np.zeros((P, 64), np.float32)
    w0[0:48] = f("L0_tok_W0").T
    w0[64:112] = f("L0_tok_W0").T
    a["w0T"] = w0
    a["w1T"] = f("L0_tok_W1").T.reshape(2, KT, 64).transpose(1, 0, 2)
    a["w2T"] = f("L0_tok_W2").T.reshape(6, P, 64).transpose(1, 0, 2)
    a["wfT"] = f("L0_tok_Wf").T.reshape(3, 64, C).transpose(1, 0, 2)
    a["lb"] = np.stack([f("L0_tok_b0"), f("L0_tok_b1"), f("L0_tok_b2")], 1)
    a["bf"] = f("L0_tok_bf")[None]
    a["txt"] = f("txt")
    for name, n in (("up1", 64), ("up2", 16)):
        m = np.zeros((n, 256), np.float32)
        at = np.clip((np.arange(256, dtype=np.float32) + np.float32(0.5)) * np.float32(n / 256) - np.float32(0.5), 0, n - 1)
        lo = np.floor(at).astype(int)
        for t in range(256):
            m[lo[t], t] += 1 - (at[t] - lo[t])
            m[min(lo[t] + 1, n - 1), t] += at[t] - lo[t]
        a[name] = m
    w = f("L0_attn_w_qkv")

    def heads(w):
        o = np.zeros((2, KT, NH0, 32), np.float32)
        o[..., 0:DH0] = w.reshape(2, KT, NH0, DH0)
        return o.reshape(2, KT, 2, P).transpose(1, 0, 2, 3)
    tiles = lambda w: w.reshape(2, KT, -1).transpose(1, 0, 2)
    a["wq"], a["wk"], a["wv"] = heads(w[:, 0:C]), heads(w[:, C:2 * C]), tiles(w[:, 2 * C:])
    wp = np.zeros((2, 4, 32, C), np.float32)
    wp[:, :, 0:DH0] = f("L0_attn_w_proj").reshape(2, 4, DH0, C)
    wp[0, 0, DH0] = f("L0_attn_b_proj")
    a["wp"] = wp.reshape(2, P, C).transpose(1, 0, 2)
    sel = np.zeros((4, 32, 4, 32), np.float32)
    for j in range(4):
        sel[j, DH0, j] = 1
    a["dsel"] = sel.reshape(P, P)
    a["gate0_w"], a["gate0_b"] = tiles(f("L0_ffn_gate_w")), f("L0_ffn_gate_b")[None]
    a["gate1_w"], a["gate1_b"] = tiles(f("L1_ffn_router_w")), f("L1_ffn_router_b")[None]
    a["tri"] = np.triu(np.ones((P, P), np.float32), 1)
    a["rank8"] = np.tile(np.arange(E, 0, -1, dtype=np.float32), (P, 1))
    a["starts"] = (np.arange(N0, dtype=np.float32) * P)[None]
    w1 = np.zeros((KT + 1, 2, E, F0), np.float32)
    w1[0:KT] = f("L0_ffn_w1").reshape(E, 2, KT, F0).transpose(2, 1, 0, 3)
    w1[KT, 1] = f("L0_ffn_b1")
    a["e0w1"] = w1
    a["e0w2"] = f("L0_ffn_w2").reshape(E, F0 // P, P, C).transpose(2, 0, 1, 3)
    a["e0b2"] = f("L0_ffn_b2")[None]
    a["e1w1"] = f("L1_ffn_w1").reshape(E, 2, KT, F1).transpose(2, 1, 0, 3)
    a["e1w2"] = f("L1_ffn_w2").reshape(E, 2, KT, F1).transpose(2, 1, 0, 3)
    a["e1w3"] = f("L1_ffn_w3").reshape(E, F1 // P, P, C).transpose(2, 0, 1, 3)
    wa = np.zeros((P, 3, PW), np.float32)
    wb = np.zeros((KB, 3, PW), np.float32)
    ma = np.zeros((P, 3, MOD), np.float32)
    mb = np.zeros((P, 3, MOD), np.float32)
    for m, n in enumerate("kvq"):
        w, m1 = f(f"L1_attn_W{n}").T, f(f"L1_attn_{n}m_w1").T
        wa[:, m], wb[0:64, m] = w[0:P], w[P:]
        wb[64:64 + MOD, m], wb[64 + MOD, m] = f(f"L1_attn_{n}m_w2").T, f(f"L1_attn_{n}m_b2")
        ma[:, m], mb[0:64, m] = m1[0:P], m1[P:]
    a["wa"], a["wb"], a["ma"], a["mb"] = wa, wb, ma, mb
    a["mbias"] = np.stack([f(f"L1_attn_{n}m_b1") for n in "kvq"], 1)
    a["lin"] = np.stack([f("L1_attn_ln_in_g"), f("L1_attn_ln_in_b")])[None]
    a["gb"] = np.stack([np.stack([f(f"L1_attn_ln{n}_g"), f(f"L1_attn_ln{n}_b")]) for n in "kvq"])[None]
    a["lr_scale"] = f("L1_attn_lr_scale")[None]
    a["up"] = np.triu(np.ones((P, P), np.float32), 1)
    t, s = np.arange(P)[:, None], np.arange(P)[None, :]
    corner = np.zeros((P, LEVELS, P), np.int32)
    for i, lv in enumerate(range(7 - LEVELS, 7)):
        corner[:, i] = (t >> (lv + 1) == s >> (lv + 1)) & ((t >> lv) & 1 == 1) & ((s >> lv) & 1 == 0)
    a["corner"] = corner
    a["eye"] = np.tile(np.eye(BLK, dtype=np.float32), (UNITS, 1, 1))
    a["woT"] = f("L1_attn_Wo").T.reshape(H // 2, P, C).transpose(1, 0, 2)
    wg = np.zeros((KT + 1, 2, C), np.float32)
    wg[0:KT] = tiles(f("L1_attn_Wg").T)
    wg[KT, 1] = f("L1_attn_bg")
    a["wg"] = wg
    return {n: np.ascontiguousarray(v) for n, v in a.items()}




def kernel(**inputs):
    import concourse.bacc as bacc
    from concourse.bass_utils import run_bass_kernel_spmd

    arrays = hostprep(inputs)
    nc = bacc.Bacc("TRN2", target_bir_lowering=False, num_devices=1)
    d = {n: nc.dram_tensor("in_" + n, v.shape, mybir.dt.from_np(v.dtype), kind="ExternalInput").ap()
         for n, v in arrays.items()}
    d["out"] = nc.dram_tensor("out", (B, NTOK, C), F32, kind="ExternalOutput").ap()
    build(nc, d)
    r = run_bass_kernel_spmd(nc, [{"in_" + n: v for n, v in arrays.items()}], core_ids=[0])
    return r.results[0]["out"]
```

```python
from contextlib import ExitStack

import numpy as np
import concourse.bass as bass
from concourse import mybir

F32 = mybir.dt.float32
BF16 = mybir.dt.bfloat16
I32 = mybir.dt.int32
ACT = mybir.ActivationFunctionType
ALU = mybir.AluOpType
AX = mybir.AxisListType

P = 128
B = 8
C = 192
KT = 96
NT = 3
G = B * NT
NTOK = NT * P
EPS = 1e-5
E = 8
NH0, DH0 = 8, 24
SCALE = DH0 ** -0.5
F0, F1 = 768, 512
N0 = 2 * G + E - 1
N1 = G + E - 1
NX = 56
H, HD = 12, 64
PW = H * HD
MOD = 48
KB = 64 + MOD + 1
NG = 3
BLK = 16
NBLK = P // BLK
UNITS = NBLK * H
LEVELS = 3
SUB = 2 * BLK - 1
SPLIT = 7


def ds(start, size):
    return bass.ds(start, size)


def after(n):
    return n + 1


class Core:

    def __init__(self, nc, ctx, d):
        self.nc, self.ctx, self.d = nc, ctx, d
        self.fresh, self.used = [], []
        self.h = self.sb("h", [P, G, C])
        self.ident = self.sb("ident", [P, P])
        self.ones = self.sb("ones", [P, P])
        self.stats = self.sb("stats", [P, G, 6])
        self.tmp24 = self.sb("tmp24", [P, 4, G])
        self.mean = self.sb("mean", [P, G])
        self.rstd = self.sb("rstd", [P, G])
        self.rstd12 = self.sb("rstd12", [P, G])
        self.vare = self.sb("vare", [P, G])
        self.half2 = self.sb("half2", [P, G])
        self.half = self.sb("half", [P, 2 * G])
        self.wtop = self.sb("wtop", [P, 2, G])
        self.pos = self.sb("pos", [P, 2, G], I32)
        self.eid = self.sb("eid", [1, N0], I32)
        self.xs = nc.dram_tensor("xs", (NX * P, C), F32, kind="Internal").ap()
        self.ys = nc.dram_tensor("ys", (N0 * P, C), F32, kind="Internal").ap()
        self.ys1 = nc.dram_tensor("ys1", (N1 * P, C), BF16, kind="Internal").ap()
        self.s_consts = self.sem("s_consts")

    def sb(self, name, shape, dt=F32, ctx=None):
        return (ctx or self.ctx).enter_context(self.nc.sbuf_tensor(name, shape, dt))

    def ps(self, name, shape, ctx, dt=F32):
        return ctx.enter_context(self.nc.psum_tensor(name, shape, dt))

    def sem(self, name):
        self.fresh.append(self.plain_sem(name))
        return self.fresh[-1]

    def plain_sem(self, name):
        self.used.append(self.nc.alloc_semaphore(name))
        return self.used[-1]

    def recycle(self):
        self.nc.clear_and_free_semaphores(self.used)
        self.nc.all_engine_barrier()
        self.used = []

    def start_at_one(self, eng):
        for s in self.fresh:
            eng.sem_inc(s, 1)
        self.fresh = []


def linker(eng, sem, base=0):
    n = [0]

    def link(ins):
        n[0] += 1
        ins.then_inc(sem, 1)
        eng.wait_ge(sem, after(base + n[0]))
    return link


def root_step(k, pool, s_var, s_root):
    pool.wait_ge(s_var, after(1))
    k.nc.gpsimd.tensor_tensor(k.rstd[:], k.vare[:], k.half[:, 0:G], ALU.pow).then_inc(s_root, 1)


def finish_stats(k, link):
    v = k.nc.vector
    me, mo = k.stats[:, :, 1], k.stats[:, :, 4]
    ve, vo = k.stats[:, :, 2], k.stats[:, :, 5]
    a, b, c = k.tmp24[:, 0, :], k.tmp24[:, 1, :], k.tmp24[:, 2, :]
    link(v.tensor_tensor(a, me, mo, ALU.add))
    link(v.tensor_scalar(k.mean[:, :], a, 0.5, None, ALU.mult))
    link(v.tensor_tensor(b, me, mo, ALU.subtract))
    link(v.tensor_tensor(a, b, b, ALU.mult))
    link(v.tensor_tensor(c, ve, vo, ALU.add))
    link(v.tensor_scalar(b, c, 1.0 / C, None, ALU.mult))
    link(v.scalar_tensor_tensor(out=c, in0=a, scalar=0.25, in1=b, op0=ALU.mult, op1=ALU.add))
    return v.tensor_scalar(k.vare[:], c, EPS, None, ALU.add)


def stats_of_h(k, dve, s_link, s_var, s_root):
    finish_stats(k, linker(dve, s_link)).then_inc(s_var, 1)
    dve.wait_ge(s_root, after(1))


def tile_of(t, g):
    return t[:, g, :] if type(g) is int else t[:, ds(g, 1), :].rearrange("p a b -> p (a b)")


def column_of(t, g):
    return t[:, g:g + 1] if type(g) is int else t[:, ds(g, 1)]


def stepped(eng, tiles, step):
    step(0, 0, 0)
    step(1, 0, 1)
    with eng.Fori(1, tiles // 2 - 1) as i:
        step(i * 2, i, 0)
        step(i * 2 + 1, i, 1)
    for n in range(tiles // 2 * 2 - 2, tiles):
        step(n, n // 2, n % 2)


def known(n):
    return type(n) is int


def tokenizer(k):
    nc, d = k.nc, k.d
    with ExitStack() as ctx:
        sb = lambda n, s, dt=F32: k.sb(n, s, dt, ctx)
        ix0 = sb("ix0", [P, 2, 16], I32)
        ix12 = sb("ix12", [80, 16], I32)
        g0 = sb("g0", [P, 2, 16, 3 * B])
        g12 = sb("g12", [80, 16, 48 * B])
        c0 = sb("c0", [P, 2, 64])
        c1 = sb("c1", [64, 16, 12])
        c2 = sb("c2", [80, 16, 48])
        t0T = sb("t0T", [P, P])
        t1T = sb("t1T", [KT, 2, 64])
        t2T = sb("t2T", [P, 6, 16])
        w0T = sb("w0T", [P, 64])
        w1T = sb("w1T", [KT, 2, 64])
        w2T = sb("w2T", [P, 6, 64])
        wfT = sb("wfT", [64, 3, C])
        lb = sb("lb", [64, 3])
        bf = sb("bf", [P, C])
        up1 = sb("up1", [64, 256])
        up2 = sb("up2", [16, 256])
        o1 = sb("o1", [64, 64])
        o2 = sb("o2", [16, 64])
        yT = sb("yT", [64, 3, 256])
        zero = sb("zero", [P, C])
        pT0 = k.ps("pT0", [P, 512], ctx)
        pT1 = k.ps("pT1", [P, 512], ctx)
        pY = k.ps("pY", [P, 2, 512], ctx)
        pO = k.ps("pO", [P, 512], ctx)
        pU = k.ps("pU", [P, 512], ctx)
        pH = k.ps("pH", [P, 512], ctx)
        s_ix, s_w, s_id, s_c0 = (k.sem("t_" + n) for n in ("ix", "w", "id", "c0"))
        s_g = k.plain_sem("t_g")
        s_cut, s_tr, s_trs, s_lv, s_lvs, s_up, s_y, s_h, s_hs, s_z, s_st, s_off = (
            k.sem("t_" + n) for n in ("cut", "tr", "trs", "lv", "lvs", "up", "y", "h", "hs", "z", "st", "off"))
        block = ctx.enter_context(nc.Block())

        @block.sync
        def _(sp):
            k.start_at_one(sp)
            sp.dma_start(ix0[:], d["idx0"].rearrange("(t p j) -> p t j", t=2, j=16)).then_inc(s_ix, 16)
            sp.dma_start(ix12[0:64, :], d["idx1"].rearrange("(p j) -> p j", j=16)).then_inc(s_ix, 16)
            sp.dma_start(ix12[64:80, :], d["idx2"].rearrange("(p j) -> p j", j=16)).then_inc(s_ix, 16)
            for t, name in ((w0T, "w0T"), (w1T, "w1T"), (w2T, "w2T"), (wfT, "wfT"), (lb, "lb"),
                            (up1, "up1"), (up2, "up2")):
                sp.dma_start(t[:], d[name]).then_inc(s_w, 16)
            sp.dma_start(bf[:], d["bf"].broadcast_to([P, C])).then_inc(s_w, 16)
            sp.dma_start(k.h[:, :, :].rearrange("p (b t) c -> p b t c", t=NT)[:, :, 2, :],
                         d["txt"].rearrange("b p c -> p b c")).then_inc(s_w, 16)
            sp.wait_ge(s_z, after(1))
            for n in range(0, NX, 8):
                sp.dma_start(k.xs[n * P:(n + 8) * P, :].rearrange("(n p) c -> p n c", p=P),
                             zero[:, :].rearrange("p (a c) -> p a c", a=1).broadcast_to([P, 8, C])).then_inc(k.s_consts, 16)
            sp.wait_ge(s_w, after(16 * 9))

        @block.gpsimd
        def _(pool):
            nc.gpsimd.memset(k.ident[:], 0.0).then_inc(s_id, 1)
            nc.gpsimd.memset(k.half[:], -0.5)
            nc.gpsimd.memset(k.half2[:], 0.5)
            nc.gpsimd.memset(k.ones[:], 1.0).then_inc(s_id, 1)
            pool.wait_ge(s_id, after(2))
            nc.gpsimd.affine_select(out=k.ident[:], in_=k.ident[:], compare_op=ALU.not_equal, fill=1.0, base=0,
                                    pattern=[[-1, P]], channel_multiplier=1).then_inc(s_id, 1)
            pool.wait_ge(s_ix, after(48))
            pool.wait_ge(s_off, after(1))
            for j in range(16):
                for t in range(2):
                    nc.gpsimd.indirect_dma_start(g0[:, t, j, :], None, d["x0r"],
                                                 bass.IndirectOffsetOnAxis(ap=ix0[:, t, j:j + 1], axis=0)).then_inc(s_g, 16)
                nc.gpsimd.indirect_dma_start(g12[:, j, :], None, d["x12r"],
                                             bass.IndirectOffsetOnAxis(ap=ix12[:, j:j + 1], axis=0)).then_inc(s_g, 16)

        @block.vector
        def _(dve):
            dve.wait_ge(s_ix, after(48))
            nc.vector.tensor_scalar(ix12[64:80, :], ix12[64:80, :], 32 * 32, None, ALU.add).then_inc(s_off, 1)
            nc.vector.memset(zero[:], 0.0).then_inc(s_z, 1)
            nc.vector.memset(c0[:], 0.0).then_inc(s_c0, 1)
            dve.wait_ge(s_c0, after(1))
            dve.wait_ge(s_g, 48 * 16)
            dve.wait_ge(s_w, after(16 * 9))

            def cut(b):
                dve.wait_ge(s_tr, after(b))
                nc.vector.tensor_copy(c0[:, :, 0:48].rearrange("p t (j c) -> p t j c", c=3),
                                      g0[:, :, :, ds(b * 3, 3)])
                nc.vector.tensor_copy(c1[:], g12[0:64, :, ds(b * 12, 12)])
                nc.vector.tensor_copy(c2[64:80, :, :], g12[64:80, :, ds(b * 48, 48)]).then_inc(s_cut, 1)

            def step(b, last=False):
                if not last:
                    cut(b + 1)
                dve.wait_ge(s_h, after(b + 1))
                for t in range(2):
                    nc.vector.tensor_tensor(tile_of(k.h, b * NT + t), pH[:, t * C:(t + 1) * C], bf[:],
                                            ALU.add).then_inc(s_hs, 1)
                dve.wait_ge(s_hs, after(2 * b + 2))
                for t in range(NT):
                    nc.vector.bn_stats(tile_of(k.stats, b * NT + t), tile_of(k.h, b * NT + t)).then_inc(s_st, 1)

            cut(0)
            with dve.Fori(0, B - 1) as b:
                step(b)
            step(B - 1, True)
            dve.wait_ge(s_st, after(G))

        @block.tensor
        def _(pe):
            pe.wait_ge(s_id, after(3))
            pe.wait_ge(s_w, after(16 * 9))

            def turn(b):
                pe.wait_ge(s_cut, after(b + 1))
                pe.wait_ge(s_trs, after(3 * b))
                nc.tensor.transpose(pT0[:, 0:P], c0[:, :, :].rearrange("p t c -> p (t c)"), k.ident[:])
                for i in range(2):
                    nc.tensor.transpose(pT1[0:KT, i * 64:(i + 1) * 64],
                                        c1[:, i * 8:(i + 1) * 8, :].rearrange("p j c -> p (j c)"), k.ident[0:64, 0:64])
                flat2 = c2[64:80, :, :].rearrange("p j c -> p (j c)")
                for i in range(6):
                    last = nc.tensor.transpose(pT1[:, P + i * 16:P + (i + 1) * 16], flat2[:, i * P:(i + 1) * P],
                                               k.ident[64:80, 64:80])
                last.then_inc(s_tr, 1)

            def step(b, end=False):
                pe.wait_ge(s_trs, after(3 * b + 3))
                pe.wait_ge(s_y, after(5 * b))
                pe.wait_ge(s_lvs, after(2 * b))
                for i in range(6):
                    nc.tensor.matmul(pO[0:16, 64:128], t2T[:, i, :], w2T[:, i, :], start=i == 0, stop=i == 5)
                for i in range(2):
                    nc.tensor.matmul(pO[0:64, 0:64], t1T[:, i, :], w1T[:, i, :], start=i == 0, stop=i == 1)
                for t in range(2):
                    last = nc.tensor.matmul(pY[0:64, t, 0:P], w0T[64 * t:64 * t + 48, :], t0T[64 * t:64 * t + 48, :],
                                            start=True, stop=True)
                last.then_inc(s_lv, 1)
                pe.wait_ge(s_lvs, after(2 * b + 2))
                nc.tensor.matmul(pU[0:64, 256:512], o2[:], up2[:], start=True, stop=True)
                nc.tensor.matmul(pU[0:64, 0:256], o1[:], up1[:], start=True, stop=True).then_inc(s_up, 1)
                if not end:
                    turn(b + 1)
                pe.wait_ge(s_y, after(5 * b + 5))
                pe.wait_ge(s_hs, after(2 * b))
                for t in range(2):
                    for i in range(3):
                        last = nc.tensor.matmul(pH[:, t * C:(t + 1) * C], yT[:, i, t * P:(t + 1) * P], wfT[:, i, :],
                                                start=i == 0, stop=i == 2)
                last.then_inc(s_h, 1)

            turn(0)
            with pe.Fori(0, B - 1) as b:
                step(b)
            step(B - 1, True)

        @block.scalar
        def _(act):
            act.wait_ge(s_w, after(16 * 9))
            act.preload_act_table(ACT.Identity)

            def turned(b):
                act.wait_ge(s_tr, after(b + 1))
                act.wait_ge(s_lv, after(b))
                nc.scalar.activation(t0T[:], pT0[:, 0:P], ACT.Copy).then_inc(s_trs, 1)
                nc.scalar.activation(t1T[:].rearrange("p i t -> p (i t)"), pT1[0:KT, 0:128], ACT.Copy).then_inc(s_trs, 1)
                nc.scalar.activation(t2T[:].rearrange("p i t -> p (i t)"), pT1[:, 128:224], ACT.Copy).then_inc(s_trs, 1)

            def step(b, end=False):
                act.wait_ge(s_lv, after(b + 1))
                act.wait_ge(s_up, after(b))
                nc.scalar.activation(o1[:], pO[0:64, 0:64], ACT.Copy).then_inc(s_lvs, 1)
                nc.scalar.activation(o2[:], pO[0:16, 64:128], ACT.Copy).then_inc(s_lvs, 1)
                act.wait_ge(s_h, after(b))
                for t in range(2):
                    nc.scalar.activation(yT[:, 0, t * P:(t + 1) * P], pY[0:64, t, 0:P], ACT.Identity,
                                         bias=lb[:, 0:1]).then_inc(s_y, 1)
                act.wait_ge(s_up, after(b + 1))
                for i in (1, 2):
                    nc.scalar.activation(yT[:, i, :], pU[0:64, (i - 1) * 256:i * 256], ACT.Identity,
                                         bias=lb[:, i:i + 1]).then_inc(s_y, 1)
                act.wait_ge(s_y, after(5 * b + 4))
                act.sem_inc(s_y, 1)
                if not end:
                    turned(b + 1)

            turned(0)
            with act.Fori(0, B - 1) as b:
                step(b)
            step(B - 1, True)


def attention(k):
    nc, d = k.nc, k.d
    NU = NT * NH0
    with ExitStack() as ctx:
        sb = lambda n, s, dt=F32: k.sb(n, s, dt, ctx)
        wq = sb("wq", [KT, 2, 2, P])
        wk = sb("wk", [KT, 2, 2, P])
        wv = sb("wv", [KT, 2, C])
        wp = sb("wp", [P, 2, C])
        dsel = sb("dsel", [P, P])
        xn = sb("xn", [P, NT, C])
        xnT = sb("xnT", [KT, 2, NTOK])
        qT = sb("qT", [P, 2, NTOK])
        kz = sb("kz", [P, 2, 4, NTOK])
        va = sb("va", [P, NT, NH0, 32])
        mx = sb("mx", [P, NU])
        pm = sb("pm", [P, 2, 4, NTOK])
        pT = sb("pT", [P, NT, NH0, NTOK])
        oR = sb("oR", [P, 2, NTOK])
        rec = sb("rec", [P, 2, NTOK])
        oN = sb("oN", [P, 2, NTOK])
        S = k.ps("aS", [P, 4, 512], ctx)
        Gp = k.ps("aG", [P, 4, 512], ctx)
        names = ("w", "st", "lk", "var", "root", "pre", "xn", "xt", "xts", "q", "k", "v", "qs", "ks", "vs", "sc", "mx", "ex",
                 "pt", "pa", "pd", "pv", "or", "dn", "rc", "on", "pj", "hs")
        (s_w, s_st, s_lk, s_var, s_root, s_pre, s_xn, s_xt, s_xts, s_q, s_k, s_v, s_qs, s_ks, s_vs, s_sc, s_mx, s_ex,
         s_pt, s_pa, s_pd, s_pv, s_or, s_dn, s_rc, s_on, s_pj, s_hs) = (k.sem("a_" + n) for n in names)
        token_rows = lambda t: S[:, 2 + t // 2, (t % 2) * C:(t % 2 + 1) * C]
        block = ctx.enter_context(nc.Block())

        def evacuator(n, kt):
            on_act = kt == 1 or (kt == 2 and n % 2)
            order = [(m, t) for m in range(6) for t in range(NT) if (t == 1 or (t == 2 and m % 2)) == on_act]
            return on_act, order.index((n, kt)), len(order)

        @block.sync
        def _(sp):
            k.start_at_one(sp)
            for t, n in ((wq, "wq"), (wk, "wk"), (wv, "wv"), (wp, "wp"), (dsel, "dsel")):
                sp.dma_start(t[:], d[n]).then_inc(s_w, 16)
            sp.wait_ge(s_w, after(80))

        @block.gpsimd
        def _(pool):
            nc.gpsimd.memset(kz[:], 0.0).then_inc(s_pre, 1)
            nc.gpsimd.memset(va[:], 1.0).then_inc(s_pre, 1)
            root_step(k, pool, s_var, s_root)
            pool.wait_ge(s_pre, after(2))

        @block.vector
        def _(dve):
            v = nc.vector
            stats_of_h(k, dve, s_lk, s_var, s_root)
            dve.wait_ge(s_pre, after(2))

            def norm(b):
                dve.wait_ge(s_xt, after(b))
                for t in range(NT):
                    v.tensor_scalar(xn[:, t, :], tile_of(k.h, b * NT + t), column_of(k.mean, b * NT + t),
                                    column_of(k.rstd, b * NT + t), ALU.subtract, ALU.mult).then_inc(s_xn, 1)

            def turned(b):
                dve.wait_ge(s_xt, after(b + 1))
                v.tensor_copy(xnT[:, 1, :], Gp[0:KT, 1, 0:NTOK]).then_inc(s_xts, 1)

            def projected(b):
                dve.wait_ge(s_q, after(b + 1))
                for g in range(2):
                    v.tensor_scalar(qT[:, g, :], Gp[:, 2 + g, 0:NTOK], SCALE, None, ALU.mult).then_inc(s_qs, 1)
                dve.wait_ge(s_k, after(b + 1))
                for j in range(4):
                    v.tensor_copy(kz[32 * j:32 * j + 32, 1, j, :], Gp[32 * j:32 * j + 32, 1, 0:NTOK]).then_inc(s_ks, 1)
                dve.wait_ge(s_v, after(b + 1))
                v.tensor_copy(va[:, 0:2, :, 0:DH0],
                              S[:, 0, 0:2 * C].rearrange("p (t h c) -> p t h c", h=NH0, c=DH0)).then_inc(s_vs, 1)
                v.tensor_copy(va[:, 2, :, 0:DH0],
                              S[:, 1, 0:C].rearrange("p (h c) -> p h c", c=DH0)).then_inc(s_vs, 1)

            def batch(b, more):
                def maxima(n):
                    for j in range(4):
                        u = 4 * n + j
                        dve.wait_ge(s_sc, after(b * NU + u + 1))
                        v.tensor_reduce(mx[:, u:u + 1], S[:, j, 0:NTOK], AX.X, ALU.max, negate=True).then_inc(s_mx, 1)

                def keys(n):
                    for kt in range(NT):
                        if not evacuator(n, kt)[0]:
                            dve.wait_ge(s_pt, after(b * 18 + n * NT + kt + 1))
                            v.tensor_copy(pT[:, kt, 4 * (n % 2):4 * (n % 2) + 4, (n // 2) * P:(n // 2 + 1) * P],
                                          Gp[:, kt, :].rearrange("p (h t) -> p h t", t=P)).then_inc(s_pd, 1)
                maxima(0)
                for n in range(1, 6):
                    maxima(n)
                    keys(n - 1)
                keys(5)
                if more:
                    norm(b + 1)
                    turned(b + 1)
                for g in range(2):
                    dve.wait_ge(s_dn, after(b * 2 + g + 1))
                    v.reciprocal(rec[:, g, :], S[:, g, 0:NTOK]).then_inc(s_rc, 1)
                for g in range(2):
                    dve.wait_ge(s_rc, after(b * 2 + g + 1))
                    v.tensor_tensor(oN[:, g, :], oR[:, g, :], rec[:, g, :], ALU.mult).then_inc(s_on, 1)
                if more:
                    projected(b + 1)
                dve.wait_ge(s_pj, after(b * NT + NT))
                for t in range(NT):
                    v.tensor_tensor(tile_of(k.h, b * NT + t), tile_of(k.h, b * NT + t), token_rows(t),
                                    ALU.add).then_inc(s_hs, 1)
                dve.wait_ge(s_hs, after(b * NT + NT))
                for t in range(NT):
                    v.bn_stats(tile_of(k.stats, b * NT + t), tile_of(k.h, b * NT + t)).then_inc(s_st, 1)

            norm(0)
            turned(0)
            projected(0)
            with dve.Fori(0, B - 1) as b:
                batch(b, True)
            batch(B - 1, False)
            dve.wait_ge(s_st, after(G))

        @block.tensor
        def _(pe):
            mm = nc.tensor.matmul
            pe.wait_ge(s_w, after(80))

            def queries_keys(b):
                pe.wait_ge(s_xn, after(NT * b + NT))
                for i in range(2):
                    for t in range(NT):
                        last = nc.tensor.transpose(Gp[0:KT, i, t * P:(t + 1) * P], xn[:, t, i * KT:(i + 1) * KT], k.ident[:])
                last.then_inc(s_xt, 1)
                pe.wait_ge(s_xts, after(2 * b + 2))
                pe.wait_ge(s_or, after(2 * b))
                for g in range(2):
                    for i in range(2):
                        last = mm(Gp[:, 2 + g, 0:NTOK], wq[:, i, g, :], xnT[:, i, :], start=i == 0, stop=i == 1)
                last.then_inc(s_q, 1)
                for g in range(2):
                    for i in range(2):
                        last = mm(Gp[:, g, 0:NTOK], wk[:, i, g, :], xnT[:, i, :], start=i == 0, stop=i == 1)
                last.then_inc(s_k, 1)

            def values(b):
                pe.wait_ge(s_rc, after(2 * b))
                for t in range(NT):
                    for i in range(2):
                        last = mm(S[:, t // 2, (t % 2) * C:(t % 2 + 1) * C], xnT[:, i, t * P:(t + 1) * P], wv[:, i, :],
                                  start=i == 0, stop=i == 1)
                last.then_inc(s_v, 1)

            def batch(b, more):
                pe.wait_ge(s_qs, after(2 * b + 2))
                pe.wait_ge(s_ks, after(8 * b + 8))
                pe.wait_ge(s_vs, after(2 * b + 2))
                pe.wait_ge(s_hs, after(NT * b))

                def scores(n):
                    for j in range(4):
                        u = 4 * n + j
                        if n:
                            pe.wait_ge(s_ex, after(b * NU + u - 3))
                        mm(S[:, j, 0:NTOK], qT[:, n % 2, (n // 2) * P:(n // 2 + 1) * P], kz[:, n % 2, j, :],
                           start=True, stop=True).then_inc(s_sc, 1)

                def turn(n):
                    pe.wait_ge(s_ex, after(b * NU + 4 * n + 4))
                    for kt in range(NT):
                        if n:
                            on_act, at, of = evacuator(n - 1, kt)
                            pe.wait_ge(s_pa if on_act else s_pd, after(b * of + at + 1))
                        for j in range(4):
                            last = nc.tensor.transpose(Gp[:, kt, j * P:(j + 1) * P], pm[:, n % 2, j, kt * P:(kt + 1) * P], k.ident[:])
                        last.then_inc(s_pt, 1)
                scores(0)
                for n in range(1, 6):
                    scores(n)
                    turn(n - 1)
                turn(5)
                pe.wait_ge(s_pa, after(b * 9 + 9))
                pe.wait_ge(s_pd, after(b * 9 + 9))
                for g in range(2):
                    for j in range(4):
                        for kt in range(NT):
                            last = mm(Gp[32 * j:32 * j + 32, 2 + g, 0:NTOK], va[:, kt, 4 * g + j, :], pT[:, kt, 4 * g + j, :],
                                      start=kt == 0, stop=kt == NT - 1)
                    last.then_inc(s_pv, 1)
                for g in range(2):
                    pe.wait_ge(s_or, after(2 * b + g + 1))
                    mm(S[:, g, 0:NTOK], dsel[:], oR[:, g, :], start=True, stop=True).then_inc(s_dn, 1)
                if more:
                    queries_keys(b + 1)
                pe.wait_ge(s_on, after(2 * b + 2))
                for t in range(NT):
                    for g in range(2):
                        last = mm(token_rows(t), oN[:, g, t * P:(t + 1) * P], wp[:, g, :], start=g == 0, stop=g == 1)
                    last.then_inc(s_pj, 1)
                if more:
                    values(b + 1)

            queries_keys(0)
            values(0)
            with pe.Fori(0, B - 1) as b:
                batch(b, True)
            batch(B - 1, False)

        @block.scalar
        def _(act):
            A = nc.scalar.activation
            act.preload_act_table(ACT.Exp)
            act.wait_ge(s_pre, after(2))

            def turned(b):
                act.wait_ge(s_xt, after(b + 1))
                A(xnT[:, 0, :], Gp[0:KT, 0, 0:NTOK], ACT.Copy).then_inc(s_xts, 1)

            def projected(b):
                act.wait_ge(s_k, after(b + 1))
                for j in range(4):
                    A(kz[32 * j:32 * j + 32, 0, j, :], Gp[32 * j:32 * j + 32, 0, 0:NTOK], ACT.Copy).then_inc(s_ks, 1)

            def batch(b, more):
                def exps(n):
                    if n >= 2:
                        act.wait_ge(s_pt, after(b * 18 + (n - 2) * NT + NT))
                    for j in range(4):
                        u = 4 * n + j
                        act.wait_ge(s_mx, after(b * NU + u + 1))
                        A(pm[:, n % 2, j, :], S[:, j, 0:NTOK], ACT.Exp, bias=mx[:, u:u + 1]).then_inc(s_ex, 1)

                def keys(n):
                    for kt in range(NT):
                        if evacuator(n, kt)[0]:
                            act.wait_ge(s_pt, after(b * 18 + n * NT + kt + 1))
                            A(pT[:, kt, 4 * (n % 2):4 * (n % 2) + 4, (n // 2) * P:(n // 2 + 1) * P],
                              Gp[:, kt, :].rearrange("p (h t) -> p h t", t=P), ACT.Copy).then_inc(s_pa, 1)
                exps(0)
                for n in range(1, 6):
                    exps(n)
                    keys(n - 1)
                keys(5)
                for g in range(2):
                    act.wait_ge(s_pv, after(b * 2 + g + 1))
                    A(oR[:, g, :], Gp[:, 2 + g, 0:NTOK], ACT.Copy).then_inc(s_or, 1)
                if more:
                    turned(b + 1)
                    projected(b + 1)

            turned(0)
            projected(0)
            with act.Fori(0, B - 1) as b:
                batch(b, True)
            batch(B - 1, False)


def route(k, tag, top, ntiles, gw, gb):
    nc, d = k.nc, k.d
    NC = top
    with ExitStack() as ctx:
        sb = lambda n, s, dt=F32: k.sb(tag + n, s, dt, ctx)
        w = sb("w", [KT, 2, E])
        bias = sb("bias", [P, E])
        tri = sb("tri", [P, P])
        rank8 = sb("rank8", [P, E])
        seg = sb("seg", [P, E, NC * G])
        starts = sb("starts", [1, ntiles])
        xb = sb("xb", [P, 2, 4, C])
        xT = sb("xT", [KT, 2, 2, 4 * P])
        lg = sb("lg", [P, G, E])
        pr = sb("pr", [P, G, E])
        key = sb("key", [P, G, E])
        oh = sb("oh", [P, E, NC, G])
        m1 = sb("m1", [P, 3, G])
        tot = sb("tot", [P, E, NC, G])
        inc = sb("inc", [P, E, NC, G])
        ne = sb("ne", [P, 3, E])
        nei = sb("nei", [P, E], I32)
        ends = sb("ends", [P, E])
        posf = sb("posf", [P, NC, G])
        cmp = sb("cmp", [1, ntiles, E])
        eidf = sb("eidf", [1, ntiles])
        xo = sb("xo", [P, G, C])
        pX = k.ps(tag + "pX", [P, 2, 2, 512], ctx)
        pL = k.ps(tag + "pL", [P, 2, 512], ctx)
        rounds = G // 4
        pC = k.ps(tag + "pC", [P, 512], ctx)
        pS = k.ps(tag + "pS", [P, 512], ctx)
        s_w, s_c, s_lk, s_xb, s_xo, s_xt, s_xts, s_l, s_ls, s_d, s_oh, s_cnt, s_pos = (
            k.sem(tag + n) for n in ("w", "c", "lk", "xb", "xo", "xt", "xts", "l", "ls", "d", "oh", "cnt", "pos"))
        s_sc = k.plain_sem(tag + "sc")
        s_var, s_root = k.sem(tag + "var"), k.sem(tag + "root")
        block = ctx.enter_context(nc.Block())

        def per_tile(t):
            return t.rearrange("p (g a) -> p g a", a=1).broadcast_to([P, G, E])

        @block.sync
        def _(sp):
            k.start_at_one(sp)
            for t, n in ((w, gw), (tri, "tri"), (rank8, "rank8")):
                sp.dma_start(t[:], d[n]).then_inc(s_w, 16)
            sp.dma_start(bias[:], d[gb].broadcast_to([P, E])).then_inc(s_w, 16)
            sp.dma_start(starts[:], d["starts"][:, 0:ntiles]).then_inc(s_w, 16)
            if top == 2:
                k.w0.load(sp, d)
            sp.wait_ge(s_w, after(80))

        @block.gpsimd
        def _(pool):
            nc.gpsimd.memset(seg[:], 1.0).then_inc(s_c, 1)
            pool.wait_ge(s_c, after(1))
            nc.gpsimd.memset(seg[:, :, 0:1], 0.0).then_inc(s_c, 1)
            root_step(k, pool, s_var, s_root)
            pool.wait_ge(s_pos, after(1))
            pool.wait_ge(s_xo, after(G))
            if top == 2:
                pool.wait_ge(k.s_consts, after(16 * (NX // 8)))
            for g in range(G):
                for c in range(NC):
                    nc.gpsimd.indirect_dma_start(k.xs, bass.IndirectOffsetOnAxis(ap=k.pos[:, c, g:g + 1], axis=0),
                                                 xo[:, g, :], None).then_inc(s_sc, 16)
            pool.wait_ge(s_sc, 16 * NC * G)

        @block.vector
        def _(dve):
            v = nc.vector
            stats_of_h(k, dve, s_lk, s_var, s_root)
            dve.wait_ge(s_w, after(80))
            dve.wait_ge(s_c, after(2))

            def norm(i, s):
                if not known(i) or i > 1:
                    dve.wait_ge(s_xt, after(i - 1))
                for x_, s_ in ((xb, s_xb), (xo, s_xo)):
                    for t in range(4):
                        g = i * 4 + t
                        v.tensor_scalar(xb[:, s, t, :] if x_ is xb else tile_of(xo, g), tile_of(k.h, g),
                                        column_of(k.mean, g), column_of(k.rstd, g), ALU.subtract, ALU.mult).then_inc(s_, 1)

            def step(i, uses, s):
                if not (known(i) and i >= rounds - 2):
                    norm(i + 2, s)
                dve.wait_ge(s_l, after(i + 1))
                four = lg[:, i * 4:i * 4 + 4, :] if known(i) else lg[:, ds(i * 4, 4), :]
                v.tensor_copy(four, pL[:, s, 0:4 * E].rearrange("p (t e) -> p t e", e=E)).then_inc(s_ls, 1)

            norm(0, 0)
            norm(1, 1)
            stepped(dve, rounds, step)
            dve.wait_ge(s_ls, after(rounds))
            link = linker(dve, s_d)
            link(v.tensor_tensor(lg[:], lg[:], bias[:, :].rearrange("p (a e) -> p a e", a=1).broadcast_to([P, G, E]), ALU.add))
            link(v.tensor_reduce(m1[:, 0, :], lg[:], AX.X, ALU.max))
            link(v.tensor_tensor(pr[:], lg[:], per_tile(m1[:, 0, :]), ALU.subtract))
            dve.sem_inc(s_oh, 1)
            dve.wait_ge(s_cnt, after(1))
            link(v.tensor_reduce(m1[:, 1, :], pr[:], AX.X, ALU.add))
            link(v.reciprocal(m1[:, 2, :], m1[:, 1, :]))
            link(v.tensor_tensor(pr[:], pr[:], per_tile(m1[:, 2, :]), ALU.mult))
            rank_b = rank8[:, :].rearrange("p (a e) -> p a e", a=1).broadcast_to([P, G, E])
            for c in range(NC):
                link(v.tensor_reduce(k.wtop[:, c, :], pr[:], AX.X, ALU.max))
                link(v.tensor_tensor(key[:], pr[:], per_tile(k.wtop[:, c, :]), ALU.is_equal))
                link(v.tensor_tensor(key[:], key[:], rank_b, ALU.mult))
                link(v.tensor_reduce(m1[:, 0, :], key[:], AX.X, ALU.max))
                ohc = oh[:, :, c, :].rearrange("p e g -> p g e")
                link(v.tensor_tensor(ohc, key[:], per_tile(m1[:, 0, :]), ALU.is_equal))
                if c + 1 < NC:
                    link(v.tensor_tensor(pr[:], pr[:], ohc, ALU.subtract))
            if NC == 2:
                link(v.tensor_tensor(m1[:, 0, :], k.wtop[:, 0, :], k.wtop[:, 1, :], ALU.add))
                link(v.reciprocal(m1[:, 1, :], m1[:, 0, :]))
                for c in range(2):
                    link(v.tensor_tensor(k.wtop[:, c, :], k.wtop[:, c, :], m1[:, 1, :], ALU.mult))
            dve.sem_inc(s_oh, 1)
            dve.wait_ge(s_cnt, after(2))
            n = E * NC * G
            flat = lambda t: t[:].rearrange("p e c g -> p (e c g)")
            link(v.tensor_copy(flat(tot), pS[:, 0:n]))
            link(v.tensor_tensor_scan(flat(inc), seg[:].rearrange("p e n -> p (e n)"), flat(tot), 0.0, ALU.mult, ALU.add))
            last = inc[:, :, NC - 1, G - 1]
            link(v.tensor_scalar(ne[:, 0, :], last, float(P - 1), None, ALU.add))
            link(v.tensor_copy(nei[:], ne[:, 0, :]))
            link(v.tensor_scalar(nei[:], nei[:], -P, None, ALU.bitwise_and))
            link(v.tensor_copy(ne[:, 2, :], nei[:]))
            link(v.tensor_tensor_scan(ends[:], k.ones[:, 0:E], ne[:, 2, :], 0.0, ALU.mult, ALU.add))
            link(v.tensor_tensor(ne[:, 0, :], ends[:], ne[:, 2, :], ALU.subtract))
            link(v.tensor_tensor(flat(inc), flat(inc), flat(tot), ALU.subtract))
            link(v.tensor_tensor(flat(inc), flat(inc), pC[:, 0:n], ALU.add))
            link(v.tensor_tensor(inc[:].rearrange("p e c g -> p e (c g)"), inc[:].rearrange("p e c g -> p e (c g)"),
                                 ne[:, 0, :].rearrange("p (e a) -> p e a", a=1).broadcast_to([P, E, NC * G]), ALU.add))
            link(v.tensor_tensor(flat(inc), flat(inc), flat(oh), ALU.mult))
            link(v.tensor_reduce(posf[:].rearrange("p c g -> p (c g)"), inc[:].rearrange("p e c g -> p (c g) e"),
                                 AX.X, ALU.add))
            link(v.tensor_copy(k.pos[:, 0:NC, :], posf[:]))
            dve.sem_inc(s_pos, 1)
            link(v.tensor_tensor(cmp[:], ends[0:1, :].rearrange("p (a e) -> p a e", a=1).broadcast_to([1, ntiles, E]),
                                 starts[:, :].rearrange("p (n a) -> p n a", a=1).broadcast_to([1, ntiles, E]), ALU.is_le))
            link(v.tensor_reduce(eidf[:], cmp[:], AX.X, ALU.add))
            link(v.tensor_scalar(eidf[:], eidf[:], float(E - 1), None, ALU.min))
            link(v.tensor_copy(k.eid[:, 0:ntiles], eidf[:]))

        @block.tensor
        def _(pe):
            pe.wait_ge(s_w, after(80))

            def turn(i, s):
                pe.wait_ge(s_xb, after(i * 4 + 4))
                if not known(i) or i > 1:
                    pe.wait_ge(s_xts, after(i - 1))
                for t in range(4):
                    for c in range(2):
                        last = nc.tensor.transpose(pX[0:KT, s, c, t * P:(t + 1) * P], xb[:, s, t, c * KT:(c + 1) * KT], k.ident[:])
                last.then_inc(s_xt, 1)

            def step(i, uses, s):
                pe.wait_ge(s_xts, after(i + 1))
                if not known(i) or i > 1:
                    pe.wait_ge(s_ls, after(i - 1))
                for t in range(4):
                    for c in range(2):
                        last = nc.tensor.matmul(pL[:, s, t * E:(t + 1) * E], xT[:, s, c, t * P:(t + 1) * P], w[:, c, :],
                                                start=c == 0, stop=c == 1)
                last.then_inc(s_l, 1)
                if not (known(i) and i >= rounds - 2):
                    turn(i + 2, s)

            turn(0, 0)
            turn(1, 1)
            stepped(pe, rounds, step)
            pe.wait_ge(s_oh, after(2))
            n = E * NC * G
            oh_flat = oh[:].rearrange("p e c g -> p (e c g)")
            nc.tensor.matmul(pC[:, 0:n], tri[:], oh_flat, start=True, stop=True)
            nc.tensor.matmul(pS[:, 0:n], k.ones[:], oh_flat, start=True, stop=True).then_inc(s_cnt, 1)

        @block.scalar
        def _(act):
            def turned(i, s):
                act.wait_ge(s_xt, after(i + 1))
                nc.scalar.activation(xT[:, s, :, :], pX[0:KT, s, :, :], ACT.Copy).then_inc(s_xts, 1)

            def step(i, uses, s):
                act.wait_ge(s_l, after(i + 1))
                if not (known(i) and i >= rounds - 2):
                    turned(i + 2, s)

            turned(0, 0)
            turned(1, 1)
            stepped(act, rounds, step)
            act.wait_ge(s_oh, after(1))
            nc.scalar.activation(pr[:].rearrange("p g e -> p (g e)"), pr[:].rearrange("p g e -> p (g e)"),
                                 ACT.Exp).then_inc(s_cnt, 1)


def load_rows(sp, x, src, s_x, s_used, tiles):
    def load(n, s):
        sp.dma_start(x[:, s, :], rows_of(src, n)).then_inc(s_x[s], 16)

    load(0, 0)
    load(1, 1)
    with sp.Fori(0, tiles // 2 - 1) as i:
        for s in range(2):
            sp.wait_ge(s_used, after(i * 2 + s + 1))
            load(i * 2 + s + 2, s)
    if tiles % 2:
        sp.wait_ge(s_used, after(tiles - 2))
        load(tiles - 1, 0)


def rows_of(t, n):
    return t[n * P:(n + 1) * P, :] if type(n) is int else t[ds(n * P, P), :]


class Weights0:

    def __init__(self, k, ctx):
        NM = F0 // P
        self.w1 = k.sb("e_w1", [KT + 1, 2, E, F0], F32, ctx)
        self.w2 = k.sb("e_w2", [P, E, NM, C], F32, ctx)
        self.b2 = k.sb("e_b2", [P, E, C], F32, ctx)
        self.loaded = k.sem("e_w")
        self.count = 16 * (2 * E + 1)

    def load(self, eng, d):
        eng.dma_start(self.b2[:], d["e0b2"].broadcast_to([P, E, C])).then_inc(self.loaded, 16)
        for e in range(E):
            eng.dma_start(self.w1[:, :, e, :], d["e0w1"][:, :, e, :]).then_inc(self.loaded, 16)
            eng.dma_start(self.w2[:, e, :, :], d["e0w2"][:, e, :, :]).then_inc(self.loaded, 16)


def experts0(k):
    nc, d = k.nc, k.d
    NM = F0 // P
    HF = F0 // 2
    with ExitStack() as ctx:
        sb = lambda n, s, dt=F32: k.sb(n, s, dt, ctx)
        w1, w2, b2 = k.w0.w1, k.w0.w2, k.w0.b2
        x = sb("e_x", [P, 2, C])
        xT = sb("e_xT", [KT + 1, 2, 2, P])
        hb = sb("e_h", [P, 2, 2, HF])
        hT = sb("e_hT", [P, 2, NM, P])
        y = sb("e_y", [P, 2, C])
        pX = k.ps("e_pX", [P, 512], ctx)
        pH = k.ps("e_pH", [P, 2, 2, 512], ctx)
        pT = k.ps("e_pT", [P, 2, 512], ctx)
        pY = k.ps("e_pY", [P, 512], ctx)
        s_on, s_xt, s_xts, s_h, s_hs, s_ht, s_hts, s_y, s_ys = (
            k.sem("e_" + n) for n in ("on", "xt", "xts", "h", "hs", "ht", "hts", "y", "ys"))
        s_x = [k.sem(f"e_x{i}") for i in range(2)]
        s_st = [k.sem(f"e_st{i}") for i in range(2)]
        block = ctx.enter_context(nc.Block())

        @block.sync
        def _(sp):
            k.start_at_one(sp)
            load_rows(sp, x, k.xs, s_x, s_xt, N0)
            for i, s in enumerate(s_st):
                sp.wait_ge(s, after(16 * ((N0 + 1 - i) // 2)))

        @block.tensor
        def _(pe):
            pe.wait_ge(k.w0.loaded, after(k.w0.count))
            pe.wait_ge(s_on, after(1))

            def expert(n):
                return pe.value_load(k.eid[0:1, ds(n, 1)], min_val=0, max_val=E - 1)

            def rows(n, uses, s):
                pe.wait_ge(s_x[s], after(uses * 16 + 16))
                for c in range(2):
                    last = nc.tensor.transpose(pX[0:KT, c * P:(c + 1) * P], x[:, s, c * KT:(c + 1) * KT], k.ident[:])
                last.then_inc(s_xt, 1)

            def output(n, s):
                e = expert(n)
                pe.wait_ge(s_hts, after(n + 1))
                pe.wait_ge(s_ys, after(n))
                for m in range(NM):
                    last = nc.tensor.matmul(pY[:, 0:C], hT[:, s, m, :], w2[:, ds(e, 1), m, :].rearrange("p a c -> p (a c)"),
                                            start=m == 0, stop=m == NM - 1)
                last.then_inc(s_y, 1)

            def step(n, uses, s):
                e = expert(n)
                pe.wait_ge(s_xts, after(n + 1))
                if not known(n) or n > 1:
                    pe.wait_ge(s_hs, after(n - 1))
                for c in range(2):
                    for f in range(2):
                        last = nc.tensor.matmul(pH[:, s, f, 0:HF], xT[0:KT + c, s, c, :],
                                                w1[0:KT + c, c, ds(e, 1), f * HF:(f + 1) * HF].rearrange("p a f -> p (a f)"),
                                                start=c == 0, stop=c == 1)
                last.then_inc(s_h, 1)
                if not (known(n) and n == N0 - 1):
                    rows(n + 1, uses + s, 1 - s)
                if not (known(n) and n == 0):
                    output(n - 1, 1 - s)
                pe.wait_ge(s_hs, after(n + 1))
                for m in range(NM):
                    last = nc.tensor.transpose(pT[:, m // 3, (m % 3) * P:(m % 3 + 1) * P],
                                               hb[:, s, m // 3, (m % 3) * P:(m % 3 + 1) * P], k.ident[:])
                last.then_inc(s_ht, 1)

            rows(0, 0, 0)
            stepped(pe, N0, step)
            output(N0 - 1, (N0 - 1) % 2)

        @block.scalar
        def _(act):
            act.preload_act_table(ACT.Gelu)

            def step(n, uses, s):
                act.wait_ge(s_h, after(n + 1))
                if not known(n) or n > 1:
                    act.wait_ge(s_ht, after(n - 1))
                nc.scalar.activation(hb[:, s, :, :], pH[:, s, :, 0:HF], ACT.Gelu).then_inc(s_hs, 1)
                if not (known(n) and n == 0):
                    store(n - 1, 1 - s)

            def store(n, s):
                act.wait_ge(s_ys, after(n + 1))
                act.dma_start(rows_of(k.ys, n), y[:, s, :]).then_inc(s_st[s], 16)

            stepped(act, N0, step)
            store(N0 - 1, (N0 - 1) % 2)

        @block.vector
        def _(dve):
            nc.vector.memset(xT[KT:KT + 1, :, :, :], 1.0).then_inc(s_on, 1)
            dve.wait_ge(k.w0.loaded, after(k.w0.count))

            def rows(n, s):
                dve.wait_ge(s_xt, after(n + 1))
                nc.vector.tensor_copy(xT[0:KT, s, :, :],
                                      pX[0:KT, 0:2 * P].rearrange("p (c t) -> p c t", c=2)).then_inc(s_xts, 1)

            def output(n, uses, s):
                e = dve.value_load(k.eid[0:1, ds(n, 1)], min_val=0, max_val=E - 1)
                dve.wait_ge(s_y, after(n + 1))
                dve.wait_ge(s_st[s], after(uses * 16))
                nc.vector.tensor_tensor(y[:, s, :], pY[:, 0:C], b2[:, ds(e, 1), :].rearrange("p a c -> p (a c)"),
                                        ALU.add).then_inc(s_ys, 1)

            def step(n, uses, s):
                if not (known(n) and n == N0 - 1):
                    rows(n + 1, 1 - s)
                if not (known(n) and n == 0):
                    output(n - 1, uses - 1 + s, 1 - s)
                dve.wait_ge(s_ht, after(n + 1))
                nc.vector.tensor_copy(hT[:, s, :, :].rearrange("p (a m) t -> p a (m t)", a=2),
                                      pT[:, :, 0:3 * P]).then_inc(s_hts, 1)

            rows(0, 0)
            stepped(dve, N0, step)
            output(N0 - 1, (N0 - 1) // 2, (N0 - 1) % 2)


RUN = 4


def gather_rows(k, ya, src, s_g, top):
    for g in range(G):
        for c in range(top):
            k.nc.gpsimd.indirect_dma_start(ya[:, g, c, :], None, src,
                                           bass.IndirectOffsetOnAxis(ap=k.pos[:, c, g:g + 1], axis=0)).then_inc(s_g[g // RUN], 16)


def combine0(k):
    nc = k.nc
    with ExitStack() as ctx:
        ya = k.sb("cb_y", [P, G, 2, C], F32, ctx)
        s_a, s_h, s_st, s_lk, s_var, s_root = (k.sem("cb_" + n) for n in ("a", "h", "st", "lk", "var", "root"))
        s_g = [k.plain_sem(f"cb_g{i}") for i in range(G // RUN)]
        block = ctx.enter_context(nc.Block())

        @block.sync
        def _(sp):
            k.start_at_one(sp)
            k.mw.load(sp, k.d)

        @block.gpsimd
        def _(pool):
            gather_rows(k, ya, k.ys, s_g, 2)
            pool.wait_ge(s_var, after(1))
            nc.gpsimd.tensor_tensor(k.rstd12[:], k.tmp24[:, 0, :], k.half[:, 0:G], ALU.pow).then_inc(s_root, 1)
            pool.wait_ge(s_root, after(1))

        @block.scalar
        def _(act):
            k.mw.exponentials(act)

        @block.vector
        def _(dve):
            k.mw.prepare(dve)
            for r in range(G // RUN):
                dve.wait_ge(s_g[r], 16 * 2 * RUN)
                for c in range(2):
                    if c:
                        dve.wait_ge(s_a, after((r + 1) * RUN))
                    for g in range(r * RUN, (r + 1) * RUN):
                        nc.vector.scalar_tensor_tensor(out=k.h[:, g, :], in0=ya[:, g, c, :], scalar=k.wtop[:, c, g:g + 1],
                                                       in1=k.h[:, g, :], op0=ALU.mult, op1=ALU.add).then_inc(s_h if c else s_a, 1)
                dve.wait_ge(s_h, after((r + 1) * RUN))
                for g in range(r * RUN, (r + 1) * RUN):
                    nc.vector.bn_stats(k.stats[:, g, :], k.h[:, g, :]).then_inc(s_st, 1)
            dve.wait_ge(s_st, after(G))
            link = linker(dve, s_lk)
            link(finish_stats(k, link))
            nc.vector.scalar_tensor_tensor(out=k.tmp24[:, 0, :], in0=k.vare[:], scalar=EPS, in1=k.tmp24[:, 2, :],
                                           op0=ALU.mult, op1=ALU.add).then_inc(s_var, 1)


class Weights1:

    def __init__(self, k, ctx):
        self.w1 = k.sb("f_w1", [KT, 2, E, F1], F32, ctx)
        self.w2 = k.sb("f_w2", [KT, 2, E, F1], F32, ctx)
        self.w3 = k.sb("f_w3", [P, E, F1 // P, C], F32, ctx)
        self.loaded = k.sem("f_w")
        self.count = 16 * 3 * E

    def load(self, eng, d):
        for e in range(E):
            eng.dma_start(self.w1[:, :, e, :], d["e1w1"][:, :, e, :]).then_inc(self.loaded, 16)
            eng.dma_start(self.w2[:, :, e, :], d["e1w2"][:, :, e, :]).then_inc(self.loaded, 16)
            eng.dma_start(self.w3[:, e, :, :], d["e1w3"][:, e, :, :]).then_inc(self.loaded, 16)


def experts1(k):
    nc, d = k.nc, k.d
    NM = F1 // P
    with ExitStack() as ctx:
        sb = lambda n, s, dt=F32: k.sb(n, s, dt, ctx)
        w1, w2, w3 = k.w1.w1, k.w1.w2, k.w1.w3
        x = sb("f_x", [P, 2, C])
        xT = sb("f_xT", [KT, 2, 2, P])
        sl = sb("f_sl", [P, 2, F1])
        hb = sb("f_h", [P, 2, F1])
        hT = sb("f_hT", [P, 2, NM, P])
        y = sb("f_y", [P, 2, C], BF16)
        pX = k.ps("f_pX", [P, 512], ctx)
        pA = k.ps("f_pA", [P, 2, 512], ctx)
        pB = k.ps("f_pB", [P, 2, 512], ctx)
        pT = k.ps("f_pT", [P, 512], ctx)
        pY = k.ps("f_pY", [P, 512], ctx)
        s_xt, s_xts, s_h, s_sl, s_hs, s_ht, s_hts, s_y, s_ys = (
            k.sem("f_" + n) for n in ("xt", "xts", "h", "sl", "hs", "ht", "hts", "y", "ys"))
        s_x = [k.sem(f"f_x{i}") for i in range(2)]
        s_st = [k.sem(f"f_st{i}") for i in range(2)]
        block = ctx.enter_context(nc.Block())

        @block.sync
        def _(sp):
            k.start_at_one(sp)
            load_rows(sp, x, k.xs, s_x, s_xt, N1)
            for i, s in enumerate(s_st):
                sp.wait_ge(s, after(16 * ((N1 + 1 - i) // 2)))

        @block.tensor
        def _(pe):
            pe.wait_ge(k.w1.loaded, after(k.w1.count))

            def expert(n):
                return pe.value_load(k.eid[0:1, ds(n, 1)], min_val=0, max_val=E - 1)

            def rows(n, uses, s):
                pe.wait_ge(s_x[s], after(uses * 16 + 16))
                for c in range(2):
                    last = nc.tensor.transpose(pX[0:KT, c * P:(c + 1) * P], x[:, s, c * KT:(c + 1) * KT], k.ident[:])
                last.then_inc(s_xt, 1)

            def output(n, s):
                e = expert(n)
                pe.wait_ge(s_hts, after(n + 1))
                pe.wait_ge(s_ys, after(n))
                for m in range(NM):
                    last = nc.tensor.matmul(pY[:, 0:C], hT[:, s, m, :], w3[:, ds(e, 1), m, :].rearrange("p a c -> p (a c)"),
                                            start=m == 0, stop=m == NM - 1)
                last.then_inc(s_y, 1)

            def step(n, uses, s):
                e = expert(n)
                pe.wait_ge(s_xts, after(n + 1))
                if not known(n) or n > 1:
                    pe.wait_ge(s_hs, after(n - 1))
                for p, w in ((pA, w1), (pB, w2)):
                    for c in range(2):
                        last = nc.tensor.matmul(p[:, s, :], xT[:, s, c, :],
                                                w[:, c, ds(e, 1), :].rearrange("p a f -> p (a f)"),
                                                start=c == 0, stop=c == 1)
                    last.then_inc(s_h, 1)
                if not (known(n) and n == N1 - 1):
                    rows(n + 1, uses + s, 1 - s)
                if not (known(n) and n == 0):
                    output(n - 1, 1 - s)
                pe.wait_ge(s_hs, after(n + 1))
                for m in range(NM):
                    last = nc.tensor.transpose(pT[:, m * P:(m + 1) * P], hb[:, s, m * P:(m + 1) * P], k.ident[:])
                last.then_inc(s_ht, 1)

            rows(0, 0, 0)
            stepped(pe, N1, step)
            output(N1 - 1, (N1 - 1) % 2)

        @block.scalar
        def _(act):
            act.preload_act_table(ACT.Silu)

            def step(n, uses, s):
                act.wait_ge(s_h, after(n * 2 + 1))
                if not known(n) or n > 1:
                    act.wait_ge(s_hs, after(n - 1))
                nc.scalar.activation(sl[:, s, :], pA[:, s, :], ACT.Silu).then_inc(s_sl, 1)
                act.wait_ge(s_ht, after(n + 1))
                nc.scalar.activation(hT[:, s, :, :].rearrange("p m t -> p (m t)"), pT[:, :], ACT.Copy).then_inc(s_hts, 1)
                if not (known(n) and n == 0):
                    store(n - 1, 1 - s)

            def store(n, s):
                act.wait_ge(s_ys, after(n + 1))
                act.dma_start(rows_of(k.ys1, n), y[:, s, :]).then_inc(s_st[s], 16)

            stepped(act, N1, step)
            store(N1 - 1, (N1 - 1) % 2)

        @block.vector
        def _(dve):
            def rows(n, s):
                dve.wait_ge(s_xt, after(n + 1))
                nc.vector.tensor_copy(xT[:, s, :, :],
                                      pX[0:KT, 0:2 * P].rearrange("p (c t) -> p c t", c=2)).then_inc(s_xts, 1)

            def output(n, uses, s):
                dve.wait_ge(s_y, after(n + 1))
                dve.wait_ge(s_st[s], after(uses * 16))
                nc.vector.tensor_copy(y[:, s, :], pY[:, 0:C]).then_inc(s_ys, 1)

            def step(n, uses, s):
                dve.wait_ge(s_h, after(n * 2 + 2))
                dve.wait_ge(s_sl, after(n + 1))
                if not known(n) or n > 1:
                    dve.wait_ge(s_ht, after(n - 1))
                nc.vector.tensor_tensor(hb[:, s, :], pB[:, s, :], sl[:, s, :], ALU.mult).then_inc(s_hs, 1)
                if not (known(n) and n == N1 - 1):
                    rows(n + 1, 1 - s)
                if not (known(n) and n == 0):
                    output(n - 1, uses - 1 + s, 1 - s)

            rows(0, 0)
            stepped(dve, N1, step)
            output(N1 - 1, (N1 - 1) // 2, (N1 - 1) % 2)


def finish(k):
    nc, d = k.nc, k.d
    with ExitStack() as ctx:
        ya = k.sb("fi_y", [P, G, 1, C], BF16, ctx)
        s_h, s_o = k.sem("fi_h"), k.sem("fi_o")
        s_g = [k.plain_sem(f"fi_g{i}") for i in range(G // RUN)]
        block = ctx.enter_context(nc.Block())

        @block.gpsimd
        def _(pool):
            gather_rows(k, ya, k.ys1, s_g, 1)

        @block.vector
        def _(dve):
            for r in range(G // RUN):
                dve.wait_ge(s_g[r], 16 * RUN)
                for g in range(r * RUN, (r + 1) * RUN):
                    nc.vector.scalar_tensor_tensor(out=k.h[:, g, :], in0=ya[:, g, 0, :], scalar=k.wtop[:, 0, g:g + 1],
                                                   in1=k.h[:, g, :], op0=ALU.mult, op1=ALU.add).then_inc(s_h, 1)

        @block.sync
        def _(sp):
            k.start_at_one(sp)
            store_result(sp, k, s_o, lambda b: sp.wait_ge(s_h, after(b * NT + NT)))


def store_result(sp, k, s_o, ready=lambda b: None):
    out = k.d["out"]
    with sp.Fori(0, B) as b:
        ready(b)
        for t in range(NT):
            sp.dma_start(out[ds(b, 1), t * P:(t + 1) * P, :].rearrange("a p c -> p (a c)"),
                         tile_of(k.h, b * NT + t)).then_inc(s_o, 16)
    sp.wait_ge(s_o, after(16 * G))


def per_head(t):
    return t.rearrange("p (h a) -> p h a", a=1).broadcast_to([P, H, HD])


def all_heads(t):
    return t.rearrange("p (a c) -> p a c", a=1).broadcast_to([P, H, HD])


class MemoryWeights:

    def __init__(self, k, ctx):
        self.k = k
        sb = lambda n, s, dt=F32: k.sb("m_" + n, s, dt, ctx)
        self.wa = sb("wa", [P, 3, PW])
        self.wb = sb("wb", [KB, 3, PW])
        self.ma = sb("ma", [P, 3, MOD])
        self.mb = sb("mb", [P, 3, MOD])
        self.mbias = sb("mbias", [64 + MOD, 3])
        self.lin = sb("lin", [P, 2, C])
        self.gb = sb("gb", [P, 3, 2, HD])
        self.lr = sb("lr", [P, 4, H])
        self.gv = sb("gv", [P, 2, H, HD])
        self.up = sb("up", [P, P])
        self.maskA = sb("maskA", [P, H, P])
        self.corner = sb("corner", [P, LEVELS, P], I32)
        self.woT = sb("woT", [P, H // 2, C])
        self.eye = sb("eye", [UNITS, BLK, BLK])
        self.wm = sb("wm", [P, 3 * H])
        self.loaded, self.linked, self.exped = (k.sem("m_" + n) for n in ("w", "lk", "exp"))

    def load(self, eng, d):
        for t, n in ((self.wa, "wa"), (self.wb, "wb"), (self.ma, "ma"), (self.mb, "mb"), (self.up, "up"),
                     (self.eye, "eye"), (self.corner, "corner"), (self.woT, "woT")):
            eng.dma_start(t[:], d[n]).then_inc(self.loaded, 16)
        eng.dma_start(self.mbias[64:64 + MOD, :], d["mbias"]).then_inc(self.loaded, 16)
        eng.dma_start(self.lin[:], d["lin"].broadcast_to([P, 2, C])).then_inc(self.loaded, 16)
        eng.dma_start(self.gb[:], d["gb"].broadcast_to([P, 3, 2, HD])).then_inc(self.loaded, 16)
        eng.dma_start(self.lr[:, 0, :], d["lr_scale"].broadcast_to([P, H])).then_inc(self.loaded, 16)

    def exponentials(self, act):
        act.wait_ge(self.loaded, after(16 * 12))
        self.k.nc.scalar.activation(self.lr[:, 1, :], self.lr[:, 0, :], ACT.Exp, scale=-1.0).then_inc(self.exped, 1)

    def prepare(self, dve):
        v, lr, gb, wb, wm = self.k.nc.vector, self.lr, self.gb, self.wb, self.wm
        dve.wait_ge(self.loaded, after(16 * 12))
        link = linker(dve, self.linked)
        link(v.tensor_scalar(wb[64:KB, :, :], wb[64:KB, :, :], 0.1, None, ALU.mult))
        for w, n in ((self.wa, P), (wb, KB)):
            w3 = w[:, :, :].rearrange("p m (h c) -> p (m h) c", c=HD)
            link(v.tensor_reduce(wm[0:n, :], w3, AX.X, ALU.add))
            link(v.tensor_scalar(wm[0:n, :], wm[0:n, :], 1.0 / HD, None, ALU.mult))
            link(v.tensor_tensor(w3, w3, wm[0:n, :].rearrange("p (h a) -> p h a", a=1).broadcast_to([n, 3 * H, HD]),
                                 ALU.subtract))
        dve.wait_ge(self.exped, after(1))
        link(v.tensor_scalar(lr[:, 1, :], lr[:, 1, :], 1.0, None, ALU.add))
        link(v.reciprocal(lr[:, 0, :], lr[:, 1, :]))
        link(v.tensor_scalar(lr[:, 1, :], lr[:, 0, :], 0.2, None, ALU.mult))
        link(v.tensor_scalar(lr[:, 2, :], lr[:, 1, :], 1.0, None, ALU.add))
        link(v.reciprocal(lr[:, 0, :], lr[:, 2, :]))
        link(v.scalar_tensor_tensor(out=lr[:, 3, :], in0=lr[:, 1, :], scalar=-1.0, in1=lr[:, 0, :], op0=ALU.mult,
                                    op1=ALU.mult))
        for i in range(2):
            link(v.tensor_tensor(self.gv[:, i, :, :], all_heads(gb[:, 1, i, :]), per_head(lr[:, 3, :]), ALU.mult))
        link(v.tensor_scalar(lr[:, 1, :], lr[:, 2, :], -1.0, None, ALU.mult))
        link(v.tensor_tensor(self.maskA[:], self.up[:, :].rearrange("p (a c) -> p a c", a=1).broadcast_to([P, H, P]),
                             lr[:, 1, :].rearrange("p (h a) -> p h a", a=1).broadcast_to([P, H, P]), ALU.mult))


def fast_weights(k, y, blocks):
    nc, d = k.nc, k.d
    HF = PW // 2
    with ExitStack() as ctx:
        sb = lambda n, s, dt=F32: k.sb("m_" + n, s, dt, ctx)
        m_ = k.mw
        wa, wb, ma, mb, mbias, lin, gb, lr, gv, maskA, corner, woT, eye = (
            m_.wa, m_.wb, m_.ma, m_.mb, m_.mbias, m_.lin, m_.gb, m_.lr, m_.gv, m_.maskA, m_.corner, m_.woT, m_.eye)
        Ab = sb("Ab", [UNITS, BLK, BLK])
        Ub = sb("Ub", [UNITS, BLK, BLK])
        prod = sb("prod", [UNITS, BLK, BLK])
        U0 = sb("U0", [P, H, P])
        yb = sb("yb", [P, NT, C])
        xf = sb("xf", [P, 3, 256])
        x0 = sb("x0", [P, P])
        x1 = sb("x1", [P, P])
        xk = sb("xk", [P, 3, P])
        zc = sb("zc", [P, 2, PW])
        sq = sb("sq", [P, 2, PW])
        zsq = sb("zsq", [P, PW])
        sm = sb("sm", [P, 4, 4, H])
        z = sb("z", [P, 2, PW])
        nv = sb("nv", [P, NT, PW])
        dummy = sb("dummy", [1, LEVELS * NG])
        kb = sb("kb", [P, NT, PW])
        kq = sb("kq", [P, NT, H // 2, 2, P])
        kz = sb("kz", [P, H, P])
        AT = sb("AT", [P, NT, H, P])
        PT = sb("PT", [P, H, P])
        T = sb("T", [P, H, P])
        U = sb("U", [P, H, P])
        X = sb("X", [P, H, P])
        R = sb("R", [P, NG, 4 * HD + 32])
        D = sb("D", [P, PW])
        oT = sb("oT", [P, H // 2, P])
        S = sb("S", [P, H // 2, 2, HD])
        pj = k.ps("m_pj", [P, 2, 512], ctx)
        pg = k.ps("m_pg", [P, 2 * NG, 512], ctx)
        SQUARES = 7
        KEYS, UNIT, VALUES, QUERIES = range(4)
        names = ("c var root xf xt xts hd hds pj z1 sq ss rt z2 z3 za zq tr trs kz kk kks "
                 "ka kas ao ai sub uo ui t1 t1s mx mxs my mys mu mus ks r dd dds ot ots su st yo yos ys").split()
        s = {n: k.sem("m_" + n) for n in names}
        block = ctx.enter_context(nc.Block())
        heads = lambda t: t.rearrange("p (h c) -> p h c", c=HD)
        quad = lambda t, g: t[:, 4 * g:4 * g + 4, :].rearrange("p h c -> p (h c)")
        a_ = lambda g: pg[:, 2 * g, :]
        b_ = lambda g: pg[:, 2 * g + 1, :]

        @block.sync
        def _(sp):
            k.start_at_one(sp)
            sp.wait_ge(s["c"], after(1))
            at, ut = blocks
            with sp.Fori(0, B) as b:
                for c in range(NT):
                    n = b * NT + c
                    sp.wait_ge(s["kas"], after(n * NG + 3))
                    for i in range(NBLK):
                        o = slice(i * BLK, (i + 1) * BLK)
                        sp.dma_start(at[i].rearrange("h s t -> s h t"), AT[o, c, :, o]).then_inc(s["ao"], 16)
                    sp.wait_ge(s["ao"], after(n * (16 * NBLK) + 16 * NBLK))
                    sp.dma_start(Ab[:], at.rearrange("i h s t -> (i h) s t")).then_inc(s["ai"], 16)
                    sp.wait_ge(s["sub"], after(n * SUB + SUB))
                    sp.dma_start(ut.rearrange("i h s t -> (i h) s t"), Ub[:]).then_inc(s["uo"], 16)
                    sp.wait_ge(s["uo"], after(n * 16 + 16))
                    for i in range(NBLK):
                        o = slice(i * BLK, (i + 1) * BLK)
                        sp.dma_start(U0[o, :, o], ut[i].rearrange("h s t -> s h t")).then_inc(s["ui"], 16)
            sp.wait_ge(s["ys"], after(16 * G))

        @block.gpsimd
        def _(pool):
            gp = nc.gpsimd
            for t in (xf, kz, R, S, U0):
                gp.memset(t[:], 0.0)
            gp.memset(xk[:], 1.0).then_inc(s["c"], 1)
            gp.tensor_tensor(k.rstd[:], k.vare[:], k.half[:, 0:G], ALU.pow)

            def root(n, i):
                pool.wait_ge(s["var"], after(n * 4 + i + 1))
                gp.tensor_tensor(sm[:, i, 1, :], sm[:, i, 0, :], (k.half2 if i == UNIT else k.half)[:, 0:H],
                                 ALU.pow).then_inc(s["root"], 1)

            def norms(n, c):
                for i in (UNIT, VALUES, QUERIES):
                    root(n, i)
                zv = heads(nv[:, c, :])
                pool.wait_ge(s["z1"], after(n * 3 + 2))
                gp.tensor_tensor(zv, zv, gv[:, 0, :, :], ALU.mult).then_inc(s["z2"], 1)
                pool.wait_ge(s["z2"], after(n + 1))
                gp.tensor_tensor(zv, zv, gv[:, 1, :, :], ALU.add).then_inc(s["z3"], 1)

            def substitute(n, steps):
                if 0 in steps:
                    if not known(n) or n:
                        pool.wait_ge(s["my"], after((n - 1) * (LEVELS * NG) + NG))
                    pool.wait_ge(s["ai"], after(n * 16 + 16))
                    gp.tensor_tensor(Ub[:], eye[:], eye[:], ALU.mult).then_inc(s["sub"], 1)
                for j in steps:
                    shape = [UNITS, j + 1, BLK - 1 - j]
                    o = prod[:, 0:j + 1, j + 1:BLK]
                    pool.wait_ge(s["sub"], after(n * SUB + 2 * j + 1))
                    gp.tensor_tensor(o, Ub[:, 0:j + 1, j:j + 1].broadcast_to(shape),
                                     Ab[:, j:j + 1, j + 1:BLK].broadcast_to(shape), ALU.mult).then_inc(s["sub"], 1)
                    pool.wait_ge(s["sub"], after(n * SUB + 2 * j + 2))
                    gp.tensor_tensor(Ub[:, 0:j + 1, j + 1:BLK], Ub[:, 0:j + 1, j + 1:BLK], o, ALU.add).then_inc(s["sub"], 1)

            root(0, KEYS)
            norms(0, 0)
            substitute(0, range(BLK - 1))
            root(1, KEYS)
            norms(1, 1)
            with pool.Fori(0, B - 1) as b:
                for c in range(NT):
                    n = b * NT + c
                    substitute(n + 1, range(SPLIT))
                    root(n + 2, KEYS)
                    substitute(n + 1, range(SPLIT, BLK - 1))
                    norms(n + 2, (c + 2) % NT)
            substitute(G - 2, range(SPLIT))
            root(G - 1, KEYS)
            substitute(G - 2, range(SPLIT, BLK - 1))
            norms(G - 1, NT - 1)
            substitute(G - 1, range(BLK - 1))

        @block.vector
        def _(dve):
            v = nc.vector
            dve.wait_ge(s["c"], after(1))
            def inputs(n):
                g = n
                dve.wait_ge(s["xt"], after(n))
                dst = [xf[:, j, 0:C] for j in range(3)]
                v.tensor_scalar(dst[0], tile_of(k.h, g), column_of(k.mean, g), column_of(k.rstd12, g),
                                ALU.subtract, ALU.mult).then_inc(s["xf"], 1)
                dve.wait_ge(s["xf"], after(n * 3 + 1))
                v.tensor_tensor(dst[1], dst[0], lin[:, 0, :], ALU.mult).then_inc(s["xf"], 1)
                dve.wait_ge(s["xf"], after(n * 3 + 2))
                v.tensor_tensor(dst[2], dst[1], lin[:, 1, :], ALU.add).then_inc(s["xf"], 1)

            def sums(n, m):
                i = (KEYS, VALUES, QUERIES)[m]
                dve.wait_ge(s["sq"], after(n * 3 + m + 1))
                v.tensor_reduce(sm[:, i, 2, :], heads(sq[:, m % 2, :]), AX.X, ALU.add).then_inc(s["ss"], 1)
                dve.wait_ge(s["ss"], after(n * 3 + m + 1))
                v.tensor_scalar(sm[:, i, 0, :], sm[:, i, 2, :], 1.0 / HD, EPS, ALU.mult, ALU.add).then_inc(s["var"], 1)

            def scaled(n, m, c):
                i = (KEYS, VALUES, QUERIES)[m]
                zm = heads(nv[:, c, :] if m == 1 else z[:, m // 2, :])
                if m != 1:
                    dve.wait_ge(s["tr"], after(n * 4))
                dve.wait_ge(s["root"], after(n * 4 + i + 1))
                v.tensor_tensor(zm, heads(zc[:, m % 2, :]), per_head(sm[:, i, 1, :]), ALU.mult).then_inc(s["z1"], 1)
                if m != 1:
                    dve.wait_ge(s["z1"], after(n * 3 + m + 1))
                    v.tensor_tensor(zm, zm, all_heads(gb[:, m, 0, :]), ALU.mult).then_inc(s["za"], 1)
                    dve.wait_ge(s["za"], after(n * 4 + m + 1))
                    v.tensor_tensor(zm, zm, all_heads(gb[:, m, 1, :]), ALU.add).then_inc(s["za"], 1)

            def lengths(n):
                dve.wait_ge(s["zq"], after(n + 1))
                v.tensor_reduce(sm[:, UNIT, 0, :], heads(zsq[:]), AX.X, ALU.add).then_inc(s["var"], 1)

            def unit_keys(n, c):
                dve.wait_ge(s["root"], after(n * 4 + UNIT + 1))
                v.tensor_scalar(sm[:, UNIT, 2, :], sm[:, UNIT, 1, :], 1e-6, None, ALU.add).then_inc(s["rt"], 1)
                dve.wait_ge(s["rt"], after(n * 4 + 1))
                v.reciprocal(sm[:, UNIT, 3, :], sm[:, UNIT, 2, :]).then_inc(s["rt"], 1)
                dve.wait_ge(s["rt"], after(n * 4 + 2))
                v.tensor_tensor(heads(z[:, 0, :]), heads(z[:, 0, :]), per_head(sm[:, UNIT, 3, :]), ALU.mult).then_inc(s["rt"], 1)
                dve.wait_ge(s["rt"], after(n * 4 + 3))
                v.tensor_tensor(heads(kb[:, c, :]), heads(z[:, 0, :]), per_head(lr[:, 2, :]), ALU.mult).then_inc(s["rt"], 1)

            def single_keys(n, c):
                dve.wait_ge(s["kk"], after(n * NG))
                for p3 in range(2):
                    dve.wait_ge(s["trs"], after(n * 4 + p3 + 1))
                    for o in (0, 64):
                        v.tensor_copy(kz[o:o + 64, p3 * 6 + o // 64:p3 * 6 + 6:2, :],
                                      kq[o:o + 64, c, 3 * p3:3 * p3 + 3, 0, :]).then_inc(s["kz"], 1)

            three = lambda t: t.rearrange("p (a c) -> p a c", a=1).broadcast_to([P, 4, P])

            def decays(n, c):
                for g3 in range(NG):
                    q4 = slice(4 * g3, 4 * g3 + 4)
                    dve.wait_ge(s["ka"], after(n * NG + g3 + 1))
                    v.tensor_tensor(AT[:, c, q4, :], pj[:, g3 % 2, :].rearrange("p (h t) -> p h t", t=P), maskA[:, q4, :],
                                    ALU.mult).then_inc(s["kas"], 1)

            def chunk(n, c, more, next_=True):
                first, m, cm = c == 0, n + 2, (c + 2) % NT
                if more:
                    inputs(m)
                for g3 in range(NG):
                    q4 = slice(4 * g3, 4 * g3 + 4)
                    dve.wait_ge(s["kk"], after(n * NG + g3 + 1))
                    v.tensor_tensor(PT[:, q4, :], b_(g3).rearrange("p (h t) -> p h t", t=P), maskA[:, q4, :],
                                    ALU.mult).then_inc(s["kks"], 1)
                if next_:
                    single_keys(n + 1, (c + 1) % NT)
                    decays(n + 1, (c + 1) % NT)
                for lv in range(LEVELS):
                    for g3 in range(NG):
                        q4 = slice(4 * g3, 4 * g3 + 4)
                        dve.wait_ge(s["my"], after(n * (LEVELS * NG) + lv * NG + g3 + 1))
                        v.memset(dummy[:, lv * NG + g3:lv * NG + g3 + 1], 0.0)
                        v.copy_predicated(T[:, q4, :], three(corner[:, lv, :]),
                                          b_(g3).rearrange("p (h t) -> p h t", t=P)).then_inc(s["mys"], 1)
                    if more and lv == 1:
                        sums(m, 0)
                dve.wait_ge(s["z3"], after(n + 1))
                for g3 in range(NG):
                    if first:
                        v.tensor_copy(R[:, g3, 0:256], nv[:, c, 256 * g3:256 * g3 + 256]).then_inc(s["r"], 1)
                    else:
                        dve.wait_ge(s["ks"], after(n * NG + g3 + 1))
                        v.tensor_tensor(R[:, g3, 0:256], a_(g3)[:, 0:256], nv[:, c, 256 * g3:256 * g3 + 256],
                                        ALU.add).then_inc(s["r"], 1)
                if more:
                    scaled(m, 0, cm)
                    lengths(m)
                    sums(m, 1)
                    unit_keys(m, cm)
                    scaled(m, 1, cm)
                    sums(m, 2)
                for g3 in range(NG):
                    if c < NT - 1:
                        dve.wait_ge(s["su"], after(n * NG + g3 + 1))
                        src = b_(g3)[:, 256:512].rearrange("p (q a c) -> p q a c", q=2, a=2)
                        for o in (0, 64):
                            dst = S[o:o + 64, 2 * g3:2 * g3 + 2, o // 64, :]
                            if first:
                                v.tensor_scalar(dst, src[o:o + 64, :, o // 64, :], -1.0, None, ALU.mult).then_inc(s["st"], 1)
                            else:
                                v.tensor_tensor(dst, dst, src[o:o + 64, :, o // 64, :], ALU.subtract).then_inc(s["st"], 1)
                    else:
                        dve.sem_inc(s["st"], 2)
                dve.wait_ge(s["yo"], after(n + 1))
                dve.wait_ge(s["ys"], after(n * 16))
                v.tensor_copy(yb[:, c, :], a_(0)[:, 256:256 + C]).then_inc(s["yos"], 1)
                if more:
                    scaled(m, 2, cm)

            for n in range(2):
                inputs(n)
                sums(n, 0)
                scaled(n, 0, n)
                lengths(n)
                sums(n, 1)
                unit_keys(n, n)
                scaled(n, 1, n)
                sums(n, 2)
                scaled(n, 2, n)
                if n == 0:
                    single_keys(0, 0)
                    decays(0, 0)
            with dve.Fori(0, B - 1) as b:
                for c in range(NT):
                    chunk(b * NT + c, c, True)
            for c in range(NT):
                chunk(G - NT + c, c, c == 0, c < NT - 1)

        @block.tensor
        def _(pe):
            mm = nc.tensor.matmul

            def ahead(step, n, c):
                if step == 0:
                    pe.wait_ge(s["xf"], after(n * 3 + 3))
                    pe.wait_ge(s["trs"], after(n * 4))
                    pe.wait_ge(s["kas"], after(n * NG))
                    for i in range(2):
                        last = nc.tensor.transpose(pj[:, 0, i * P:(i + 1) * P], xf[:, 2, i * P:(i + 1) * P], k.ident[:])
                    last.then_inc(s["xt"], 1)
                if step == 1:
                    pe.wait_ge(s["xts"], after(n * 3 + 3))
                    for m in range(3):
                        mm(pj[64:64 + MOD, 1, m * P:(m + 1) * P], ma[:, m, :], x0[:], start=True, stop=False)
                        last = mm(pj[64:64 + MOD, 1, m * P:(m + 1) * P], mb[:, m, :], x1[:], start=False, stop=True)
                    last.then_inc(s["hd"], 1)
                if step in (2, 3, 4):
                    m = step - 2
                    if m == 0:
                        pe.wait_ge(s["hds"], after(n * 3 + 3))
                    else:
                        pe.wait_ge(s["sq"], after(n * 3 + m))
                    for f in range(2):
                        mm(pj[:, f, 0:HF], x0[:], wa[:, m, f * HF:(f + 1) * HF], start=True, stop=False)
                        last = mm(pj[:, f, 0:HF], xk[0:KB, m, :], wb[:, m, f * HF:(f + 1) * HF], start=False, stop=True)
                    last.then_inc(s["pj"], 1)
                if step in (5, 6):
                    m = step - 5
                    if m == 0:
                        pe.wait_ge(s["sq"], after(n * 3 + 3))
                        pe.wait_ge(s["rt"], after(n * 4 + 3))
                    else:
                        pe.wait_ge(s["za"], after(n * 4 + 4))
                    for f in range(2):
                        if m == 1:
                            pe.wait_ge(s["trs"], after(n * 4 + f + 1))
                        for q in range(3):
                            last = nc.tensor.transpose(pj[:, f, q * P:(q + 1) * P], z[:, m, (3 * f + q) * P:(3 * f + q + 1) * P],
                                                       k.ident[:])
                        last.then_inc(s["tr"], 1)

            def decays(n, c):
                pe.wait_ge(s["trs"], after(n * 4 + 4))
                pe.wait_ge(s["kz"], after(n * 4 + 4))
                for g3 in range(NG):
                    if g3 == 2:
                        pe.wait_ge(s["kas"], after(n * NG + 1))
                    for hh in range(4):
                        h = 4 * g3 + hh
                        last = mm(pj[:, g3 % 2, hh * P:(hh + 1) * P], kz[:, h, :], kq[:, c, h // 2, 0, :], start=True, stop=True)
                    last.then_inc(s["ka"], 1)

            def chunk(n, c, more, next_=True):
                first, m, cm = c == 0, n + 2, (c + 2) % NT
                pe.wait_ge(s["dds"], after(n * 3))
                pe.wait_ge(s["st"], after(n * 6))
                for g3 in range(NG):
                    for hh in range(4):
                        h = 4 * g3 + hh
                        last = mm(b_(g3)[:, hh * P:(hh + 1) * P], kz[:, h, :], kq[:, c, h // 2, 1, :], start=True, stop=True)
                    last.then_inc(s["kk"], 1)
                pe.wait_ge(s["ots"], after(n * 3))
                pe.wait_ge(s["yos"], after(n))
                pe.wait_ge(s["ui"], after(n * (16 * NBLK) + 16 * NBLK))
                for g3 in range(NG):
                    for hh in range(4):
                        last = nc.tensor.transpose(a_(g3)[:, hh * P:(hh + 1) * P], U0[:, 4 * g3 + hh, :], k.ident[:])
                    last.then_inc(s["t1"], 1)
                if next_:
                    ahead(6, n + 1, (c + 1) % NT)
                for lv in range(LEVELS):
                    j = n * (LEVELS * NG) + lv * NG
                    for g3 in range(NG):
                        if lv == 0:
                            pe.wait_ge(s["t1s"], after(n * NG + g3 + 1))
                        else:
                            pe.wait_ge(s["mus"], after(j - NG + g3 + 1))
                        for hh in range(4):
                            h = 4 * g3 + hh
                            last = mm(a_(g3)[:, hh * P:(hh + 1) * P], AT[:, c, h, :], T[:, h, :], start=True, stop=True)
                        last.then_inc(s["mx"], 1)
                    if next_ and lv == 0:
                        decays(n + 1, (c + 1) % NT)
                    if more and lv == 2:
                        ahead(3, m, cm)
                    for g3 in range(NG):
                        pe.wait_ge(s["mxs"], after(j + g3 + 1))
                        if lv == 0:
                            pe.wait_ge(s["kks"], after(n * NG + g3 + 1))
                        for hh in range(4):
                            h = 4 * g3 + hh
                            last = mm(b_(g3)[:, hh * P:(hh + 1) * P], (U0 if lv == 0 else U)[:, h, :], X[:, h, :],
                                      start=True, stop=True)
                        last.then_inc(s["my"], 1)
                    if more and lv < 2:
                        ahead(2 * lv, m, cm)
                    for g3 in range(NG):
                        pe.wait_ge(s["mys"], after(j + g3 + 1))
                        for hh in range(4):
                            last = nc.tensor.transpose(a_(g3)[:, hh * P:(hh + 1) * P], T[:, 4 * g3 + hh, :], k.ident[:])
                        last.then_inc(s["mu"], 1)
                    if more and lv == 0:
                        ahead(1, m, cm)
                if first:
                    pe.wait_ge(s["mus"], after(n * (LEVELS * NG) + LEVELS * NG))
                    pe.sem_inc(s["ks"], 3)
                else:
                    for g3 in range(NG):
                        pe.wait_ge(s["mus"], after(n * (LEVELS * NG) + (LEVELS - 1) * NG + g3 + 1))
                        for q in range(2):
                            pr = 2 * g3 + q
                            last = mm(a_(g3)[:, q * P:(q + 1) * P], kq[:, c, pr, 0, :],
                                      S[:, pr, :, :].rearrange("p a c -> p (a c)"), start=True, stop=True)
                        last.then_inc(s["ks"], 1)
                for g3 in range(NG):
                    pe.wait_ge(s["r"], after(n * NG + g3 + 1))
                    for hh in range(4):
                        h = 4 * g3 + hh
                        last = mm(b_(g3)[:, hh * P:hh * P + 96], U[:, h, :], R[:, g3, hh * HD:hh * HD + 96], start=True, stop=True)
                    last.then_inc(s["dd"], 1)
                if more:
                    ahead(4, m, cm)
                for g3 in range(NG):
                    pe.wait_ge(s["dds"], after(n * NG + g3 + 1))
                    for q in range(2):
                        pr = 2 * g3 + q
                        o = a_(g3)[:, q * P:(q + 1) * P]
                        if not first:
                            mm(o, S[:, pr, :, :].rearrange("p a c -> p (a c)"), kq[:, c, pr, 1, :], start=True, stop=False,
                               skip_group_check=True)
                        for e in range(2):
                            h = 2 * pr + e
                            last = mm(a_(g3)[64 * e:64 * e + 64, q * P:(q + 1) * P], D[:, h * HD:(h + 1) * HD], PT[:, h, :],
                                      start=first, stop=True, skip_group_check=True)
                    last.then_inc(s["ot"], 1)
                    if c < NT - 1:
                        for q in range(2):
                            pr = 2 * g3 + q
                            last = mm(b_(g3)[:, 256 + q * P:256 + (q + 1) * P], kb[:, c, pr * P:(pr + 1) * P],
                                      D[:, pr * P:(pr + 1) * P], start=True, stop=True)
                        last.then_inc(s["su"], 1)
                if c == NT - 1:
                    pe.sem_inc(s["su"], 3)
                if more:
                    ahead(5, m, cm)
                pe.wait_ge(s["ots"], after(n * NG + 3))
                for q in range(H // 2):
                    last = mm(a_(0)[:, 256:256 + C], oT[:, q, :], woT[:, q, :], start=q == 0, stop=q == H // 2 - 1)
                last.then_inc(s["yo"], 1)

            for step in range(7):
                ahead(step, 0, 0)
            decays(0, 0)
            for step in range(6):
                ahead(step, 1, 1)
            with pe.Fori(0, B - 1) as b:
                for c in range(NT):
                    chunk(b * NT + c, c, True)
            for c in range(NT):
                chunk(G - NT + c, c, c == 0, c < NT - 1)

        @block.scalar
        def _(act):
            A = nc.scalar.activation
            act.preload_act_table(ACT.Gelu)

            def ahead(step, n, c):
                if step == 0:
                    act.wait_ge(s["xt"], after(n + 1))
                    act.wait_ge(s["pj"], after(n * 3))
                    A(x0[:], pj[:, 0, 0:P], ACT.Copy).then_inc(s["xts"], 1)
                    A(x1[:], pj[:, 0, P:2 * P], ACT.Copy).then_inc(s["xts"], 1)
                    A(xk[0:64, :, :], pj[0:64, 0, P:2 * P].rearrange("p (a t) -> p a t", a=1).broadcast_to([64, 3, P]),
                      ACT.Copy).then_inc(s["xts"], 1)
                if step == 1:
                    act.wait_ge(s["hd"], after(n + 1))
                    for m in range(3):
                        A(xk[64:64 + MOD, m, :], pj[64:64 + MOD, 1, m * P:(m + 1) * P], ACT.Gelu,
                          bias=mbias[64:64 + MOD, m:m + 1]).then_inc(s["hds"], 1)
                if step in (2, 3, 4):
                    m = step - 2
                    act.wait_ge(s["pj"], after(n * 3 + m + 1))
                    if m != 1:
                        act.wait_ge(s["z1"], after(n * 3 + m // 2))
                    A(zc[:, m % 2, :].rearrange("p (f c) -> p f c", f=2), pj[:, :, 0:HF], ACT.Copy)
                    A(sq[:, m % 2, :].rearrange("p (f c) -> p f c", f=2), pj[:, :, 0:HF], ACT.Square).then_inc(s["sq"], 1)
                if step == SQUARES:
                    act.wait_ge(s["za"], after(n * 4 + 2))
                    A(zsq[:], z[:, 0, :], ACT.Square).then_inc(s["zq"], 1)
                if step in (5, 6):
                    m = step - 5
                    for f in range(2):
                        act.wait_ge(s["tr"], after(n * 4 + 2 * m + f + 1))
                        A(kq[:, c, 3 * f:3 * f + 3, m, :], pj[:, f, 0:3 * P].rearrange("p (h t) -> p h t", t=P),
                          ACT.Copy).then_inc(s["trs"], 1)

            def chunk(n, c, more, next_=True):
                m, cm = n + 2, (c + 2) % NT
                for g3 in range(NG):
                    act.wait_ge(s["t1"], after(n * NG + g3 + 1))
                    A(quad(T, g3), a_(g3), ACT.Copy).then_inc(s["t1s"], 1)
                if next_:
                    ahead(6, n + 1, (c + 1) % NT)
                for lv in range(LEVELS):
                    j = n * (LEVELS * NG) + lv * NG
                    for g3 in range(NG):
                        act.wait_ge(s["mx"], after(j + g3 + 1))
                        A(quad(X, g3), a_(g3), ACT.Copy).then_inc(s["mxs"], 1)
                    if more and lv != 1:
                        ahead((0, None, 3)[lv], m, cm)
                    for g3 in range(NG):
                        act.wait_ge(s["mu"], after(j + g3 + 1))
                        A(quad(U, g3), a_(g3), ACT.Copy).then_inc(s["mus"], 1)
                    if more:
                        ahead((1, 2, SQUARES)[lv], m, cm)
                for g3 in range(NG):
                    act.wait_ge(s["dd"], after(n * NG + g3 + 1))
                    act.wait_ge(s["su"], after(n * NG))
                    A(heads(D[:, 256 * g3:256 * g3 + 256]), b_(g3).rearrange("p (h t) -> p h t", t=P)[:, :, 0:HD],
                      ACT.Copy).then_inc(s["dds"], 1)
                if more:
                    ahead(4, m, cm)
                act.wait_ge(s["yo"], after(n))
                for g3 in range(NG):
                    act.wait_ge(s["ot"], after(n * NG + g3 + 1))
                    A(oT[:, 2 * g3:2 * g3 + 2, :].rearrange("p q t -> p (q t)"), a_(g3)[:, 0:256], ACT.Copy).then_inc(s["ots"], 1)
                if more:
                    ahead(5, m, cm)
                act.wait_ge(s["yos"], after(n + 1))
                act.dma_start(y[ds(n * P, P), :], yb[:, c, :]).then_inc(s["ys"], 16)

            for n in range(2):
                for step in (0, 1, 2, 3, SQUARES, 4, 5, 6)[:8 - n]:
                    ahead(step, n, n)
            with act.Fori(0, B - 1) as b:
                for c in range(NT):
                    chunk(b * NT + c, c, True)
            for c in range(NT):
                chunk(G - NT + c, c, c == 0, c < NT - 1)


def gate(k, y):
    nc, d = k.nc, k.d
    with ExitStack() as ctx:
        sb = lambda n, s, dt=F32: k.sb("g_" + n, s, dt, ctx)
        wg = sb("wg", [KT + 1, 2, C])
        xb = sb("xb", [P, 2, 2, C])
        xT = sb("xT", [KT + 1, 2, 2, 2 * P])
        sg = sb("sg", [P, 2, 2, C])
        ym = sb("ym", [P, G, C])
        pX = k.ps("g_pX", [P, 2, 512], ctx)
        pG = k.ps("g_pG", [P, 2, 512], ctx)
        s_w, s_y, s_on, s_x, s_xt, s_xts, s_g, s_sg, s_m, s_h, s_st = (
            k.sem("g_" + n) for n in ("w", "y", "on", "x", "xt", "xts", "g", "sg", "m", "h", "st"))
        rounds = G // 2
        block = ctx.enter_context(nc.Block())

        @block.sync
        def _(sp):
            k.start_at_one(sp)
            sp.dma_start(wg[:], d["wg"]).then_inc(s_w, 16)
            sp.dma_start(ym[:], y.rearrange("(g p) c -> p g c", p=P)).then_inc(s_y, 16)
            k.w1.load(sp, d)
            sp.wait_ge(s_w, after(16))

        @block.vector
        def _(dve):
            v = nc.vector
            v.memset(xT[KT:KT + 1, :, :, :], 1.0).then_inc(s_on, 1)
            dve.wait_ge(s_y, after(16))

            def norm(i, s):
                if not known(i) or i > 1:
                    dve.wait_ge(s_xt, after(i - 1))
                for t in range(2):
                    g = i * 2 + t
                    v.tensor_scalar(xb[:, s, t, :], tile_of(k.h, g), column_of(k.mean, g), column_of(k.rstd, g),
                                    ALU.subtract, ALU.mult).then_inc(s_x, 1)

            def step(i, uses, s):
                if not (known(i) and i >= rounds - 2):
                    norm(i + 2, s)
                dve.wait_ge(s_sg, after(i + 1))
                for t in range(2):
                    v.tensor_tensor(sg[:, s, t, :], sg[:, s, t, :], tile_of(ym, i * 2 + t), ALU.mult).then_inc(s_m, 1)
                dve.wait_ge(s_m, after(i * 2 + 2))
                for t in range(2):
                    v.tensor_tensor(tile_of(k.h, i * 2 + t), tile_of(k.h, i * 2 + t), sg[:, s, t, :], ALU.add).then_inc(s_h, 1)
                dve.wait_ge(s_h, after(i * 2 + 2))
                for t in range(2):
                    v.bn_stats(tile_of(k.stats, i * 2 + t), tile_of(k.h, i * 2 + t)).then_inc(s_st, 1)

            norm(0, 0)
            norm(1, 1)
            stepped(dve, rounds, step)
            dve.wait_ge(s_st, after(G))

        @block.tensor
        def _(pe):
            pe.wait_ge(s_w, after(16))
            pe.wait_ge(s_on, after(1))

            def turn(i, s):
                pe.wait_ge(s_x, after(i * 2 + 2))
                if not known(i) or i > 1:
                    pe.wait_ge(s_xts, after(i - 1))
                for t in range(2):
                    for c in range(2):
                        last = nc.tensor.transpose(pX[0:KT, s, (2 * c + t) * P:(2 * c + t + 1) * P],
                                                   xb[:, s, t, c * KT:(c + 1) * KT], k.ident[:])
                last.then_inc(s_xt, 1)

            def step(i, uses, s):
                pe.wait_ge(s_xts, after(i + 1))
                if not known(i) or i > 1:
                    pe.wait_ge(s_sg, after(i - 1))
                for t in range(2):
                    for c in range(2):
                        last = nc.tensor.matmul(pG[:, s, t * C:(t + 1) * C], xT[0:KT + c, s, c, t * P:(t + 1) * P],
                                                wg[0:KT + c, c, :], start=c == 0, stop=c == 1)
                last.then_inc(s_g, 1)
                if not (known(i) and i >= rounds - 2):
                    turn(i + 2, s)

            turn(0, 0)
            turn(1, 1)
            stepped(pe, rounds, step)

        @block.scalar
        def _(act):
            act.preload_act_table(ACT.Sigmoid)

            def turned(i, s):
                act.wait_ge(s_xt, after(i + 1))
                if not known(i) or i > 1:
                    act.wait_ge(s_g, after(i - 1))
                nc.scalar.activation(xT[0:KT, s, :, :].rearrange("p c t -> p (c t)"), pX[0:KT, s, :], ACT.Copy).then_inc(s_xts, 1)

            def step(i, uses, s):
                act.wait_ge(s_g, after(i + 1))
                if not known(i) or i > 1:
                    act.wait_ge(s_h, after((i - 1) * 2))
                nc.scalar.activation(sg[:, s, :, :].rearrange("p t c -> p (t c)"), pG[:, s, 0:2 * C], ACT.Sigmoid).then_inc(s_sg, 1)
                if not (known(i) and i >= rounds - 2):
                    turned(i + 2, s)

            turned(0, 0)
            turned(1, 1)
            stepped(act, rounds, step)


def build(nc, d):
    with ExitStack() as ctx:
        k = Core(nc, ctx, d)
        y = nc.dram_tensor("m_y", (NTOK * B, C), F32, kind="Internal").ap()
        blocks = [nc.dram_tensor("m_blocks%d" % i, (NBLK, H, BLK, BLK), F32, kind="Internal").ap() for i in range(2)]
        tokenizer(k)
        attention(k)
        with ExitStack() as weights:
            k.w0 = Weights0(k, weights)
            route(k, "r0", 2, N0, "gate0_w", "gate0_b")
            experts0(k)
        with ExitStack() as weights:
            k.mw = MemoryWeights(k, weights)
            combine0(k)
            k.recycle()
            fast_weights(k, y, blocks)
        with ExitStack() as weights:
            k.w1 = Weights1(k, weights)
            gate(k, y)
            route(k, "r1", 1, N1, "gate1_w", "gate1_b")
            experts1(k)
        finish(k)


def hostprep(inputs):
    f = lambda n: np.asarray(inputs[n])
    a = {}
    x = f("x")
    for lv, p in enumerate((1, 2, 4)):
        n = 64 // p
        a[f"x{lv}r"] = x.reshape(B, 3, n, p, n, p).transpose(2, 4, 0, 3, 5, 1).reshape(n * n, B * p * p * 3)
        a[f"idx{lv}"] = f(f"L0_tok_idx{lv}")
    x1, x2 = a.pop("x1r"), a.pop("x2r")
    a["x12r"] = np.zeros((len(x1) + len(x2), x2.shape[1]), np.float32)
    a["x12r"][0:len(x1), 0:x1.shape[1]], a["x12r"][len(x1):] = x1, x2
    w0 = np.zeros((P, 64), np.float32)
    w0[0:48] = f("L0_tok_W0").T
    w0[64:112] = f("L0_tok_W0").T
    a["w0T"] = w0
    a["w1T"] = f("L0_tok_W1").T.reshape(2, KT, 64).transpose(1, 0, 2)
    a["w2T"] = f("L0_tok_W2").T.reshape(6, P, 64).transpose(1, 0, 2)
    a["wfT"] = f("L0_tok_Wf").T.reshape(3, 64, C).transpose(1, 0, 2)
    a["lb"] = np.stack([f("L0_tok_b0"), f("L0_tok_b1"), f("L0_tok_b2")], 1)
    a["bf"] = f("L0_tok_bf")[None]
    a["txt"] = f("txt")
    for name, n in (("up1", 64), ("up2", 16)):
        m = np.zeros((n, 256), np.float32)
        at = np.clip((np.arange(256, dtype=np.float32) + np.float32(0.5)) * np.float32(n / 256) - np.float32(0.5), 0, n - 1)
        lo = np.floor(at).astype(int)
        for t in range(256):
            m[lo[t], t] += 1 - (at[t] - lo[t])
            m[min(lo[t] + 1, n - 1), t] += at[t] - lo[t]
        a[name] = m
    w = f("L0_attn_w_qkv")

    def heads(w):
        o = np.zeros((2, KT, NH0, 32), np.float32)
        o[..., 0:DH0] = w.reshape(2, KT, NH0, DH0)
        return o.reshape(2, KT, 2, P).transpose(1, 0, 2, 3)
    tiles = lambda w: w.reshape(2, KT, -1).transpose(1, 0, 2)
    a["wq"], a["wk"], a["wv"] = heads(w[:, 0:C]), heads(w[:, C:2 * C]), tiles(w[:, 2 * C:])
    wp = np.zeros((2, 4, 32, C), np.float32)
    wp[:, :, 0:DH0] = f("L0_attn_w_proj").reshape(2, 4, DH0, C)
    wp[0, 0, DH0] = f("L0_attn_b_proj")
    a["wp"] = wp.reshape(2, P, C).transpose(1, 0, 2)
    sel = np.zeros((4, 32, 4, 32), np.float32)
    for j in range(4):
        sel[j, DH0, j] = 1
    a["dsel"] = sel.reshape(P, P)
    a["gate0_w"], a["gate0_b"] = tiles(f("L0_ffn_gate_w")), f("L0_ffn_gate_b")[None]
    a["gate1_w"], a["gate1_b"] = tiles(f("L1_ffn_router_w")), f("L1_ffn_router_b")[None]
    a["tri"] = np.triu(np.ones((P, P), np.float32), 1)
    a["rank8"] = np.tile(np.arange(E, 0, -1, dtype=np.float32), (P, 1))
    a["starts"] = (np.arange(N0, dtype=np.float32) * P)[None]
    w1 = np.zeros((KT + 1, 2, E, F0), np.float32)
    w1[0:KT] = f("L0_ffn_w1").reshape(E, 2, KT, F0).transpose(2, 1, 0, 3)
    w1[KT, 1] = f("L0_ffn_b1")
    a["e0w1"] = w1
    a["e0w2"] = f("L0_ffn_w2").reshape(E, F0 // P, P, C).transpose(2, 0, 1, 3)
    a["e0b2"] = f("L0_ffn_b2")[None]
    a["e1w1"] = f("L1_ffn_w1").reshape(E, 2, KT, F1).transpose(2, 1, 0, 3)
    a["e1w2"] = f("L1_ffn_w2").reshape(E, 2, KT, F1).transpose(2, 1, 0, 3)
    a["e1w3"] = f("L1_ffn_w3").reshape(E, F1 // P, P, C).transpose(2, 0, 1, 3)
    wa = np.zeros((P, 3, PW), np.float32)
    wb = np.zeros((KB, 3, PW), np.float32)
    ma = np.zeros((P, 3, MOD), np.float32)
    mb = np.zeros((P, 3, MOD), np.float32)
    for m, n in enumerate("kvq"):
        w, m1 = f(f"L1_attn_W{n}").T, f(f"L1_attn_{n}m_w1").T
        wa[:, m], wb[0:64, m] = w[0:P], w[P:]
        wb[64:64 + MOD, m], wb[64 + MOD, m] = f(f"L1_attn_{n}m_w2").T, f(f"L1_attn_{n}m_b2")
        ma[:, m], mb[0:64, m] = m1[0:P], m1[P:]
    a["wa"], a["wb"], a["ma"], a["mb"] = wa, wb, ma, mb
    a["mbias"] = np.stack([f(f"L1_attn_{n}m_b1") for n in "kvq"], 1)
    a["lin"] = np.stack([f("L1_attn_ln_in_g"), f("L1_attn_ln_in_b")])[None]
    a["gb"] = np.stack([np.stack([f(f"L1_attn_ln{n}_g"), f(f"L1_attn_ln{n}_b")]) for n in "kvq"])[None]
    a["lr_scale"] = f("L1_attn_lr_scale")[None]
    a["up"] = np.triu(np.ones((P, P), np.float32), 1)
    t, s = np.arange(P)[:, None], np.arange(P)[None, :]
    corner = np.zeros((P, LEVELS, P), np.int32)
    for i, lv in enumerate(range(7 - LEVELS, 7)):
        corner[:, i] = (t >> (lv + 1) == s >> (lv + 1)) & ((t >> lv) & 1 == 1) & ((s >> lv) & 1 == 0)
    a["corner"] = corner
    a["eye"] = np.tile(np.eye(BLK, dtype=np.float32), (UNITS, 1, 1))
    a["woT"] = f("L1_attn_Wo").T.reshape(H // 2, P, C).transpose(1, 0, 2)
    wg = np.zeros((KT + 1, 2, C), np.float32)
    wg[0:KT] = tiles(f("L1_attn_Wg").T)
    wg[KT, 1] = f("L1_attn_bg")
    a["wg"] = wg
    return {n: np.ascontiguousarray(v) for n, v in a.items()}


def kernel(**inputs):
    import concourse.bacc as bacc
    from concourse.bass_utils import run_bass_kernel_spmd

    arrays = hostprep(inputs)
    nc = bacc.Bacc("TRN2", target_bir_lowering=False, num_devices=1)
    d = {n: nc.dram_tensor("in_" + n, v.shape, mybir.dt.from_np(v.dtype), kind="ExternalInput").ap()
         for n, v in arrays.items()}
    d["out"] = nc.dram_tensor("out", (B, NTOK, C), F32, kind="ExternalOutput").ap()
    build(nc, d)
    r = run_bass_kernel_spmd(nc, [{"in_" + n: v for n, v in arrays.items()}], core_ids=[0])
    return r.results[0]["out"]
```
